# Optimizing a Trainium2 kernel written in Bass

```python
import numpy as np
import jax
import jax.numpy as jnp

def _softmax(x, axis=-1):
    return jax.nn.softmax(x, axis=axis)
def _gelu(x):
    return jax.nn.gelu(x, approximate=True)
def _silu(x):
    return jax.nn.silu(x)
def _sigmoid(x):
    return jax.nn.sigmoid(x)
def _layernorm(x, axis=-1, eps=1e-5):
    m = jnp.mean(x, axis=axis, keepdims=True)
    v = jnp.var(x, axis=axis, keepdims=True)
    return (x - m) / jnp.sqrt(v + eps)
def _scatter_add(tgt, idx, src, axis=0):
    return tgt.at[idx].add(src)
def _segment_sum(src, seg, n):
    return jax.ops.segment_sum(src, seg, n)

kernel_name = 'mk_conv_preact_d4_conv_nchw64_c308da'

def setup_inputs(seed: int = 0):
    np.random.seed(seed)
    _w = jnp.asarray
    def _rec_inputs():
        import jax
        import jax.numpy as jnp
        _gk = jax.random.key(seed)
        x = 7.22e-05 + 1 * jax.random.normal(jax.random.fold_in(_gk, 1), (8, 64, 128, 128), jnp.float32)
        return x
    x = _rec_inputs()
    def _L0_conv_setup():
        import jax, jax.numpy as jnp
        import numpy as np
        C = 64
        K = 3
        B, H, W = (8, 128, 128)

        def conv2d(x, w, b, pad, groups=1):
            y = jax.lax.conv_general_dilated(x, w, window_strides=(1, 1), padding=[(pad, pad), (pad, pad)], feature_group_count=groups, dimension_numbers=('NCHW', 'OIHW', 'NCHW'))
            return y + b[None, :, None, None]
        key = jax.random.key(seed)
        ks = jax.random.split(key, 11)
        s3 = 1.0 / np.sqrt(C * 9)
        inp = {'x': jax.random.normal(ks[0], (B, C, H, W), jnp.float32), 'w0': jax.random.normal(ks[1], (C, C, 3, 3), jnp.float32) * s3, 'b0': jax.random.normal(ks[2], (C,), jnp.float32) * 0.01, 'w1': jax.random.normal(ks[3], (C, 1, 3, 3), jnp.float32) * (1.0 / 3.0), 'b1': jax.random.normal(ks[4], (C,), jnp.float32) * 0.01, 'w2': jax.random.normal(ks[5], (1, 1, K), jnp.float32) * (1.0 / np.sqrt(K)), 'b2': jax.random.normal(ks[6], (1,), jnp.float32) * 0.01, 'w3': jax.random.normal(ks[7], (C * K * K, C, 1, 1), jnp.float32) * (1.0 / np.sqrt(C)), 'b3': jax.random.normal(ks[8], (C * K * K,), jnp.float32) * 0.01, 'wf': jax.random.normal(ks[9], (C, C, 3, 3), jnp.float32) * s3, 'bf': jax.random.normal(ks[10], (C,), jnp.float32) * 0.01}
        return inp
    _L0_conv_all = _L0_conv_setup()
    _L0_conv_in = {k: v for k, v in _L0_conv_all.items() if k in ('w0', 'b0', 'w1', 'b1', 'w2', 'b2', 'w3', 'b3', 'wf', 'bf', )}
    del _L0_conv_all

    def _L1_conv_setup():
        import jax, jax.numpy as jnp
        import numpy as np
        B, C, H, W = (16, 64, 256, 256)
        M1, M2 = (32, 32)
        ERR_TH = 0.1

        def dht_2d(x):
            f = jnp.fft.fftn(x, axes=(2, 3))
            ff = jnp.fft.fftn(x[:, :, ::-1, ::-1], axes=(2, 3))
            return (f.real - ff.imag).astype(x.dtype)

        def idht_2d(X):
            n = X.shape[2] * X.shape[3]
            return dht_2d(X) / n

        def spectral_pass(x_ht, w, size1, size2):
            m1, m2 = (w.shape[2], w.shape[3])
            conv = jnp.einsum('bixy,ioxy->boxy', x_ht[:, :, :m1, :m2], w)
            return jnp.pad(conv, ((0, 0), (0, 0), (0, size1 - m1), (0, size2 - m2)))
        key = jax.random.key(seed)
        k1, k2, k3 = jax.random.split(key, 3)
        scale = 1.0 / (C * C)
        x = jax.random.normal(k1, (B, C, H, W), dtype=jnp.float32)
        weights1 = scale * jax.random.uniform(k2, (C, C, M1, M2), dtype=jnp.float32)
        refine_weights1 = scale * jax.random.uniform(k3, (C, C, M1, M2), dtype=jnp.float32)
        return {'x': x, 'weights1': weights1, 'refine_weights1': refine_weights1}
    _L1_conv_all = _L1_conv_setup()
    _L1_conv_in = {k: v for k, v in _L1_conv_all.items() if k in ('weights1', 'refine_weights1', )}
    del _L1_conv_all

    def _L2_conv_setup():
        import jax, jax.numpy as jnp
        import numpy as np

        def _stencils():
            sobel_x = [[1, 0, -1], [2, 0, -2], [1, 0, -1]]
            sobel_y = [[1, 2, 1], [0, 0, 0], [-1, -2, -1]]
            lap = [[0, 1, 0], [1, -4, 1], [0, 1, 0]]
            edge = [[-1, -1, -1], [-1, 8, -1], [-1, -1, -1]]
            sobel_xy = [[2, 1, 0], [1, 0, -1], [0, -1, -2]]
            sobel_yx = [[0, -1, -2], [1, 0, -1], [2, 1, 0]]
            roberts_x = [[0, 0, 0], [0, 1, 0], [0, 0, -1]]
            roberts_y = [[0, 0, 0], [0, 0, 1], [0, -1, 0]]
            return np.asarray([sobel_x, sobel_y, lap, edge, sobel_xy, sobel_yx, roberts_x, roberts_y], dtype=np.float32)

        def _depthwise3x3(x, k):
            C = x.shape[1]
            w = jnp.broadcast_to(k, (C, 1, 3, 3))
            return jax.lax.conv_general_dilated(x, w, window_strides=(1, 1), padding=((1, 1), (1, 1)), dimension_numbers=('NCHW', 'OIHW', 'NCHW'), feature_group_count=C)

        def _highpass(x):
            ones = jnp.full((3, 3), 1.0 / 9.0, dtype=x.dtype)
            return x - _depthwise3x3(x, ones)
        key = jax.random.key(seed)
        B, C, H, W = (8, 64, 256, 256)
        x = jax.random.normal(key, (B, C, H, W), dtype=jnp.float32)
        alpha = jnp.ones((9,), dtype=jnp.float32)
        beta = jnp.zeros((1,), dtype=jnp.float32)
        kernels = jnp.asarray(_stencils())
        return {'x': x, 'alpha': alpha, 'beta': beta, 'kernels': kernels}
    _L2_conv_all = _L2_conv_setup()
    _L2_conv_in = {k: v for k, v in _L2_conv_all.items() if k in ('alpha', 'beta', 'kernels', )}
    del _L2_conv_all

    def _L3_conv_setup():
        import jax, jax.numpy as jnp
        import numpy as np
        from jax import lax
        KERNEL = 9
        STRIDE = 1
        PAD = 4
        key = jax.random.key(seed)
        kx, kk = jax.random.split(key)
        X = jax.random.normal(kx, (32, 64, 256, 256), dtype=jnp.float32)
        K = jax.random.normal(kk, (1, 1, KERNEL, KERNEL), dtype=jnp.float32)
        return {'X': X, 'K': K}
    _L3_conv_all = _L3_conv_setup()
    _L3_conv_in = {k: v for k, v in _L3_conv_all.items() if k in ('K', )}
    del _L3_conv_all

    return {
        "x": x,
        "L0_conv_w0": _L0_conv_in["w0"],
        "L0_conv_b0": _L0_conv_in["b0"],
        "L0_conv_w1": _L0_conv_in["w1"],
        "L0_conv_b1": _L0_conv_in["b1"],
        "L0_conv_w2": _L0_conv_in["w2"],
        "L0_conv_b2": _L0_conv_in["b2"],
        "L0_conv_w3": _L0_conv_in["w3"],
        "L0_conv_b3": _L0_conv_in["b3"],
        "L0_conv_wf": _L0_conv_in["wf"],
        "L0_conv_bf": _L0_conv_in["bf"],
        "L1_conv_weights1": _L1_conv_in["weights1"],
        "L1_conv_refine_weights1": _L1_conv_in["refine_weights1"],
        "L2_conv_alpha": _L2_conv_in["alpha"],
        "L2_conv_beta": _L2_conv_in["beta"],
        "L2_conv_kernels": _L2_conv_in["kernels"],
        "L3_conv_K": _L3_conv_in["K"],
    }

def reference(x, L0_conv_w0, L0_conv_b0, L0_conv_w1, L0_conv_b1, L0_conv_w2, L0_conv_b2, L0_conv_w3, L0_conv_b3, L0_conv_wf, L0_conv_bf, L1_conv_weights1, L1_conv_refine_weights1, L2_conv_alpha, L2_conv_beta, L2_conv_kernels, L3_conv_K):
    import jax
    import jax.numpy as jnp
    def _L0_conv_ref(x, w0, b0, w1, b1, w2, b2, w3, b3, wf, bf):
        import jax, jax.numpy as jnp
        import numpy as np
        C = 64
        K = 3
        B, H, W = (8, 128, 128)

        def conv2d(x, w, b, pad, groups=1):
            y = jax.lax.conv_general_dilated(x, w, window_strides=(1, 1), padding=[(pad, pad), (pad, pad)], feature_group_count=groups, dimension_numbers=('NCHW', 'OIHW', 'NCHW'))
            return y + b[None, :, None, None]
        b, c, h, w = x.shape
        pre = x
        x0 = conv2d(x, w0, b0, pad=1)
        x1 = conv2d(x0, w1, b1, pad=1, groups=c)
        m = jnp.mean(x0, axis=(2, 3))
        x2 = jax.lax.conv_general_dilated(m[:, None, :], w2, window_strides=(1,), padding=[(K // 2, K // 2)], dimension_numbers=('NCH', 'OIH', 'NCH')) + b2[None, :, None]
        out = x1 + x2[:, 0, :, None, None]
        fil = jnp.einsum('oc,bchw->bohw', w3[:, :, 0, 0], out) + b3[None, :, None, None]
        filter_x = fil.reshape(b, c, K * K, h, w)
        xp = jnp.pad(x0, ((0, 0), (0, 0), (1, 1), (1, 1)))
        unfold_x = jnp.stack([xp[:, :, i:i + h, j:j + w] for i in range(3) for j in range(3)], axis=2)
        out = jnp.sum(unfold_x * filter_x, axis=2)
        out = jnp.where(out >= 0, out, 0.2 * out)
        out = conv2d(out, wf, bf, pad=1) + pre
        return out

    def _L1_conv_ref(x, weights1, refine_weights1):
        import jax, jax.numpy as jnp
        import numpy as np
        B, C, H, W = (16, 64, 256, 256)
        M1, M2 = (32, 32)
        ERR_TH = 0.1

        def dht_2d(x):
            f = jnp.fft.fftn(x, axes=(2, 3))
            ff = jnp.fft.fftn(x[:, :, ::-1, ::-1], axes=(2, 3))
            return (f.real - ff.imag).astype(x.dtype)

        def idht_2d(X):
            n = X.shape[2] * X.shape[3]
            return dht_2d(X) / n

        def spectral_pass(x_ht, w, size1, size2):
            m1, m2 = (w.shape[2], w.shape[3])
            conv = jnp.einsum('bixy,ioxy->boxy', x_ht[:, :, :m1, :m2], w)
            return jnp.pad(conv, ((0, 0), (0, 0), (0, size1 - m1), (0, size2 - m2)))
        size1, size2 = (x.shape[-2], x.shape[-1])
        x_ht = dht_2d(x)
        out_ht = spectral_pass(x_ht, weights1, size1, size2)
        x_reconstructed = idht_2d(out_ht)
        mask = (jnp.abs(x - x_reconstructed) > ERR_TH).astype(x.dtype)
        x_refine = x * mask
        x_refine_ht = dht_2d(x_refine)
        out_ht = out_ht + spectral_pass(x_refine_ht, refine_weights1, size1, size2)
        return idht_2d(out_ht)

    def _L2_conv_ref(x, alpha, beta, kernels):
        import jax, jax.numpy as jnp
        import numpy as np

        def _stencils():
            sobel_x = [[1, 0, -1], [2, 0, -2], [1, 0, -1]]
            sobel_y = [[1, 2, 1], [0, 0, 0], [-1, -2, -1]]
            lap = [[0, 1, 0], [1, -4, 1], [0, 1, 0]]
            edge = [[-1, -1, -1], [-1, 8, -1], [-1, -1, -1]]
            sobel_xy = [[2, 1, 0], [1, 0, -1], [0, -1, -2]]
            sobel_yx = [[0, -1, -2], [1, 0, -1], [2, 1, 0]]
            roberts_x = [[0, 0, 0], [0, 1, 0], [0, 0, -1]]
            roberts_y = [[0, 0, 0], [0, 0, 1], [0, -1, 0]]
            return np.asarray([sobel_x, sobel_y, lap, edge, sobel_xy, sobel_yx, roberts_x, roberts_y], dtype=np.float32)

        def _depthwise3x3(x, k):
            C = x.shape[1]
            w = jnp.broadcast_to(k, (C, 1, 3, 3))
            return jax.lax.conv_general_dilated(x, w, window_strides=(1, 1), padding=((1, 1), (1, 1)), dimension_numbers=('NCHW', 'OIHW', 'NCHW'), feature_group_count=C)

        def _highpass(x):
            ones = jnp.full((3, 3), 1.0 / 9.0, dtype=x.dtype)
            return x - _depthwise3x3(x, ones)
        k = jnp.einsum('a,ahw->hw', alpha[:8], kernels)
        out = _depthwise3x3(x, k)
        return out + x * beta[0] + _highpass(x) * alpha[8]

    def _L3_conv_ref(X, K):
        import jax, jax.numpy as jnp
        import numpy as np
        from jax import lax
        KERNEL = 9
        STRIDE = 1
        PAD = 4
        B, C, H, W = X.shape
        Xr = X.reshape(B * C, 1, H, W)
        out = lax.conv_general_dilated(Xr, K, window_strides=(STRIDE, STRIDE), padding=[(PAD, PAD), (PAD, PAD)], dimension_numbers=('NCHW', 'OIHW', 'NCHW'))
        return out.reshape(B, C, out.shape[2], out.shape[3])

    def _gn(v, G=32, eps=1e-5):
        B_, C_, H_, W_ = v.shape
        g = v.reshape(B_, G, C_ // G, H_, W_)
        m = jnp.mean(g, axis=(2, 3, 4), keepdims=True)
        s = jnp.var(g, axis=(2, 3, 4), keepdims=True)
        return ((g - m) / jnp.sqrt(s + eps)).reshape(v.shape)

    def _ln_c(v, eps=1e-6):
        m = jnp.mean(v, axis=1, keepdims=True)
        s = jnp.var(v, axis=1, keepdims=True)
        return (v - m) / jnp.sqrt(s + eps)

    def _ln_t(v, eps=1e-5):
        m = jnp.mean(v, axis=-1, keepdims=True)
        s = jnp.var(v, axis=-1, keepdims=True)
        return (v - m) / jnp.sqrt(s + eps)

    def _to_tokens(v):
        B_, C_, H_, W_ = v.shape
        return v.reshape(B_, C_, H_ * W_).transpose(0, 2, 1)
    def _from_tokens(t, like):
        B_, C_, H_, W_ = like.shape
        return t.transpose(0, 2, 1).reshape(B_, C_, H_, W_)

    x = x + _L0_conv_ref(_gn(x), L0_conv_w0, L0_conv_b0, L0_conv_w1, L0_conv_b1, L0_conv_w2, L0_conv_b2, L0_conv_w3, L0_conv_b3, L0_conv_wf, L0_conv_bf)
    x = x + _L1_conv_ref(_gn(x), L1_conv_weights1, L1_conv_refine_weights1)
    x = x + _L2_conv_ref(_gn(x), L2_conv_alpha, L2_conv_beta, L2_conv_kernels)
    x = x + _L3_conv_ref(_gn(x), L3_conv_K)
    return x


_drawn_inputs = setup_inputs


def setup_inputs(seed=0):
    import zlib

    import numpy as np

    out = dict(_drawn_inputs(seed))
    spreads = {'L2_conv_alpha': (1.0, 0.2)}
    factors = {'L0_conv_b0': 5.384,
     'L0_conv_b1': 7.658,
     'L0_conv_w2': 8.0,
     'L0_conv_b3': 7.289,
     'L0_conv_bf': 64.0,
     'L1_conv_weights1': 64.0,
     'L1_conv_refine_weights1': 64.0}
    for name, (base, spread) in spreads.items():
        noise = np.random.default_rng([zlib.crc32(name.encode()), seed]).standard_normal(out[name].shape)
        drawn = base * np.exp(spread * noise) if base else spread * noise
        out[name] = jnp.asarray(drawn.astype(out[name].dtype))
    for name, factor in factors.items():
        out[name] = (out[name] * factor).astype(out[name].dtype)
    return out
```

```python
from contextlib import ExitStack

import concourse.bass as bass
from concourse import mybir

B, C, H, W = 8, 64, 128, 128
P = 128
G = 32
F = 32
EPS = 1e-5


def layer0_statistics(nc, t):
    F32 = mybir.dt.float32
    ALU = mybir.AluOpType
    ACT = mybir.ActivationFunctionType
    AX = mybir.AxisListType.X
    with ExitStack() as ctx:
        def sb(name, shape, dt=F32):
            return ctx.enter_context(nc.sbuf_tensor(name, shape, dt))

        def sem(name):
            return ctx.enter_context(nc.semaphore(name))

        ROWS = H // 2
        CH = 16
        NCH = ROWS // CH
        NBUF = 4
        XC = sb("st_x", [P, NBUF, CH * W])
        BS = sb("st_bn", [P, B, NCH * 4 * 6])
        EC = sb("st_edgecols", [P, B, NCH, 2])
        ER = sb("st_edgerow", [P, B, W])
        MV = sb("st_mv", [P, B, 2])
        EX = sb("st_ex", [P, 2, B])
        M = sb("st_m", [P, 2, B])
        VAR = sb("st_var", [P, B])
        RX = sb("st_rx", [P, 3, B])
        D = sb("st_d", [P, 3, B])
        ECS = sb("st_ecs", [P, B, 2])
        V = sb("st_v", [P, 9, B])
        V2 = sb("st_v2", [P, 9, B])
        taps = sb("st_w0taps", [P, 9, C])
        grp = sb("st_grp", [P, P])
        band = sb("st_band", [C, P])
        cnt = sb("st_cnt", [P, 9])
        half = sb("st_half", [P, 2])
        b0 = sb("st_b0", [C, 1])
        b12 = sb("st_b12", [P, 3])
        b3 = sb("st_b3", [P, 9])
        XM = sb("st_xm", [C, B])
        X2 = sb("st_x2", [P, B])
        STD = sb("st_std", [P, B])
        pg = ctx.enter_context(nc.psum_tensor("st_pg", [P, 2 * B], F32))
        pm = ctx.enter_context(nc.psum_tensor("st_pm", [C, B], F32))
        px = ctx.enter_context(nc.psum_tensor("st_px", [P, B], F32))
        p3 = ctx.enter_context(nc.psum_tensor("st_p3", [P, 9 * B], F32))

        chunk_in = [sem(f"st_chunk_in{n}") for n in range(NBUF)]
        const_in = sem("st_const_in")
        chunk_used = sem("st_chunk_used")
        chain = sem("st_chain")
        group_done = sem("st_group_done")
        std_done = sem("st_std_done")
        mean_done = sem("st_mean_done")
        xm_done = sem("st_xm_done")
        x2_done = sem("st_x2_done")
        x2_out = sem("st_x2_out")
        b3_done = sem("st_b3_done")

        C_EX = B + 3
        C_VAR = C_EX + 4
        C_V = C_VAR + 14 + 4 + 18

        block = ctx.enter_context(nc.Block())
        halves = t.x.rearrange("b c (h r) w -> b h c (r w)", h=2)

        @block.sync
        def _(sp):
            for q in range(NCH):
                for h in range(2):
                    sp.dma_start(XC[C * h:C * h + C, q, :], halves[0, h, :, q * CH * W:(q + 1) * CH * W])\
                        .then_inc(chunk_in[q], 16)
            with sp.Fori(1, B) as b:
                for q in range(NCH):
                    sp.wait_ge(chunk_used, b * NCH + (q + 1 - NCH))
                    for h in range(2):
                        sp.dma_start(XC[C * h:C * h + C, q, :], halves[b, h, :, q * CH * W:(q + 1) * CH * W])\
                            .then_inc(chunk_in[q], 16)

        @block.scalar
        def _(act):
            n = 0
            for dst, src in ((taps[:, :, :], t.w0taps), (grp[:, :], t.grp), (band[:, :], t.band),
                             (cnt[:, :], t.cnt), (half[:, :], t.half), (b0[:, :], t.b0[0:C, :]),
                             (b12[:, :], t.b12), (b3[:, :], t.b3), (t.w3f[:, :, :], t.w3blk),
                             (ER[0:C, :, :], t.x[:, :, 0, :].rearrange("b c w -> c b w")),
                             (ER[C:P, :, :], t.x[:, :, H - 1, :].rearrange("b c w -> c b w"))):
                act.dma_start(dst, src).then_inc(const_in, 16)
                n += 16
            act.wait_ge(chain, C_VAR)
            act.activation(STD[:, :], VAR[:, :], ACT.Sqrt).then_inc(std_done, 1)
            act.wait_ge(mean_done, 1)
            act.activation(XM[:, :], pm[:, :], ACT.Identity, scale=1.0 / (H * W), bias=b0[:, :]).then_inc(xm_done, 1)
            act.wait_ge(x2_done, 1)
            act.activation(X2[:, :], px[:, :], ACT.Identity, bias=b12[:, 2:3]).then_inc(x2_out, 1)
            act.wait_ge(x2_out, 1)
            act.activation(X2[:, :], X2[:, :], ACT.Identity, bias=b12[:, 0:1]).then_inc(x2_out, 1)

        N_CONST = 11 * 16

        @block.tensor
        def _(pe):
            pe.wait_ge(chain, C_EX)
            pe.matmul(pg[:, :], grp[:, :], EX[:, :, :].rearrange("p a b -> p (a b)"), start=True, stop=True)\
                .then_inc(group_done, 1)
            pe.wait_ge(chain, C_V)
            for k in range(9):
                last = pe.matmul(pm[:, :], taps[:, k, :], V[:, k, :], start=(k == 0), stop=(k == 8))
            last.then_inc(mean_done, 1)
            pe.wait_ge(xm_done, 1)
            pe.matmul(px[:, :], band[:, :], XM[:, :], start=True, stop=True).then_inc(x2_done, 1)
            pe.wait_ge(x2_out, 2)
            for k in range(9):
                last = pe.matmul(p3[:, k * B:(k + 1) * B], t.w3f[:, k, :], X2[:, :], start=True, stop=True)
            last.then_inc(b3_done, 1)

        @block.vector
        def _(dve):
            done = [0]

            def step(ins):
                done[0] += 1
                ins.then_inc(chain, 1)
                dve.wait_ge(chain, done[0])

            with dve.Fori(0, B) as b:
                for q in range(NCH):
                    dve.wait_ge(chunk_in[q], 32 * b + 32)
                    for j in range(4):
                        at = (4 * q + j) * 6
                        dve.bn_stats(BS[:, bass.ds(b, 1), at:at + 6], XC[:, q, 512 * j:512 * j + 512])
                    dve.tensor_reduce(EC[:, bass.ds(b, 1), q, :],
                                      XC[:, q, :].rearrange("p (r w) -> p w r", w=W)[:, 0:W:W - 1, :],
                                      AX, ALU.add).then_inc(chunk_used, 1)
            dve.wait_ge(chunk_used, NCH * B)
            for b in range(B):
                step(dve.bn_aggr(MV[:, b, :], BS[:, b, :]))
            dve.wait_ge(const_in, N_CONST)
            mean, var = MV[:, :, 0], MV[:, :, 1]
            step(dve.tensor_copy(EX[:, 0, :], mean))
            step(dve.tensor_tensor(EX[:, 1, :], mean, mean, ALU.mult))
            step(dve.tensor_tensor(EX[:, 1, :], EX[:, 1, :], var, ALU.add))
            assert done[0] == C_EX
            dve.wait_ge(group_done, 1)
            step(dve.tensor_copy(M[:, :, :].rearrange("p a b -> p (a b)"), pg[:, :]))
            step(dve.tensor_tensor(VAR[:, :], M[:, 0, :], M[:, 0, :], ALU.mult))
            step(dve.tensor_tensor(VAR[:, :], M[:, 1, :], VAR[:, :], ALU.subtract))
            step(dve.tensor_scalar(VAR[:, :], VAR[:, :], EPS, None, ALU.add))
            assert done[0] == C_VAR
            dve.wait_ge(std_done, 1)
            scale, shift = t.gn0[:, 0, :], t.gn0[:, 1, :]
            step(dve.reciprocal(scale, STD[:, :]))
            step(dve.tensor_tensor(STD[:, :], scale, scale, ALU.mult))
            step(dve.tensor_tensor(STD[:, :], STD[:, :], VAR[:, :], ALU.mult))
            step(dve.tensor_scalar(STD[:, :], STD[:, :], -0.5, 1.5, ALU.mult, ALU.add))
            step(dve.tensor_tensor(scale, scale, STD[:, :], ALU.mult))
            step(dve.scalar_tensor_tensor(shift, M[:, 0, :], -1.0, scale, ALU.mult, ALU.mult))
            step(dve.tensor_scalar(t.gn0[:, 2, :], scale, 1.0, None, ALU.add))
            step(dve.tensor_scalar(t.gn0[:, 3, :], shift, b12[:, 1:2], None, ALU.add))
            step(dve.tensor_reduce(ECS[:, :, :], EC[:, :, :, :].rearrange("p b q e -> p b e q"), AX, ALU.add))
            step(dve.tensor_scalar(D[:, 1, :], mean, float(ROWS * W), None, ALU.mult))
            step(dve.tensor_tensor(D[:, 0, :], D[:, 1, :], ECS[:, :, 1], ALU.subtract))
            step(dve.tensor_tensor(D[:, 2, :], D[:, 1, :], ECS[:, :, 0], ALU.subtract))
            step(dve.tensor_reduce(RX[:, 1, :], ER[:, :, :], AX, ALU.add))
            step(dve.tensor_tensor(RX[:, 0, :], RX[:, 1, :], ER[:, :, W - 1], ALU.subtract))
            step(dve.tensor_tensor(RX[:, 2, :], RX[:, 1, :], ER[:, :, 0], ALU.subtract))
            step(dve.tensor_copy(V2[:, 3:6, :], D[:, :, :]))
            step(dve.scalar_tensor_tensor(V2[:, 0:3, :], RX[:, :, :], half[:, 1:2], D[:, :, :], ALU.mult, ALU.add))
            step(dve.scalar_tensor_tensor(V2[:, 6:9, :], RX[:, :, :], half[:, 0:1], D[:, :, :], ALU.mult, ALU.add))
            for k in range(9):
                step(dve.tensor_tensor(V[:, k, :], V2[:, k, :], scale, ALU.mult))
                step(dve.scalar_tensor_tensor(V[:, k, :], shift, cnt[:, k:k + 1], V[:, k, :], ALU.mult, ALU.add))
            assert done[0] == C_V
            dve.wait_ge(b3_done, 1)
            for k in range(9):
                dve.tensor_scalar(t.b3p[:, :, k], p3[:, k * B:(k + 1) * B], b3[:, k:k + 1], None, ALU.add)\
                    .then_inc(chain, 1)
            dve.wait_ge(chain, done[0] + 9)


class Tile:

    def __init__(self, pair, offset, per_sample):
        self.n = 2 * pair + offset if offset else 2 * pair
        self.half = pair + offset // 2 if offset // 2 else pair
        self.s = offset % 2
        self.i = self.n % per_sample
        self.b = self.n // per_sample


def pipeline(eng, tiles, per_sample, offsets, body):
    lo, hi = -min(offsets.values()) + 2, tiles - max(offsets.values())
    hi -= (hi - lo) % 2

    def straight(g):
        body({k: Tile((g + o) // 2, (g + o) % 2, per_sample) if 0 <= g + o < tiles else None
              for k, o in offsets.items()})

    for g in range(-max(offsets.values()), lo):
        straight(g)
    with eng.Fori(0, (hi - lo) // 2) as n:
        for u in range(2):
            body({k: Tile(n, lo + u + o, per_sample) for k, o in offsets.items()})
    for g in range(hi, tiles - min(offsets.values())):
        straight(g)


def wait(eng, sem, value):
    if not isinstance(value, int) or value > 0:
        eng.wait_ge(sem, value)


def layer0_convolutions(nc, t):
    F32 = mybir.dt.float32
    F32R = mybir.dt.float32r
    ALU = mybir.AluOpType
    ACT = mybir.ActivationFunctionType
    SL = 4
    PER = H // 2 // SL
    TILES = B * PER
    WP = W + 2
    TAPS = 9
    LO = slice(0, C)
    UP = slice(C, P)
    with ExitStack() as ctx:
        def sb(name, shape, dt=F32):
            return ctx.enter_context(nc.sbuf_tensor(name, shape, dt))

        def sem(name):
            return ctx.enter_context(nc.semaphore(name))

        XT = sb("c_x", [P, 2, SL + 1, WP])
        XH = sb("c_xh", [P, 2, SL + 1, WP], F32R)
        XL = sb("c_xl", [P, 2, SL + 1, WP], F32R)
        X0E = sb("c_x0e", [P, H // 2, WP])
        X0O = sb("c_x0o", [P, H // 2 + 1, WP])
        Y = sb("c_y", [P, 2, SL * W])
        YH = sb("c_yh", [P, 2, SL * W], F32R)
        YL = sb("c_yl", [P, 2, SL * W], F32R)
        PR = sb("c_pr", [P, 6, SL * W])
        AC = sb("c_ac", [P, 2, SL * W])
        TE = sb("c_te", [P, 2, SL * W])
        TO = sb("c_to", [P, H // 2 + 1, WP])
        TH = sb("c_th", [P, 2, SL + 1, WP], F32R)
        TL = sb("c_tl", [P, 2, SL + 1, WP], F32R)
        XR = sb("c_xr", [P, 2, SL * W])
        OUT = sb("c_out", [P, 2, SL * W])
        mask = sb("c_mask", [P, PER])
        b0 = sb("c_b0", [P, 1])
        w1 = sb("c_w1", [P, TAPS])
        WS = sb("c_ws", [P, 6, P])
        W0H, W0L = sb("c_w0h", [P, 6, P], F32R), sb("c_w0l", [P, 6, P], F32R)
        WFH, WFL = sb("c_wfh", [P, 6, P], F32R), sb("c_wfl", [P, 6, P], F32R)
        W3H, W3L = sb("c_w3h", [P, TAPS, P], F32R), sb("c_w3l", [P, TAPS, P], F32R)
        p0 = [ctx.enter_context(nc.psum_tensor(f"c_p0{s}", [P, SL * W], F32)) for s in range(2)]
        p3 = [ctx.enter_context(nc.psum_tensor(f"c_p3{s}", [P, SL * W], F32)) for s in range(3)]
        pf = [ctx.enter_context(nc.psum_tensor(f"c_pf{s}", [P, SL * W], F32)) for s in range(2)]

        const_in = sem("c_const_in")
        ws_in = sem("c_ws_in")
        cleared = sem("c_cleared")
        w_hi = sem("c_w_hi")
        w_lo = sem("c_w_lo")
        xt_in = [sem(f"c_xt_in{s}") for s in range(2)]
        xr_in = [sem(f"c_xr_in{s}") for s in range(2)]
        xn_done = sem("c_xn_done")
        xh_done = sem("c_xh_done")
        xl_done = sem("c_xl_done")
        w0_done = sem("c_w0_done")
        x0_out = sem("c_x0_out")
        x0_odd = [sem(f"c_x0_odd{s}") for s in range(2)]
        dw_done = sem("c_dw_done")
        yh_done = sem("c_yh_done")
        yl_done = sem("c_yl_done")
        w3_done = sem("c_w3_done")
        mult_done = sem("c_mult_done")
        add_done = sem("c_add_done")
        lrelu_done = sem("c_lrelu_done")
        t_odd = [sem(f"c_t_odd{s}") for s in range(2)]
        th_done = sem("c_th_done")
        tl_done = sem("c_tl_done")
        wf_done = sem("c_wf_done")
        res_done = sem("c_res_done")
        fin_done = sem("c_fin_done")
        stored = [sem(f"c_stored{s}") for s in range(2)]

        block = ctx.enter_context(nc.Block())
        odd_rows = t.x_rows.rearrange("b c (r e) w -> e b c r w", e=2)
        even_rows = t.x.rearrange("b c (r e) w -> e b c r w", e=2)
        out_rows = t.x1.rearrange("b c (r e) w -> e b c r w", e=2)

        def at(tile, pairs=SL, off=0):
            return bass.ds(tile.i * SL + off, pairs)

        def rows(ap):
            return ap.rearrange("p (r w) -> p r w", w=W)

        @block.sync
        def _(sp):
            for dst, src in ((mask[:, :], t.mask), (b0[:, :], t.b0), (w1[:, :], t.w1)):
                sp.dma_start(dst, src).then_inc(const_in, 16)
            sp.dma_start(WS[:, :, :], t.w0blk).then_inc(ws_in, 16)
            wait(sp, w_lo, 1)
            sp.dma_start(WS[:, :, :], t.wfblk).then_inc(ws_in, 16)
            sp.wait_ge(cleared, 1)

            def body(at_stage):
                if x0 := at_stage["x0"]:
                    sp.wait_ge(x0_out, x0.n + 1)
                    wait(sp, x0_odd[x0.s], 32 * x0.half)
                    sp.dma_start(X0O[UP, at(x0), :], X0E[LO, at(x0), :]).then_inc(x0_odd[x0.s], 16)
                    sp.dma_start(X0O[LO, at(x0, off=1), :], X0E[UP, at(x0), :]).then_inc(x0_odd[x0.s], 16)
                if l := at_stage["lrelu"]:
                    sp.wait_ge(lrelu_done, l.n + 1)
                    sp.dma_start(TO[UP, at(l), 1:W + 1], rows(TE[LO, l.s, :])).then_inc(t_odd[l.s], 16)
                    sp.dma_start(TO[LO, at(l, off=1), 1:W + 1], rows(TE[UP, l.s, :])).then_inc(t_odd[l.s], 16)
                if f := at_stage["fin"]:
                    sp.wait_ge(fin_done, f.n + 1)
                    for e, half in enumerate((LO, UP)):
                        sp.dma_start(out_rows[e, f.b, :, bass.ds(f.i * SL, SL), :], rows(OUT[half, f.s, :]))\
                            .then_inc(stored[f.s], 16)
                if r := at_stage["xr"]:
                    wait(sp, fin_done, r.n - 1)
                    for e, half in enumerate((LO, UP)):
                        sp.dma_start(rows(XR[half, r.s, :]), even_rows[e, r.b, :, bass.ds(r.i * SL, SL), :])\
                            .then_inc(xr_in[r.s], 16)
                if x := at_stage["xt"]:
                    wait(sp, xl_done, x.n - 1)
                    for e, half in enumerate((LO, UP)):
                        sp.dma_start(XT[half, x.s, :, 1:W + 1],
                                     odd_rows[e, x.b, :, bass.ds(x.i * SL, SL + 1), :]).then_inc(xt_in[x.s], 16)

            pipeline(sp, TILES, PER, {"xt": 7, "x0": 4, "lrelu": -1, "xr": -3, "fin": -5}, body)
            for s in range(2):
                sp.wait_ge(stored[s], 32 * TILES // 2)

        @block.gpsimd
        def _(pool):
            def add(m, j):
                pool.wait_ge(mult_done, 9 * m.n + (j + 1))
                if j == 1:
                    wait(pool, lrelu_done, m.n - 1)
                    pool.tensor_tensor(AC[:, m.s, :], PR[:, (9 * m.s) % 6, :], PR[:, (9 * m.s + 1) % 6, :],
                                       ALU.add).then_inc(add_done, 1)
                else:
                    pool.wait_ge(add_done, 8 * m.n + (j - 1))
                    pool.tensor_tensor(AC[:, m.s, :], AC[:, m.s, :], PR[:, (9 * m.s + j) % 6, :],
                                       ALU.add).then_inc(add_done, 1)

            def body(at_stage):
                m = at_stage["main"]
                if ts := at_stage["tsplit"]:
                    pool.wait_ge(th_done, ts.n + 1)
                    wait(pool, wf_done, ts.n - 1)
                    pool.tensor_tensor(TL[:, ts.s, :, :], TO[:, at(ts, SL + 1), :], TH[:, ts.s, :, :],
                                       ALU.subtract).then_inc(tl_done, 1)
                for j in range(1, 4):
                    if m:
                        add(m, j)
                if y := at_stage["ysplit"]:
                    pool.wait_ge(yh_done, y.n + 1)
                    pool.tensor_tensor(YL[:, y.s, :], Y[:, y.s, :], YH[:, y.s, :], ALU.subtract).then_inc(yl_done, 1)
                for j in range(4, 7):
                    if m:
                        add(m, j)
                if x := at_stage["norm"]:
                    pool.wait_ge(xh_done, x.n + 1)
                    pool.tensor_tensor(XL[:, x.s, :, :], XT[:, x.s, :, :], XH[:, x.s, :, :],
                                       ALU.subtract).then_inc(xl_done, 1)
                for j in range(7, 9):
                    if m:
                        add(m, j)

            pipeline(pool, TILES, PER, {"norm": 6, "ysplit": 1, "main": 0, "tsplit": -3}, body)

        @block.scalar
        def _(act):
            act.wait_ge(ws_in, 16)
            act.activation(W0H[:, :, :], WS[:, :, :], ACT.Copy).then_inc(w_hi, 1)
            act.activation(W3H[:, :, :], t.w3f[:, :, :], ACT.Copy).then_inc(w_hi, 1)
            act.wait_ge(ws_in, 32)
            act.activation(WFH[:, :, :], WS[:, :, :], ACT.Copy).then_inc(w_hi, 1)
            act.wait_ge(const_in, 48)
            act.wait_ge(cleared, 1)

            def body(at_stage):
                if ts := at_stage["tsplit"]:
                    nxt = ts.half + (ts.s + 1) // 2
                    act.wait_ge(t_odd[ts.s], 32 * ts.half + 32)
                    if not (isinstance(ts.n, int) and ts.n == TILES - 1):
                        act.wait_ge(t_odd[1 - ts.s], 32 * nxt + 32)
                    wait(act, wf_done, ts.n - 1)
                    act.activation(TH[:, ts.s, :, :], TO[:, at(ts, SL + 1), :], ACT.Copy).then_inc(th_done, 1)
                if y := at_stage["ysplit"]:
                    act.wait_ge(dw_done, 9 * y.n + 9)
                    wait(act, w3_done, 9 * y.n - 9)
                    act.activation(YH[:, y.s, :], Y[:, y.s, :], ACT.Copy).then_inc(yh_done, 1)
                if x0 := at_stage["x0"]:
                    act.wait_ge(w0_done, x0.n + 1)
                    act.activation(X0E[:, at(x0), 1:W + 1], rows(p0[x0.s][:, :]), ACT.Identity,
                                   bias=b0[:, :]).then_inc(x0_out, 1)
                if x := at_stage["norm"]:
                    act.wait_ge(xt_in[x.s], 32 * x.half + 32)
                    act.activation(XT[:, x.s, :, 1:W + 1], XT[:, x.s, :, 1:W + 1], ACT.Identity,
                                   scale=t.gn0[:, 0, bass.ds(x.b, 1)], bias=t.gn0[:, 1, bass.ds(x.b, 1)])\
                        .then_inc(xn_done, 1)
                    act.wait_ge(xn_done, 3 * x.n + 1)
                    act.activation(XT[LO, x.s, 0, :], XT[LO, x.s, 0, :], ACT.Copy,
                                   scale=mask[LO, bass.ds(x.i, 1)]).then_inc(xn_done, 1)
                    act.activation(XT[UP, x.s, SL, :], XT[UP, x.s, SL, :], ACT.Copy,
                                   scale=mask[UP, bass.ds(x.i, 1)]).then_inc(xn_done, 1)
                    act.wait_ge(xn_done, 3 * x.n + 3)
                    wait(act, w0_done, x.n - 1)
                    act.activation(XH[:, x.s, :, :], XT[:, x.s, :, :], ACT.Copy).then_inc(xh_done, 1)
                if f := at_stage["res"]:
                    act.wait_ge(xr_in[f.s], 32 * f.half + 32)
                    act.activation(XR[:, f.s, :], XR[:, f.s, :], ACT.Identity,
                                   scale=t.gn0[:, 2, bass.ds(f.b, 1)], bias=t.gn0[:, 3, bass.ds(f.b, 1)])\
                        .then_inc(res_done, 1)

            pipeline(act, TILES, PER, {"norm": 6, "x0": 4, "ysplit": 1, "tsplit": -3, "res": -4}, body)

        @block.tensor
        def _(pe):
            pe.wait_ge(w_hi, 3)
            pe.wait_ge(w_lo, 3)

            def conv(psum, wh, wl, xh, xl, s):
                todo = []
                for n in range(6):
                    d, dx = divmod(n, 3)
                    for w, x in ((wh, xh), (wh, xl), (wl, xh)):
                        todo.append((psum[s], w[:, n, :], x[:, s, d:d + SL, dx:dx + W]))
                return todo

            def body(at_stage):
                jobs = []
                if a := at_stage["w0"]:
                    pe.wait_ge(xh_done, a.n + 1)
                    pe.wait_ge(xl_done, a.n + 1)
                    wait(pe, x0_out, a.n - 1)
                    jobs.append((conv(p0, W0H, W0L, XH, XL, a.s), w0_done))
                if f := at_stage["wf"]:
                    pe.wait_ge(th_done, f.n + 1)
                    pe.wait_ge(tl_done, f.n + 1)
                    wait(pe, fin_done, f.n - 1)
                    jobs.append((conv(pf, WFH, WFL, TH, TL, f.s), wf_done))
                others = [(o, w, x, n == 0, n == len(job) - 1, s) for job, s in jobs for n, (o, w, x) in enumerate(job)]
                m = at_stage["main"]

                def some(n):
                    for o, w, x, first, final, s in others[:n]:
                        ins = pe.matmul(o[:, :], w, x, start=first, stop=final)
                        if final:
                            ins.then_inc(s, 1)
                    del others[:n]

                if m:
                    pe.wait_ge(yh_done, m.n + 1)
                    pe.wait_ge(yl_done, m.n + 1)
                    for k in range(TAPS):
                        wait(pe, mult_done, 9 * m.n + (k - 2))
                        for n, (w, y) in enumerate(((W3H, YH), (W3H, YL), (W3L, YH))):
                            last = pe.matmul(p3[k % 3][:, :], w[:, k, :], y[:, m.s, :], start=(n == 0), stop=(n == 2))
                        last.then_inc(w3_done, 1)
                        some(4)
                some(len(others))

            pipeline(pe, TILES, PER, {"w0": 5, "main": 0, "wf": -4}, body)

        @block.vector
        def _(dve):
            for s in range(2):
                dve.memset(XT[:, s, :, 0:WP:W + 1], 0.0)
            dve.memset(X0E[:, :, 0:WP:W + 1], 0.0)
            for buf in (X0O, TO):
                dve.memset(buf[:, :, 0:WP:W + 1], 0.0)
                dve.memset(buf[LO, 0, 1:W + 1], 0.0)
                last = dve.memset(buf[UP, H // 2, 1:W + 1], 0.0)
            last.then_inc(cleared, 1)
            dve.wait_ge(w_hi, 1)
            dve.tensor_tensor(W0L[:, :, :], WS[:, :, :], W0H[:, :, :], ALU.subtract).then_inc(w_lo, 1)
            dve.wait_ge(w_hi, 2)
            dve.tensor_tensor(W3L[:, :, :], t.w3f[:, :, :], W3H[:, :, :], ALU.subtract).then_inc(w_lo, 1)
            dve.wait_ge(w_hi, 3)
            dve.tensor_tensor(WFL[:, :, :], WS[:, :, :], WFH[:, :, :], ALU.subtract).then_inc(w_lo, 1)
            dve.wait_ge(const_in, 48)

            def shifted(tile, k):
                dy, dx = divmod(k, 3)
                if dy == 1:
                    return X0E[:, at(tile), dx:dx + W]
                return X0O[:, at(tile, off=dy // 2), dx:dx + W]

            def body(at_stage):
                m, d = at_stage["main"], at_stage["dw"]
                if d:
                    nxt = d.half + (d.s + 1) // 2
                    dve.wait_ge(x0_odd[d.s], 32 * d.half + 32)
                    if not (isinstance(d.n, int) and d.n == TILES - 1):
                        dve.wait_ge(x0_odd[1 - d.s], 32 * nxt + 32)
                for k in range(TAPS):
                    if m:
                        n = 9 * m.s + k
                        dve.wait_ge(w3_done, 9 * m.n + (k + 1))
                        wait(dve, add_done, 8 * m.n + (max(1, k - 6) if k >= 6 else k - 5))
                        dve.scalar_tensor_tensor(rows(PR[:, n % 6, :]), rows(p3[k % 3][:, :]),
                                                 t.b3p[:, bass.ds(m.b, 1), k], shifted(m, k),
                                                 ALU.add, ALU.mult).then_inc(mult_done, 1)
                    if d:
                        y = rows(Y[:, d.s, :])
                        if k == 0:
                            wait(dve, yl_done, d.n - 1)
                            dve.tensor_scalar(y, shifted(d, k), w1[:, 0:1], None, ALU.mult).then_inc(dw_done, 1)
                        else:
                            dve.wait_ge(dw_done, 9 * d.n + k)
                            dve.scalar_tensor_tensor(y, shifted(d, k), w1[:, k:k + 1], y, ALU.mult, ALU.add)\
                                .then_inc(dw_done, 1)
                    if k == 3 and (l := at_stage["lrelu"]):
                        dve.wait_ge(add_done, 8 * l.n + 8)
                        wait(dve, t_odd[l.s], 32 * l.half)
                        dve.scalar_tensor_tensor(TE[:, l.s, :], AC[:, l.s, :], 0.2, AC[:, l.s, :],
                                                 ALU.mult, ALU.max).then_inc(lrelu_done, 1)
                    if k == 6 and (f := at_stage["fin"]):
                        dve.wait_ge(wf_done, f.n + 1)
                        dve.wait_ge(res_done, f.n + 1)
                        wait(dve, stored[f.s], 32 * f.half)
                        dve.tensor_tensor(OUT[:, f.s, :], pf[f.s][:, :], XR[:, f.s, :], ALU.add).then_inc(fin_done, 1)

            pipeline(dve, TILES, PER, {"dw": 2, "main": 0, "lrelu": -1, "fin": -5}, body)


CT = 4
TILES_C = C // CT
MODES = F // 2 * F


def of_sample(tensor, b):
    if isinstance(b, int):
        return tensor[:, b]
    ap = tensor[:, bass.ds(b, 1)]
    return ap.rearrange("p o a c -> p (o a) c") if len(ap.shape) == 4 else ap.rearrange("p o a -> p (o a)")


class Chain:

    def __init__(self, eng, sem, length, turn):
        self.eng, self.sem, self.base, self.n, self.length = eng, sem, turn * length, 0, length

    def __call__(self, ins):
        self.n += 1
        ins.then_inc(self.sem, 1)
        self.eng.wait_ge(self.sem, self.base + self.n)


CHAIN = 12
CHAIN_SUMS, CHAIN_VAR = 3, 7


def group_scale_steps(dve, step, s, sums_done, sums, std_done, std, turn):
    ALU = mybir.AluOpType
    bn = s.bn[:, :, :].rearrange("p g (e k) -> p (g e) k", k=3)
    mean, m2 = bn[:, :, 1], bn[:, :, 2]
    step(dve.tensor_copy(s.sums[:, 0, :], mean))
    step(dve.tensor_tensor(s.sq[:, :], mean, mean, ALU.mult))
    step(dve.scalar_tensor_tensor(s.sums[:, 1, :], m2, 1.0 / W, s.sq[:, :], ALU.mult, ALU.add))
    dve.wait_ge(sums_done, turn + 1)
    step(dve.tensor_reduce(s.ms[:, :], sums[:, :].rearrange("p (g e) -> p g e", e=2), mybir.AxisListType.X, ALU.add))
    m, e2 = s.ms[:, 0:G], s.ms[:, G:2 * G]
    step(dve.tensor_tensor(s.var[:, :], m, m, ALU.mult))
    step(dve.tensor_tensor(s.var[:, :], e2, s.var[:, :], ALU.subtract))
    step(dve.tensor_scalar(s.var[:, :], s.var[:, :], EPS, None, ALU.add))
    dve.wait_ge(std_done, turn + 1)
    step(dve.reciprocal(s.r[:, :], std[:, :]))
    step(dve.tensor_tensor(s.t[:, :], s.r[:, :], s.r[:, :], ALU.mult))
    step(dve.tensor_tensor(s.t[:, :], s.t[:, :], s.var[:, :], ALU.mult))
    step(dve.tensor_scalar(s.t[:, :], s.t[:, :], -0.5, 1.5, ALU.mult, ALU.add))
    step(dve.tensor_tensor(s.r[:, :], s.r[:, :], s.t[:, :], ALU.mult))


class GroupScaleBuffers:
    def __init__(self, sb, name):
        F32 = mybir.dt.float32
        self.bn = sb(name + "_bn", [P, G, 6], F32)
        self.sums = sb(name + "_sums", [P, 2, 2 * G], F32)
        self.sq = sb(name + "_sq", [P, 2 * G], F32)
        self.ms = sb(name + "_ms", [P, 2 * G], F32)
        self.var = sb(name + "_var", [P, G], F32)
        self.std = sb(name + "_std", [P, G], F32)
        self.r = sb(name + "_r", [P, G], F32)
        self.t = sb(name + "_t", [P, G], F32)


def forward_rows(pe, psum, x, basis, q):
    for c in range(CT):
        last = pe.matmul(psum[:, c * P:(c + 1) * P], x[:, CT * q + c, :], basis[:, :], start=True, stop=True)
    return last


def forward_columns(pe, psum, T, basis):
    for u in range(F):
        half, u1 = divmod(u, F // 2)
        for k in range(4):
            last = pe.matmul(psum[C * half:C * half + C, u1 * F:(u1 + 1) * F], T[:, k * F + u, :],
                             basis[:, k, :], start=(k == 0), stop=(k == 3))
    return last


def tile_of_T(T, psum, q):
    return (T[:, :, CT * q:CT * q + CT],
            psum[:, :].rearrange("p (c k) -> p k c", c=CT))


class Mixing:

    QM = 128
    CHUNKS = MODES // QM
    EIGHT = 8

    def __init__(self, nc, ctx, sb, sem, name, hd, wt, out, banks):
        self.hd, self.wt, self.out, self.banks = hd, wt, out, banks
        self.w_in = [sem(f"{name}_w_in{s}") for s in range(2)]
        self.old_in = [sem(f"{name}_old_in{s}") for s in range(2)]
        self.hd_done = sem(f"{name}_hd_done")
        self.pe_done = sem(f"{name}_pe_done")
        self.out_done = sem(f"{name}_out_done")
        self.stored = [sem(f"{name}_stored{s}") for s in range(2)]

    def load(self, sp, weights, q):
        s = q % 2
        if q >= 2:
            sp.wait_ge(self.pe_done, 16 * (q - 1))
        for half in range(2):
            x = F // 2 * half + 4 * q
            sp.dma_start(self.wt[s][C * half:C * half + C, :, :],
                         weights[:, :, x:x + 4, :].rearrange("i o x y -> i o (x y)")).then_inc(self.w_in[s], 16)

    def load_old(self, sp, old, q):
        s = q % 2
        if q >= 2:
            sp.wait_ge(self.stored[s], 16)
        sp.dma_start(self.out[s], old[:, q * self.QM:(q + 1) * self.QM, :].rearrange("p m o -> p (m o)"))\
            .then_inc(self.old_in[s], 16)

    def store(self, sp, new, q):
        s = q % 2
        sp.wait_ge(self.out_done, 16 * q + 16)
        sp.dma_start(new[:, q * self.QM:(q + 1) * self.QM, :].rearrange("p m o -> p (m o)"), self.out[s])\
            .then_inc(self.stored[s], 16)

    def spread(self, dve, H, q):
        s = q % 2
        if q >= 2:
            dve.wait_ge(self.pe_done, 16 * (q - 1))
        for half in range(2):
            last = dve.tensor_copy(
                self.hd[C * half:C * half + C, s, :, B * half:B * half + B],
                H[C * half:C * half + C, :, q * self.QM:(q + 1) * self.QM].rearrange("p b m -> p m b"))
        last.then_inc(self.hd_done, 1)

    def multiply(self, pe, q):
        s = q % 2
        pe.wait_ge(self.w_in[s], 32 * (q // 2) + 32)
        pe.wait_ge(self.hd_done, q + 1)
        for n in range(self.QM // self.EIGHT):
            at = 16 * q + n
            if at >= len(self.banks):
                pe.wait_ge(self.out_done, at - len(self.banks) + 1)
            bank = self.banks[at % len(self.banks)]
            for j in range(self.EIGHT):
                m = n * self.EIGHT + j
                last = pe.matmul(bank[0:2 * B, C * j:C * j + C], self.hd[:, s, m, :], self.wt[s][:, :, m],
                                 start=True, stop=True)
            last.then_inc(self.pe_done, 1)

    def take(self, dve, q, add):
        s = q % 2
        if add:
            dve.wait_ge(self.old_in[s], 16 * (q // 2) + 16)
        elif q >= 2:
            dve.wait_ge(self.stored[s], 16 * (q // 2))
        for n in range(16):
            at = 16 * q + n
            dve.wait_ge(self.pe_done, at + 1)
            bank = self.banks[at % len(self.banks)]
            dst = self.out[s][:, n * 512:(n + 1) * 512]
            if add:
                ins = dve.tensor_tensor(dst, dst, bank[0:2 * B, :], mybir.AluOpType.add)
            else:
                ins = dve.tensor_copy(dst, bank[0:2 * B, :])
            ins.then_inc(self.out_done, 1)


def layer1_analyse(nc, t):
    F32 = mybir.dt.float32
    ALU = mybir.AluOpType
    ACT = mybir.ActivationFunctionType
    with ExitStack() as ctx:
        def sb(name, shape, dt=F32):
            return ctx.enter_context(nc.sbuf_tensor(name, shape, dt))

        def sem(name):
            return ctx.enter_context(nc.semaphore(name))

        def pb(name):
            return ctx.enter_context(nc.psum_tensor(name, [P, 512], F32))

        X = sb("a_x", [P, 2, C, W])
        T = sb("a_t", [P, P, C])
        HM = sb("a_h", [P, B, MODES])
        WT = sb("a_w", [P, 2, C, 128])
        HD = sb("a_hd", [P, 2, 128, 2 * B])
        rows_basis = sb("a_rows", [P, P])
        cols_basis = sb("a_cols", [P, 4, F])
        ones = sb("a_ones", [P, P])
        st = GroupScaleBuffers(sb, "a_gs")
        SC = sb("a_sc", [P, 2, 2, G])
        pT = [pb(f"a_pt{i}") for i in range(4)]
        pH = pb("a_ph")
        pS = ctx.enter_context(nc.psum_tensor("a_ps", [P, 4 * G], F32))

        const_in = sem("a_const_in")
        ones_set = sem("a_ones_set")
        cleared = sem("a_cleared")
        x_in = [sem(f"a_x_in{s}") for s in range(2)]
        bn_done = sem("a_bn_done")
        chain = sem("a_chain")
        sums_done = sem("a_sums_done")
        std_done = sem("a_std_done")
        scale_done = sem("a_scale_done")
        scale_saved = sem("a_scale_saved")
        norm_done = sem("a_norm_done")
        rows_done = sem("a_rows_done")
        t_out = sem("a_t_out")
        cols_done = sem("a_cols_done")
        h_out = sem("a_h_out")
        mix = Mixing(nc, ctx, sb, sem, "a_mix", HD, [WT[:, s, :, :] for s in range(2)],
                     [X[0:2 * B, s, :, :].rearrange("p c w -> p (c w)") for s in range(2)], pT)

        block = ctx.enter_context(nc.Block())
        x1 = t.x1.rearrange("b c h w -> b h c w")

        @block.sync
        def _(sp):
            for dst, src in ((rows_basis[:, :], t.fwd_rows), (cols_basis[:, :, :], t.fwd_cols)):
                sp.dma_start(dst, src).then_inc(const_in, 16)

            def load(b, s):
                for c in range(0, C, 8):
                    sp.dma_start(X[:, s, c:c + 8, :], x1[b, :, c:c + 8, :]).then_inc(x_in[s], 16)

            load(0, 0)
            load(1, 1)
            mix.load(sp, t.weights1, 0)
            mix.load(sp, t.weights1, 1)
            with sp.Fori(1, B // 2) as bb:
                for s in range(2):
                    sp.wait_ge(rows_done, TILES_C * (2 * bb + (s - 1)))
                    load(2 * bb + s, s)
            for q in range(2, mix.CHUNKS):
                mix.load(sp, t.weights1, q)
                mix.store(sp, t.o_ht, q - 2)
            for q in range(mix.CHUNKS - 2, mix.CHUNKS):
                mix.store(sp, t.o_ht, q)
            for s in range(2):
                sp.wait_ge(mix.stored[s], 32)

        @block.scalar
        def _(act):
            def std(b):
                act.wait_ge(chain, CHAIN * b + CHAIN_VAR)
                act.activation(st.std[:, :], st.var[:, :], ACT.Sqrt).then_inc(std_done, 1)

            def normalise(b, s):
                act.wait_ge(scale_done, b + 1)
                for g in range(G):
                    last = act.activation(X[:, s, 2 * g:2 * g + 2, :], X[:, s, 2 * g:2 * g + 2, :], ACT.Identity,
                                          scale=SC[:, s, 0, g:g + 1], bias=SC[:, s, 1, g:g + 1])
                last.then_inc(norm_done, 1)

            def body(b, s, more):
                if more:
                    std(b + 1)
                act.wait_ge(cols_done, b + 1)
                for q in range(TILES_C):
                    act.wait_ge(rows_done, TILES_C * b + (q + 1))
                    dst, src = tile_of_T(T, pT[q % 4], q)
                    act.activation(dst, src, ACT.Copy).then_inc(t_out, 1)
                if more:
                    normalise(b + 1, 1 - s)

            act.nop().then_inc(t_out, 4)
            std(0)
            normalise(0, 0)
            with act.Fori(0, B // 2 - 1) as bb:
                for s in range(2):
                    body(2 * bb + s, s, True)
            body(B - 2, 0, True)
            body(B - 1, 1, False)

        @block.tensor
        def _(pe):
            def sums(b):
                pe.wait_ge(chain, CHAIN * b + CHAIN_SUMS)
                pe.matmul(pS[:, :], ones[:, :], st.sums[:, :, :].rearrange("p a g -> p (a g)"), start=True, stop=True)\
                    .then_inc(sums_done, 1)

            def body(b, s, more):
                if more:
                    sums(b + 1)
                pe.wait_ge(norm_done, b + 1)
                for q in range(TILES_C):
                    pe.wait_ge(t_out, TILES_C * b + (q + 1))
                    forward_rows(pe, pT[q % 4], X[:, s, :, :], rows_basis, q).then_inc(rows_done, 1)
                pe.wait_ge(t_out, TILES_C * b + (TILES_C + 4))
                pe.wait_ge(h_out, b + 1)
                forward_columns(pe, pH, T, cols_basis).then_inc(cols_done, 1)

            pe.nop().then_inc(cols_done, 1)
            pe.wait_ge(const_in, 32)
            pe.wait_ge(ones_set, 1)
            sums(0)
            with pe.Fori(0, B // 2 - 1) as bb:
                for s in range(2):
                    body(2 * bb + s, s, True)
            body(B - 2, 0, True)
            body(B - 1, 1, False)
            pe.wait_ge(t_out, TILES_C * B + 4)
            for q in range(mix.CHUNKS):
                mix.multiply(pe, q)

        @block.vector
        def _(dve):
            def scales(b, s):
                dve.wait_ge(x_in[s], 128 * (b // 2) + 128)
                for g in range(G):
                    last = dve.bn_stats(st.bn[:, g, :], X[:, s, 2 * g:2 * g + 2, :].rearrange("p c w -> p (c w)"))
                last.then_inc(bn_done, 1)
                dve.wait_ge(bn_done, b + 1)
                step = Chain(dve, chain, CHAIN, b)
                group_scale_steps(dve, step, st, sums_done, pS, std_done, st.std, b)
                scale, shift = SC[:, s, 0, :], SC[:, s, 1, :]
                dve.tensor_copy(scale, st.r[:, :])
                dve.scalar_tensor_tensor(shift, st.ms[:, 0:G], -1.0, st.r[:, :], ALU.mult, ALU.mult).then_inc(scale_done, 1)
                dve.wait_ge(scale_done, b + 1)
                dve.tensor_copy(of_sample(t.gn1, b), SC[:, s, :, :]).then_inc(scale_saved, 1)
                dve.wait_ge(scale_saved, b + 1)

            def body(b, s, more):
                if more:
                    scales(b + 1, 1 - s)
                dve.wait_ge(cols_done, b + 2)
                dve.tensor_copy(of_sample(HM, b), pH[:, :])\
                    .then_inc(h_out, 1)

            dve.memset(ones[:, :], 1.0 / 256).then_inc(ones_set, 1)
            dve.memset(HD[:, :, :, :], 0.0).then_inc(cleared, 1)
            dve.wait_ge(cleared, 1)
            dve.nop().then_inc(h_out, 1)
            scales(0, 0)
            with dve.Fori(0, B // 2 - 1) as bb:
                for s in range(2):
                    body(2 * bb + s, s, True)
            body(B - 2, 0, True)
            body(B - 1, 1, False)
            dve.wait_ge(h_out, B + 1)
            for q in range(2):
                mix.spread(dve, HM, q)
            for q in range(mix.CHUNKS):
                mix.take(dve, q, False)
                if q + 2 < mix.CHUNKS:
                    mix.spread(dve, HM, q + 2)


def inverse_columns(pe, psum, O, basis, q):
    for c in range(CT):
        last = pe.matmul(psum[:, c * W:(c + 1) * W], O[:, :, CT * q + c], basis[:, :], start=True, stop=True)
    return last


def inverse_rows(pe, psum, Z, basis):
    return pe.matmul(psum[:, :], basis[:, :], Z, start=True, stop=True)


def load_diagonal(sp, O, o_ht, b, sem):
    src = o_ht.rearrange("(h b) (u v) o -> b h v u o", h=2, v=F)
    for k in range(4):
        for half in range(2):
            u = F * k + F // 2 * half
            sp.dma_start(O[F * k:F * k + F, u:u + F // 2, :], src[b, half, :, :, :]).then_inc(sem, 16)


def layer1_refine(nc, t):
    F32 = mybir.dt.float32
    ALU = mybir.AluOpType
    ACT = mybir.ActivationFunctionType
    ERR_TH = 0.1
    with ExitStack() as ctx:
        def sb(name, shape, dt=F32):
            return ctx.enter_context(nc.sbuf_tensor(name, shape, dt))

        def sem(name):
            return ctx.enter_context(nc.semaphore(name))

        def pb(name):
            return ctx.enter_context(nc.psum_tensor(name, [P, 512], F32))

        X = sb("r_x", [P, 2, C, W])
        O = sb("r_o", [P, P, C])
        T = sb("r_t", [P, P, C])
        HM = sb("r_h", [P, B, MODES])
        WT = sb("r_w", [P, C, 128])
        HD = sb("r_hd", [P, 2, 128, 2 * B])
        Z = sb("r_z", [P, 2, CT * W])
        D = sb("r_d", [P, 3, CT * W])
        SC = sb("r_sc", [P, 2, 2, G])
        rows_basis = sb("r_rows", [P, P])
        cols_basis = sb("r_cols", [P, 4, F])
        inv_cols = sb("r_icols", [P, W])
        inv_rows = sb("r_irows", [P, P])
        pZ = [pb(f"r_pz{i}") for i in range(2)]
        pR = [pb(f"r_pr{i}") for i in range(2)]
        pT = [pb(f"r_pt{i}") for i in range(3)]
        pH = pb("r_ph")

        const_in = sem("r_const_in")
        cleared = sem("r_cleared")
        x_in = [sem(f"r_x_in{s}") for s in range(2)]
        o_in = sem("r_o_in")
        sc_ready = sem("r_sc_ready")
        norm_done = sem("r_norm_done")
        icols_done = sem("r_icols_done")
        z_out = sem("r_z_out")
        irows_done = sem("r_irows_done")
        diff_done = sem("r_diff_done")
        abs_done = sem("r_abs_done")
        masked = sem("r_masked")
        rows_done = sem("r_rows_done")
        t_out = sem("r_t_out")
        cols_done = sem("r_cols_done")
        h_out = sem("r_h_out")
        mix = Mixing(nc, ctx, sb, sem, "r_mix", HD,
                     [WT, O[:, :, :].rearrange("p a b -> p (a b)").rearrange("p (o m) -> p o m", o=C)],
                     [X[0:2 * B, s, :, :].rearrange("p c w -> p (c w)") for s in range(2)], [*pT, *pR])
        NT = TILES_C

        block = ctx.enter_context(nc.Block())
        x1 = t.x1.rearrange("b c h w -> b h c w")

        @block.sync
        def _(sp):
            for dst, src in ((rows_basis[:, :], t.fwd_rows), (cols_basis[:, :, :], t.fwd_cols),
                             (inv_cols[:, :], t.inv_cols), (inv_rows[:, :], t.inv_rows)):
                sp.dma_start(dst, src).then_inc(const_in, 16)

            def load(b, s):
                for c in range(0, C, 8):
                    sp.dma_start(X[:, s, c:c + 8, :], x1[b, :, c:c + 8, :]).then_inc(x_in[s], 16)

            load(0, 0)
            sp.wait_ge(cleared, 1)
            load_diagonal(sp, O, t.o_ht, 0, o_in)
            load(1, 1)
            mix.load(sp, t.refine1, 0)

            def body(b, s, load_x):
                sp.wait_ge(icols_done, NT * b + NT)
                load_diagonal(sp, O, t.o_ht, b + 1, o_in)
                if load_x:
                    sp.wait_ge(rows_done, NT * b + NT)
                    load(b + 2, s)

            with sp.Fori(0, B // 2 - 1) as bb:
                for s in range(2):
                    body(2 * bb + s, s, True)
            body(B - 2, 0, False)
            sp.wait_ge(rows_done, NT * B)
            mix.load(sp, t.refine1, 1)
            mix.load_old(sp, t.o_ht, 0)
            mix.load_old(sp, t.o_ht, 1)
            for q in range(2, mix.CHUNKS):
                mix.load(sp, t.refine1, q)
                mix.store(sp, t.o_sum, q - 2)
                mix.load_old(sp, t.o_ht, q)
            for q in range(mix.CHUNKS - 2, mix.CHUNKS):
                mix.store(sp, t.o_sum, q)
            for s in range(2):
                sp.wait_ge(mix.stored[s], 32)


        @block.scalar
        def _(act):
            def normalise(b, s, q):
                for g in (2 * q, 2 * q + 1):
                    last = act.activation(X[:, s, 2 * g:2 * g + 2, :], X[:, s, 2 * g:2 * g + 2, :], ACT.Identity,
                                          scale=SC[:, s, 0, g:g + 1], bias=SC[:, s, 1, g:g + 1])
                last.then_inc(norm_done, 1)

            def body(b, s, more):
                if more:
                    act.wait_ge(sc_ready, b + 2)
                    act.wait_ge(x_in[1 - s], 128 * ((b + 1) // 2) + 128)
                act.wait_ge(cols_done, b + 1)
                for q in range(NT + 5):
                    if q < NT:
                        act.wait_ge(icols_done, NT * b + (q + 1))
                        if q >= 2:
                            act.wait_ge(irows_done, NT * b + (q - 1))
                        act.activation(Z[:, q % 2, :], pZ[q % 2][:, :], ACT.Copy).then_inc(z_out, 1)
                    if 0 <= q - 2 < NT:
                        n = q - 2
                        act.wait_ge(diff_done, NT * b + (n + 1))
                        act.activation(D[:, n % 3, :], D[:, n % 3, :], ACT.Abs).then_inc(abs_done, 1)
                    if q < NT and more:
                        normalise(b + 1, 1 - s, q)
                    if 0 <= q - 5 < NT:
                        n = q - 5
                        act.wait_ge(rows_done, NT * b + (n + 1))
                        dst, src = tile_of_T(T, pT[n % 3], n)
                        act.activation(dst, src, ACT.Copy).then_inc(t_out, 1)

            act.wait_ge(sc_ready, 1)
            act.wait_ge(x_in[0], 128)
            for q in range(NT):
                normalise(0, 0, q)
            with act.Fori(0, B // 2 - 1) as bb:
                for s in range(2):
                    body(2 * bb + s, s, True)
            body(B - 2, 0, True)
            body(B - 1, 1, False)

        @block.tensor
        def _(pe):
            def body(b, s):
                pe.wait_ge(o_in, 128 * b + 128)
                for q in range(NT + 4):
                    if q < NT:
                        if q >= 2:
                            pe.wait_ge(z_out, NT * b + (q - 1))
                        inverse_columns(pe, pZ[q % 2], O, inv_cols, q).then_inc(icols_done, 1)
                    if 0 <= q - 1 < NT:
                        n = q - 1
                        pe.wait_ge(z_out, NT * b + (n + 1))
                        if n >= 2:
                            pe.wait_ge(diff_done, NT * b + (n - 1))
                        inverse_rows(pe, pR[n % 2], Z[:, n % 2, :], inv_rows).then_inc(irows_done, 1)
                    if 0 <= q - 4 < NT:
                        n = q - 4
                        pe.wait_ge(masked, NT * b + (n + 1))
                        if n >= 3:
                            pe.wait_ge(t_out, NT * b + (n - 2))
                        forward_rows(pe, pT[n % 3], X[:, s, :, :], rows_basis, n).then_inc(rows_done, 1)
                pe.wait_ge(t_out, NT * b + NT)
                pe.wait_ge(h_out, b + 1)
                forward_columns(pe, pH, T, cols_basis).then_inc(cols_done, 1)

            pe.nop().then_inc(cols_done, 1)
            pe.wait_ge(const_in, 64)
            with pe.Fori(0, B // 2) as bb:
                for s in range(2):
                    body(2 * bb + s, s)
            for q in range(mix.CHUNKS):
                mix.multiply(pe, q)

        @block.vector
        def _(dve):
            def scales(b, s):
                dve.tensor_copy(SC[:, s, :, :], of_sample(t.gn1, b)).then_inc(sc_ready, 1)

            def body(b, s, more):
                if more:
                    scales(b + 1, 1 - s)
                for q in range(NT + 3):
                    if q < NT:
                        dve.wait_ge(norm_done, NT * b + (q + 1))
                        dve.wait_ge(irows_done, NT * b + (q + 1))
                        if q >= 3:
                            dve.wait_ge(masked, NT * b + (q - 2))
                        dve.tensor_tensor(D[:, q % 3, :], X[:, s, CT * q:CT * q + CT, :].rearrange("p c w -> p (c w)"),
                                          pR[q % 2][:, :], ALU.subtract).then_inc(diff_done, 1)
                    if 0 <= q - 2 < NT:
                        n = q - 2
                        x = X[:, s, CT * n:CT * n + CT, :].rearrange("p c w -> p (c w)")
                        dve.wait_ge(abs_done, NT * b + (n + 1))
                        dve.scalar_tensor_tensor(x, D[:, n % 3, :], ERR_TH, x, ALU.is_gt, ALU.mult).then_inc(masked, 1)
                dve.wait_ge(cols_done, b + 2)
                dve.tensor_copy(of_sample(HM, b), pH[:, :]).then_inc(h_out, 1)

            dve.memset(O[:, :, :], 0.0).then_inc(cleared, 1)
            scales(0, 0)
            dve.memset(HD[:, :, :, :], 0.0).then_inc(cleared, 1)
            dve.wait_ge(cleared, 2)
            dve.nop().then_inc(h_out, 1)
            with dve.Fori(0, B // 2 - 1) as bb:
                for s in range(2):
                    body(2 * bb + s, s, True)
            body(B - 2, 0, True)
            body(B - 1, 1, False)
            dve.wait_ge(h_out, B + 1)
            for q in range(2):
                mix.spread(dve, HM, q)
            for q in range(mix.CHUNKS):
                mix.take(dve, q, True)
                if q + 2 < mix.CHUNKS:
                    mix.spread(dve, HM, q + 2)


def band_matrices(dve, bands, shifts, coefs, size, offset, step):
    ALU = mybir.AluOpType
    for dx in range(size):
        for dy in range(size):
            diagonal, k = shifts[:, offset + dy, :], coefs[:, dy * size + dx:dy * size + dx + 1]
            if dy == 0:
                step(dve.tensor_scalar(bands[:, dx, :], diagonal, k, None, ALU.mult))
            else:
                step(dve.scalar_tensor_tensor(bands[:, dx, :], diagonal, k, bands[:, dx, :], ALU.mult, ALU.add))


def layers2_and_3(nc, t):
    F32 = mybir.dt.float32
    F32R = mybir.dt.float32r
    ALU = mybir.AluOpType
    ACT = mybir.ActivationFunctionType
    S2, S3 = 3, 9
    PAD = S3 // 2
    NT = TILES_C
    HALF = NT // 2
    with ExitStack() as ctx:
        def sb(name, shape, dt=F32):
            return ctx.enter_context(nc.sbuf_tensor(name, shape, dt))

        def sem(name):
            return ctx.enter_context(nc.semaphore(name))

        def pb(name):
            return ctx.enter_context(nc.psum_tensor(name, [P, 512], F32))

        X = sb("s_x", [P, 2, C, W])
        O = sb("s_o", [P, P, C])
        Z = sb("s_z", [P, 2, CT * W])
        GN = {n: sb(f"s_g{n}", [P, 2, CT, W + 2 * PAD]) for n in (2, 3)}
        GH = {n: sb(f"s_gh{n}", [P, 2, CT, W + 2 * PAD], F32R) for n in (2, 3)}
        GL = {n: sb(f"s_gl{n}", [P, 2, CT, W + 2 * PAD], F32R) for n in (2, 3)}
        BF = {2: sb("s_b2", [P, S2, P]), 3: sb("s_b3", [P, S3, P])}
        BH = {2: sb("s_bh2", [P, S2, P], F32R), 3: sb("s_bh3", [P, S3, P], F32R)}
        BL = {2: sb("s_bl2", [P, S2, P], F32R), 3: sb("s_bl3", [P, S3, P], F32R)}
        shifts = sb("s_shifts", [P, S3, P])
        alpha = sb("s_alpha", [P, 9])
        beta = sb("s_beta", [P, 1])
        stencils = sb("s_stencils", [P, 8, S2 * S2])
        K2 = sb("s_k2", [P, S2 * S2])
        K3 = sb("s_k3", [P, S3 * S3])
        small = sb("s_small", [P, 2])
        inv_cols = sb("s_icols", [P, W])
        inv_rows = sb("s_irows", [P, P])
        ones = sb("s_ones", [P, P])
        ST = {n: GroupScaleBuffers(sb, f"s_gs{n}") for n in (2, 3)}
        SC = {n: sb(f"s_sc{n}", [P, 2, 2, G]) for n in (2, 3)}
        pZ = [pb(f"s_pz{i}") for i in range(2)]
        pA = [pb(f"s_pa{i}") for i in range(2)]
        pC = [pb(f"s_pc{i}") for i in range(3)]
        pS = ctx.enter_context(nc.psum_tensor("s_ps", [P, 4 * G], F32))

        const_in = sem("s_const_in")
        cleared = sem("s_cleared")
        built = sem("s_built")
        b_hi = sem("s_b_hi")
        b_lo = sem("s_b_lo")
        x_in = [[sem(f"s_x_in{s}{q}") for q in range(4)] for s in range(2)]
        o_in = sem("s_o_in")
        icols_done = sem("s_icols_done")
        z_out = sem("s_z_out")
        irows_done = sem("s_irows_done")
        x_sum = {n: sem(f"s_x_sum{n}") for n in (2, 3)}
        bn_done = {n: sem(f"s_bn_done{n}") for n in (2, 3)}
        chain = {n: sem(f"s_chain{n}") for n in (2, 3)}
        sums_done = {n: sem(f"s_sums_done{n}") for n in (2, 3)}
        std_done = {n: sem(f"s_std_done{n}") for n in (2, 3)}
        scale_done = {n: sem(f"s_scale_done{n}") for n in (2, 3)}
        g_done = {n: sem(f"s_g_done{n}") for n in (2, 3)}
        gl_done = {n: sem(f"s_gl_done{n}") for n in (2, 3)}
        conv_done = {n: sem(f"s_conv_done{n}") for n in (2, 3)}
        out_done = sem("s_out_done")
        stored = [[sem(f"s_stored{s}{q}") for q in range(4)] for s in range(2)]

        block = ctx.enter_context(nc.Block())
        x1 = t.x1.rearrange("b c h w -> b h c w")
        out = t.out.rearrange("b c h w -> b h c w")
        BUILT = 12 + S2 * S2 + S3 * S3

        def steps(eng, body):
            body(0, 0, True, False)
            with eng.Fori(0, B // 2 - 1) as bb:
                for u in range(2):
                    body(2 * bb + (1 + u), (1 + u) % 2, True, True)
            body(B - 1, (B - 1) % 2, True, True)
            body(B, B % 2, False, True)

        def tile_of(s, q):
            return X[:, s, CT * q:CT * q + CT, :].rearrange("p c w -> p (c w)")


        @block.sync
        def _(sp):
            n = 0
            for dst, src in ((inv_cols[:, :], t.inv_cols), (inv_rows[:, :], t.inv_rows),
                             (shifts[:, :, :], t.shifts), (alpha[:, :], t.alpha),
                             (beta[:, :], t.beta),
                             (stencils[:, :, :].rearrange("p a k -> p (a k)"), t.stencils),
                             (K3[:, :], t.k3)):
                sp.dma_start(dst, src).then_inc(const_in, 16)

            def load(b, s, q):
                for c in range(16 * q, 16 * q + 16, 8):
                    sp.dma_start(X[:, s, c:c + 8, :], x1[b, :, c:c + 8, :]).then_inc(x_in[s][q], 16)

            for q in range(4):
                load(0, 0, q)
            sp.wait_ge(cleared, 1)
            load_diagonal(sp, O, t.o_sum, 0, o_in)

            def body(b, s, here, before):
                if here and not (isinstance(b, int) and b == B - 1):
                    sp.wait_ge(icols_done, NT * b + NT)
                    load_diagonal(sp, O, t.o_sum, b + 1, o_in)
                for q in range(4):
                    if before:
                        sp.wait_ge(out_done, NT * (b - 1) + (4 * q + 4))
                        for c in range(16 * q, 16 * q + 16, 8):
                            sp.dma_start(out[b - 1, :, c:c + 8, :], X[:, 1 - s, c:c + 8, :]).then_inc(stored[1 - s][q], 16)
                    if here and not (isinstance(b, int) and b == B - 1):
                        if before:
                            sp.wait_ge(stored[1 - s][q], 32 * ((b + 1) // 2))
                        load(b + 1, 1 - s, q)

            steps(sp, body)
            for s in range(2):
                for q in range(4):
                    sp.wait_ge(stored[s][q], 32 * B // 2)

        def normalised_tiles(act, n, b, s, tiles):
            for q in tiles:
                at, g = NT * b + q, 2 * q
                if q >= 2:
                    act.wait_ge(gl_done[n], NT * b + (q - 1))
                for i in range(2):
                    last = act.activation(GN[n][:, q % 2, 2 * i:2 * i + 2, PAD:PAD + W],
                                          X[:, s, CT * q + 2 * i:CT * q + 2 * i + 2, :], ACT.Identity,
                                          scale=SC[n][:, s, 0, g + i:g + i + 1], bias=SC[n][:, s, 1, g + i:g + i + 1])
                last.then_inc(g_done[n], 1)
                act.wait_ge(g_done[n], 2 * NT * b + (2 * q + 1))
                if q >= 2:
                    act.wait_ge(conv_done[n], NT * b + (q - 1))
                act.activation(GH[n][:, q % 2, :, :], GN[n][:, q % 2, :, :], ACT.Copy).then_inc(g_done[n], 1)

        @block.scalar
        def _(act):
            def std(n, b):
                act.wait_ge(chain[n], CHAIN * b + CHAIN_VAR)
                act.activation(ST[n].std[:, :], ST[n].var[:, :], ACT.Sqrt).then_inc(std_done[n], 1)

            def body(b, s, here, before):
                if here:
                    for q in range(NT):
                        act.wait_ge(icols_done, NT * b + (q + 1))
                        if q >= 2:
                            act.wait_ge(irows_done, NT * b + (q - 1))
                        act.activation(Z[:, q % 2, :], pZ[q % 2][:, :], ACT.Copy).then_inc(z_out, 1)
                if before:
                    normalised_tiles(act, 3, b - 1, 1 - s, range(2, 5))
                if here:
                    std(2, b)
                if before:
                    normalised_tiles(act, 3, b - 1, 1 - s, range(5, HALF + 2))
                if here:
                    act.wait_ge(scale_done[2], b + 1)
                    normalised_tiles(act, 2, b, s, range(NT))
                if before:
                    normalised_tiles(act, 3, b - 1, 1 - s, range(HALF + 2, HALF + 4))
                if here:
                    std(3, b)
                if before:
                    normalised_tiles(act, 3, b - 1, 1 - s, range(HALF + 4, NT))
                if here:
                    act.wait_ge(scale_done[3], b + 1)
                    if before:
                        act.wait_ge(gl_done[3], NT * b)
                        act.wait_ge(conv_done[3], NT * b)
                    normalised_tiles(act, 3, b, s, range(2))

            act.wait_ge(built, BUILT)
            for n in (2, 3):
                act.activation(BH[n][:, :, :], BF[n][:, :, :], ACT.Copy).then_inc(b_hi, 1)
            steps(act, body)

        @block.gpsimd
        def _(pool):
            def low_parts(n, b, tiles):
                for q in tiles:
                    pool.wait_ge(g_done[n], 2 * NT * b + (2 * q + 2))
                    pool.tensor_tensor(GL[n][:, q % 2, :, :], GN[n][:, q % 2, :, :], GH[n][:, q % 2, :, :],
                                       ALU.subtract).then_inc(gl_done[n], 1)

            def body(b, s, here, before):
                if before:
                    low_parts(3, b - 1, range(2, HALF + 2))
                if here:
                    low_parts(2, b, range(NT))
                if before:
                    low_parts(3, b - 1, range(HALF + 2, NT))
                if here:
                    low_parts(3, b, range(2))

            for n in (2, 3):
                pool.wait_ge(b_hi, n - 1)
                pool.tensor_tensor(BL[n][:, :, :], BF[n][:, :, :], BH[n][:, :, :], ALU.subtract).then_inc(b_lo, 1)
            steps(pool, body)

        @block.tensor
        def _(pe):
            def sums(n, b):
                pe.wait_ge(chain[n], CHAIN * b + CHAIN_SUMS)
                pe.matmul(pS[:, :], ones[:, :], ST[n].sums[:, :, :].rearrange("p a g -> p (a g)"), start=True,
                          stop=True).then_inc(sums_done[n], 1)

            def convolve(n, b, tiles, banks, taken):
                size = {2: S2, 3: S3}[n]
                off = PAD - size // 2
                for q in tiles:
                    bank = banks[q % len(banks)]
                    pe.wait_ge(gl_done[n], NT * b + (q + 1))
                    if q >= len(banks):
                        pe.wait_ge(taken, NT * b + (q + 1 - len(banks)))
                    for dx in range(size):
                        for k, (w, g) in enumerate(((BH, GH), (BH, GL), (BL, GH))):
                            last = pe.matmul(bank[:, :], w[n][:, dx, :], g[n][:, q % 2, :, off + dx:off + dx + W],
                                             start=(dx == 0 and k == 0), stop=(dx == size - 1 and k == 2))
                    last.then_inc(conv_done[n], 1)

            def body(b, s, here, before):
                if here:
                    pe.wait_ge(o_in, 128 * b + 128)
                    for q in range(NT + 1):
                        if q < NT:
                            if q >= 2:
                                pe.wait_ge(z_out, NT * b + (q - 1))
                            inverse_columns(pe, pZ[q % 2], O, inv_cols, q).then_inc(icols_done, 1)
                        if q >= 1:
                            pe.wait_ge(z_out, NT * b + q)
                            if q >= 3:
                                pe.wait_ge(x_sum[2], NT * b + (q - 2))
                            inverse_rows(pe, pA[(q - 1) % 2], Z[:, (q - 1) % 2, :], inv_rows).then_inc(irows_done, 1)
                if before:
                    if not here:
                        pe.wait_ge(out_done, NT * (b - 1))
                    convolve(3, b - 1, range(1), pC, out_done)
                if here:
                    sums(2, b)
                if before:
                    convolve(3, b - 1, range(1, HALF), pC, out_done)
                if here:
                    convolve(2, b, range(NT), pA, x_sum[3])
                if before:
                    convolve(3, b - 1, range(HALF, HALF + 1), pC, out_done)
                if here:
                    sums(3, b)
                if before:
                    convolve(3, b - 1, range(HALF + 1, NT), pC, out_done)

            pe.wait_ge(const_in, 16 * 7)
            pe.wait_ge(b_hi, 2)
            pe.wait_ge(b_lo, 2)
            steps(pe, body)

        @block.vector
        def _(dve):
            def tile_sum(n, b, s, q, bank):
                x = tile_of(s, q)
                dve.tensor_tensor(x, x, bank[:, :], ALU.add).then_inc(x_sum[n], 1)

            def tile_statistics(n, b, s, q):
                dve.wait_ge(x_sum[n], NT * b + (q + 1))
                for g in (2 * q, 2 * q + 1):
                    last = dve.bn_stats(ST[n].bn[:, g, :], X[:, s, 2 * g:2 * g + 2, :].rearrange("p c w -> p (c w)"))
                if q == NT - 1:
                    last.then_inc(bn_done[n], 1)

            def scales(n, b, s):
                dve.wait_ge(bn_done[n], b + 1)
                step = Chain(dve, chain[n], CHAIN, b)
                group_scale_steps(dve, step, ST[n], sums_done[n], pS, std_done[n], ST[n].std, b)
                dve.tensor_copy(SC[n][:, s, 0, :], ST[n].r[:, :])
                dve.scalar_tensor_tensor(SC[n][:, s, 1, :], ST[n].ms[:, 0:G], -1.0, ST[n].r[:, :], ALU.mult, ALU.mult)\
                    .then_inc(scale_done[n], 1)
                dve.wait_ge(scale_done[n], b + 1)

            def results(b, s, tiles):
                for q in tiles:
                    x = tile_of(s, q)
                    dve.wait_ge(conv_done[3], NT * b + (q + 1))
                    dve.tensor_tensor(x, x, pC[q % 3][:, :], ALU.add).then_inc(out_done, 1)

            def body(b, s, here, before):
                if here:
                    for q in range(NT + 1):
                        if q < NT:
                            if q % 4 == 0:
                                dve.wait_ge(x_in[s][q // 4], 32 * (b // 2) + 32)
                            dve.wait_ge(irows_done, NT * b + (q + 1))
                            tile_sum(2, b, s, q, pA[q % 2])
                        if q >= 1:
                            tile_statistics(2, b, s, q - 1)
                    scales(2, b, s)
                if before:
                    results(b - 1, 1 - s, range(HALF))
                if here:
                    for q in range(NT + 1):
                        if q < NT:
                            dve.wait_ge(conv_done[2], NT * b + (q + 1))
                            tile_sum(3, b, s, q, pA[q % 2])
                        if q >= 1:
                            tile_statistics(3, b, s, q - 1)
                    scales(3, b, s)
                if before:
                    results(b - 1, 1 - s, range(HALF, NT))

            for n in (2, 3):
                for s in range(2):
                    dve.memset(GN[n][:, s, :, 0:PAD], 0.0)
                    dve.memset(GN[n][:, s, :, PAD + W:], 0.0)
            dve.memset(ones[:, :], 1.0 / 256)
            dve.memset(O[:, :, :], 0.0).then_inc(cleared, 1)
            dve.wait_ge(const_in, 16 * 7)
            done = [0]

            def step(ins):
                done[0] += 1
                ins.then_inc(built, 1)
                dve.wait_ge(built, done[0])

            step(dve.tensor_scalar(K2[:, :], stencils[:, 0, :], alpha[:, 0:1], None, ALU.mult))
            for a in range(1, 8):
                step(dve.scalar_tensor_tensor(K2[:, :], stencils[:, a, :], alpha[:, a:a + 1], K2[:, :],
                                              ALU.mult, ALU.add))
            step(dve.tensor_scalar(small[:, 0:1], alpha[:, 8:9], -1.0 / 9.0, None, ALU.mult))
            step(dve.tensor_tensor(small[:, 1:2], alpha[:, 8:9], beta[:, :], ALU.add))
            step(dve.tensor_scalar(K2[:, :], K2[:, :], small[:, 0:1], None, ALU.add))
            step(dve.tensor_tensor(K2[:, 4:5], K2[:, 4:5], small[:, 1:2], ALU.add))
            band_matrices(dve, BF[2], shifts, K2, S2, PAD - 1, step)
            band_matrices(dve, BF[3], shifts, K3, S3, 0, step)
            assert done[0] == BUILT
            steps(dve, body)


def conv_blocks(w):
    import numpy as np
    blocks = np.zeros((2, C, 6, 2, C), np.float32)
    for d in range(2):
        for row_in in range(2):
            for row_out in range(2):
                dy = 2 * d + row_in - row_out
                if 0 <= dy < 3:
                    for dx in range(3):
                        blocks[row_in, :, 3 * d + dx, row_out, :] = w[:, :, dy, dx].T
    return blocks.reshape(P, 6, P)


def layer0_arrays(x, w0, b0, w1, b1, w2, b2, w3, b3, wf, bf):
    import numpy as np
    f32 = np.float32

    def both(a):
        return np.concatenate([a, a]).astype(f32)

    w3blk = np.zeros((2, C, 9, 2, C), f32)
    for p in range(2):
        w3blk[p, :, :, p, :] = w3.reshape(C, 9, C).transpose(2, 1, 0)
    taps = both(w0.reshape(C, C, 9).transpose(1, 2, 0))
    grp = np.zeros((P, P), f32)
    band = np.zeros((C, 2, C), f32)
    for c in range(C):
        for p in range(P):
            grp[p, [c0 + q for q in (0, C) for c0 in range(C) if c0 // 2 == (p % C) // 2]] = 0.25
        for k in range(3):
            if 0 <= c + k - 1 < C:
                band[c + k - 1, :, c] = w2[0, 0, k]
    cnt = np.zeros((2, C, 3, 3), f32)
    for h in range(2):
        for dy in range(3):
            for dx in range(3):
                gone = (dy == 0 and h == 1) or (dy == 2 and h == 0)
                cnt[h, :, dy, dx] = (H // 2 - gone) * (W - (dx != 1))
    half = np.zeros((2, C, 2), f32)
    half[0, :, 0] = half[1, :, 1] = -1.0
    mask = np.ones((2, C, 16), f32)
    mask[0, :, 0] = mask[1, :, 15] = 0.0
    b12 = np.zeros((2, C, 3), f32)
    b12[:, :, 0], b12[:, :, 1], b12[:, :, 2] = b1, bf, b2[0]
    x_rows = np.zeros((B, C, H + 2, W), f32)
    x_rows[:, :, 1:H + 1] = x
    return {
        "x": x, "x_rows": x_rows, "w0taps": taps, "grp": grp, "band": band.reshape(C, P),
        "cnt": cnt.reshape(P, 9), "half": half.reshape(P, 2), "b0": both(b0).reshape(P, 1),
        "b12": b12.reshape(P, 3), "b3": both(b3.reshape(C, 9)), "w3blk": w3blk.reshape(P, 9, P),
        "w0blk": conv_blocks(w0), "wfblk": conv_blocks(wf), "w1": both(w1.reshape(C, 9)),
        "mask": mask.reshape(P, 16),
    }


def spectral_bases():
    import numpy as np
    tau = 2 * np.pi / H
    n, k = np.meshgrid(np.arange(H), np.arange(F), indexing="ij")
    fa, fb = tau * (n * k % H), tau * ((n + 1) * k % H)
    ia, ib = fa.T, (tau * (n * (k + 1) % H)).T
    f32 = np.float32
    return {
        "fwd_rows": np.concatenate([np.cos(fa), np.sin(fa), np.cos(fb), np.sin(fb)], 1).astype(f32),
        "fwd_cols": np.stack([np.cos(fa), -np.sin(fa), -np.sin(fb), -np.cos(fb)], 1).astype(f32),
        "inv_cols": np.concatenate([np.cos(ia), np.sin(ia), np.cos(ib), np.sin(ib)], 0).astype(f32),
        "inv_rows": (np.concatenate([np.cos(ia), -np.sin(ia), -np.sin(ib), -np.cos(ib)], 0) / (H * W)).astype(f32),
    }


def row_shifts():
    import numpy as np
    return np.stack([np.eye(P, k=4 - dy) for dy in range(9)], 1).astype(np.float32)


def stencil_arrays(alpha, beta, kernels, k3):
    import numpy as np
    flat = {"alpha": alpha, "beta": beta, "stencils": kernels, "k3": k3}
    return {name: np.ascontiguousarray(np.broadcast_to(a.reshape(1, -1), (P, a.size))) for name, a in flat.items()}


_INS = ["x", "x_rows", "w0taps", "grp", "band", "cnt", "half", "b0", "b12", "b3", "w3blk", "w0blk", "wfblk", "w1",
        "mask", "weights1", "refine1", "fwd_rows", "fwd_cols", "inv_cols", "inv_rows", "shifts", "alpha", "beta",
        "stencils", "k3"]


class Arrays:

    def __init__(self, args):
        (self.x, self.x_rows, self.w0taps, self.grp, self.band, self.cnt, self.half, self.b0, self.b12, self.b3,
         self.w3blk, self.w0blk, self.wfblk, self.w1, self.mask, self.weights1, self.refine1, self.fwd_rows,
         self.fwd_cols, self.inv_cols, self.inv_rows, self.shifts, self.alpha, self.beta, self.stencils, self.k3,
         self.out) = args


def conv_stack_kernel(nc, *args):
    F32 = mybir.dt.float32
    t = Arrays(args)
    t.x1 = nc.dram_tensor("x1", (B, C, H, W), F32, kind="Internal").ap()
    t.o_ht = nc.dram_tensor("o_ht", (2 * B, MODES, C), F32, kind="Internal").ap()
    t.o_sum = nc.dram_tensor("o_sum", (2 * B, MODES, C), F32, kind="Internal").ap()
    with ExitStack() as ctx:
        t.gn0 = ctx.enter_context(nc.sbuf_tensor("gn0", [P, 4, B], F32))
        t.b3p = ctx.enter_context(nc.sbuf_tensor("b3p", [P, B, 9], F32))
        t.w3f = ctx.enter_context(nc.sbuf_tensor("w3f", [P, 9, P], F32))
        layer0_statistics(nc, t)
        layer0_convolutions(nc, t)
    with ExitStack() as ctx:
        t.gn1 = ctx.enter_context(nc.sbuf_tensor("gn1", [P, B, 2, G], F32))
        layer1_analyse(nc, t)
        layer1_refine(nc, t)
    layers2_and_3(nc, t)


def kernel(**inputs):
    import numpy as np
    import concourse.bacc as bacc
    from concourse.bass_utils import run_bass_kernel_spmd

    given = {name: np.asarray(a) for name, a in inputs.items()}
    laid_out = {
        **layer0_arrays(given["x"], *[given[f"L0_conv_{k}"]
                                      for k in ("w0", "b0", "w1", "b1", "w2", "b2", "w3", "b3", "wf", "bf")]),
        "weights1": given["L1_conv_weights1"], "refine1": given["L1_conv_refine_weights1"],
        **spectral_bases(), "shifts": row_shifts(),
        **stencil_arrays(given["L2_conv_alpha"], given["L2_conv_beta"], given["L2_conv_kernels"],
                         given["L3_conv_K"]),
    }
    nc = bacc.Bacc("TRN2", target_bir_lowering=False, num_devices=1)
    arrays, args = {}, []
    for name in _INS:
        a = np.ascontiguousarray(laid_out[name])
        arrays[f"in_{name}_dram"] = a
        args.append(nc.dram_tensor(f"in_{name}_dram", a.shape, mybir.dt.from_np(a.dtype), kind="ExternalInput").ap())
    args.append(nc.dram_tensor("out_dram", (B, C, H, W), mybir.dt.float32, kind="ExternalOutput").ap())
    conv_stack_kernel(nc, *args)
    r = run_bass_kernel_spmd(nc, [arrays], core_ids=[0])
    return r.results[0]["out_dram"]
```

```python
from contextlib import ExitStack

import concourse.bass as bass
from concourse import mybir

B, C, H, W = 8, 64, 128, 128
P = 128
G = 32
F = 32
EPS = 1e-5


def layer0_statistics(nc, t):
    F32 = mybir.dt.float32
    ALU = mybir.AluOpType
    ACT = mybir.ActivationFunctionType
    AX = mybir.AxisListType.X
    with ExitStack() as ctx:
        def sb(name, shape, dt=F32):
            return ctx.enter_context(nc.sbuf_tensor(name, shape, dt))

        def sem(name):
            return ctx.enter_context(nc.semaphore(name))

        ROWS = H // 2
        CH = 16
        NCH = ROWS // CH
        NBUF = 4
        XC = sb("st_x", [P, NBUF, CH * W])
        BS = sb("st_bn", [P, B, NCH * 4 * 6])
        EC = sb("st_edgecols", [P, B, NCH, 2])
        ER = sb("st_edgerow", [P, B, W])
        MV = sb("st_mv", [P, B, 2])
        EX = sb("st_ex", [P, 2, B])
        M = sb("st_m", [P, 2, B])
        VAR = sb("st_var", [P, B])
        RX = sb("st_rx", [P, 3, B])
        D = sb("st_d", [P, 3, B])
        ECS = sb("st_ecs", [P, B, 2])
        V = sb("st_v", [P, 9, B])
        V2 = sb("st_v2", [P, 9, B])
        taps = sb("st_w0taps", [P, 9, C])
        grp = sb("st_grp", [P, P])
        band = sb("st_band", [C, P])
        cnt = sb("st_cnt", [P, 9])
        half = sb("st_half", [P, 2])
        b0 = sb("st_b0", [C, 1])
        b12 = sb("st_b12", [P, 3])
        b3 = sb("st_b3", [P, 9])
        XM = sb("st_xm", [C, B])
        X2 = sb("st_x2", [P, B])
        STD = sb("st_std", [P, B])
        pg = ctx.enter_context(nc.psum_tensor("st_pg", [P, 2 * B], F32))
        pm = ctx.enter_context(nc.psum_tensor("st_pm", [C, B], F32))
        px = ctx.enter_context(nc.psum_tensor("st_px", [P, B], F32))
        p3 = ctx.enter_context(nc.psum_tensor("st_p3", [P, 9 * B], F32))

        chunk_in = [sem(f"st_chunk_in{n}") for n in range(NBUF)]
        const_in = sem("st_const_in")
        chunk_used = sem("st_chunk_used")
        chain = sem("st_chain")
        group_done = sem("st_group_done")
        std_done = sem("st_std_done")
        mean_done = sem("st_mean_done")
        xm_done = sem("st_xm_done")
        x2_done = sem("st_x2_done")
        x2_out = sem("st_x2_out")
        b3_done = sem("st_b3_done")

        C_EX = B + 3
        C_VAR = C_EX + 4
        C_V = C_VAR + 14 + 4 + 18

        block = ctx.enter_context(nc.Block())
        halves = t.x.rearrange("b c (h r) w -> b h c (r w)", h=2)

        @block.sync
        def _(sp):
            for q in range(NCH):
                for h in range(2):
                    sp.dma_start(XC[C * h:C * h + C, q, :], halves[0, h, :, q * CH * W:(q + 1) * CH * W])\
                        .then_inc(chunk_in[q], 16)
            with sp.Fori(1, B) as b:
                for q in range(NCH):
                    sp.wait_ge(chunk_used, b * NCH + (q + 1 - NCH))
                    for h in range(2):
                        sp.dma_start(XC[C * h:C * h + C, q, :], halves[b, h, :, q * CH * W:(q + 1) * CH * W])\
                            .then_inc(chunk_in[q], 16)

        @block.scalar
        def _(act):
            n = 0
            for dst, src in ((taps[:, :, :], t.w0taps), (grp[:, :], t.grp), (band[:, :], t.band),
                             (cnt[:, :], t.cnt), (half[:, :], t.half), (b0[:, :], t.b0[0:C, :]),
                             (b12[:, :], t.b12), (b3[:, :], t.b3), (t.w3f[:, :, :], t.w3blk),
                             (ER[0:C, :, :], t.x[:, :, 0, :].rearrange("b c w -> c b w")),
                             (ER[C:P, :, :], t.x[:, :, H - 1, :].rearrange("b c w -> c b w"))):
                act.dma_start(dst, src).then_inc(const_in, 16)
                n += 16
            act.wait_ge(chain, C_VAR)
            act.activation(STD[:, :], VAR[:, :], ACT.Sqrt).then_inc(std_done, 1)
            act.wait_ge(mean_done, 1)
            act.activation(XM[:, :], pm[:, :], ACT.Identity, scale=1.0 / (H * W), bias=b0[:, :]).then_inc(xm_done, 1)
            act.wait_ge(x2_done, 1)
            act.activation(X2[:, :], px[:, :], ACT.Identity, bias=b12[:, 2:3]).then_inc(x2_out, 1)
            act.wait_ge(x2_out, 1)
            act.activation(X2[:, :], X2[:, :], ACT.Identity, bias=b12[:, 0:1]).then_inc(x2_out, 1)

        N_CONST = 11 * 16

        @block.tensor
        def _(pe):
            pe.wait_ge(chain, C_EX)
            pe.matmul(pg[:, :], grp[:, :], EX[:, :, :].rearrange("p a b -> p (a b)"), start=True, stop=True)\
                .then_inc(group_done, 1)
            pe.wait_ge(chain, C_V)
            for k in range(9):
                last = pe.matmul(pm[:, :], taps[:, k, :], V[:, k, :], start=(k == 0), stop=(k == 8))
            last.then_inc(mean_done, 1)
            pe.wait_ge(xm_done, 1)
            pe.matmul(px[:, :], band[:, :], XM[:, :], start=True, stop=True).then_inc(x2_done, 1)
            pe.wait_ge(x2_out, 2)
            for k in range(9):
                last = pe.matmul(p3[:, k * B:(k + 1) * B], t.w3f[:, k, :], X2[:, :], start=True, stop=True)
            last.then_inc(b3_done, 1)

        @block.vector
        def _(dve):
            done = [0]

            def step(ins):
                done[0] += 1
                ins.then_inc(chain, 1)
                dve.wait_ge(chain, done[0])

            with dve.Fori(0, B) as b:
                for q in range(NCH):
                    dve.wait_ge(chunk_in[q], 32 * b + 32)
                    for j in range(4):
                        at = (4 * q + j) * 6
                        dve.bn_stats(BS[:, bass.ds(b, 1), at:at + 6], XC[:, q, 512 * j:512 * j + 512])
                    dve.tensor_reduce(EC[:, bass.ds(b, 1), q, :],
                                      XC[:, q, :].rearrange("p (r w) -> p w r", w=W)[:, 0:W:W - 1, :],
                                      AX, ALU.add).then_inc(chunk_used, 1)
            dve.wait_ge(chunk_used, NCH * B)
            for b in range(B):
                step(dve.bn_aggr(MV[:, b, :], BS[:, b, :]))
            dve.wait_ge(const_in, N_CONST)
            mean, var = MV[:, :, 0], MV[:, :, 1]
            step(dve.tensor_copy(EX[:, 0, :], mean))
            step(dve.tensor_tensor(EX[:, 1, :], mean, mean, ALU.mult))
            step(dve.tensor_tensor(EX[:, 1, :], EX[:, 1, :], var, ALU.add))
            assert done[0] == C_EX
            dve.wait_ge(group_done, 1)
            step(dve.tensor_copy(M[:, :, :].rearrange("p a b -> p (a b)"), pg[:, :]))
            step(dve.tensor_tensor(VAR[:, :], M[:, 0, :], M[:, 0, :], ALU.mult))
            step(dve.tensor_tensor(VAR[:, :], M[:, 1, :], VAR[:, :], ALU.subtract))
            step(dve.tensor_scalar(VAR[:, :], VAR[:, :], EPS, None, ALU.add))
            assert done[0] == C_VAR
            dve.wait_ge(std_done, 1)
            scale, shift = t.gn0[:, 0, :], t.gn0[:, 1, :]
            step(dve.reciprocal(scale, STD[:, :]))
            step(dve.tensor_tensor(STD[:, :], scale, scale, ALU.mult))
            step(dve.tensor_tensor(STD[:, :], STD[:, :], VAR[:, :], ALU.mult))
            step(dve.tensor_scalar(STD[:, :], STD[:, :], -0.5, 1.5, ALU.mult, ALU.add))
            step(dve.tensor_tensor(scale, scale, STD[:, :], ALU.mult))
            step(dve.scalar_tensor_tensor(shift, M[:, 0, :], -1.0, scale, ALU.mult, ALU.mult))
            step(dve.tensor_scalar(t.gn0[:, 2, :], scale, 1.0, None, ALU.add))
            step(dve.tensor_scalar(t.gn0[:, 3, :], shift, b12[:, 1:2], None, ALU.add))
            step(dve.tensor_reduce(ECS[:, :, :], EC[:, :, :, :].rearrange("p b q e -> p b e q"), AX, ALU.add))
            step(dve.tensor_scalar(D[:, 1, :], mean, float(ROWS * W), None, ALU.mult))
            step(dve.tensor_tensor(D[:, 0, :], D[:, 1, :], ECS[:, :, 1], ALU.subtract))
            step(dve.tensor_tensor(D[:, 2, :], D[:, 1, :], ECS[:, :, 0], ALU.subtract))
            step(dve.tensor_reduce(RX[:, 1, :], ER[:, :, :], AX, ALU.add))
            step(dve.tensor_tensor(RX[:, 0, :], RX[:, 1, :], ER[:, :, W - 1], ALU.subtract))
            step(dve.tensor_tensor(RX[:, 2, :], RX[:, 1, :], ER[:, :, 0], ALU.subtract))
            step(dve.tensor_copy(V2[:, 3:6, :], D[:, :, :]))
            step(dve.scalar_tensor_tensor(V2[:, 0:3, :], RX[:, :, :], half[:, 1:2], D[:, :, :], ALU.mult, ALU.add))
            step(dve.scalar_tensor_tensor(V2[:, 6:9, :], RX[:, :, :], half[:, 0:1], D[:, :, :], ALU.mult, ALU.add))
            for k in range(9):
                step(dve.tensor_tensor(V[:, k, :], V2[:, k, :], scale, ALU.mult))
                step(dve.scalar_tensor_tensor(V[:, k, :], shift, cnt[:, k:k + 1], V[:, k, :], ALU.mult, ALU.add))
            assert done[0] == C_V
            dve.wait_ge(b3_done, 1)
            for k in range(9):
                dve.tensor_scalar(t.b3p[:, :, k], p3[:, k * B:(k + 1) * B], b3[:, k:k + 1], None, ALU.add)\
                    .then_inc(chain, 1)
            dve.wait_ge(chain, done[0] + 9)


class Tile:

    def __init__(self, pair, offset, per_sample):
        self.n = 2 * pair + offset if offset else 2 * pair
        self.half = pair + offset // 2 if offset // 2 else pair
        self.s = offset % 2
        self.i = self.n % per_sample
        self.b = self.n // per_sample


def pipeline(eng, tiles, per_sample, offsets, body):
    lo, hi = -min(offsets.values()) + 2, tiles - max(offsets.values())
    hi -= (hi - lo) % 2

    def straight(g):
        body({k: Tile((g + o) // 2, (g + o) % 2, per_sample) if 0 <= g + o < tiles else None
              for k, o in offsets.items()})

    for g in range(-max(offsets.values()), lo):
        straight(g)
    with eng.Fori(0, (hi - lo) // 2) as n:
        for u in range(2):
            body({k: Tile(n, lo + u + o, per_sample) for k, o in offsets.items()})
    for g in range(hi, tiles - min(offsets.values())):
        straight(g)


def wait(eng, sem, value):
    if not isinstance(value, int) or value > 0:
        eng.wait_ge(sem, value)


def layer0_convolutions(nc, t):
    F32 = mybir.dt.float32
    F32R = mybir.dt.float32r
    ALU = mybir.AluOpType
    ACT = mybir.ActivationFunctionType
    SL = 4
    PER = H // 2 // SL
    TILES = B * PER
    WP = W + 2
    TAPS = 9
    RING = 8
    LO = slice(0, C)
    UP = slice(C, P)
    with ExitStack() as ctx:
        def sb(name, shape, dt=F32):
            return ctx.enter_context(nc.sbuf_tensor(name, shape, dt))

        def sem(name):
            return ctx.enter_context(nc.semaphore(name))

        XT = sb("c_x", [P, 2, SL + 1, WP])
        XH = sb("c_xh", [P, 2, SL + 1, WP], F32R)
        XL = sb("c_xl", [P, 2, SL + 1, WP], F32R)
        X0E = sb("c_x0e", [P, RING * SL, WP])
        X0O = sb("c_x0o", [P, H // 2 + 1, WP])
        Y = sb("c_y", [P, 2, SL * W])
        YH = sb("c_yh", [P, 2, SL * W], F32R)
        YL = sb("c_yl", [P, 2, SL * W], F32R)
        PR = sb("c_pr", [P, 8, SL * W])
        PL = sb("c_pl", [P, 2, SL * W])
        AC = sb("c_ac", [P, 2, SL * W])
        TE = sb("c_te", [P, 2, SL * W])
        TO = sb("c_to", [P, H // 2 + 1, WP])
        TH = sb("c_th", [P, 2, SL + 1, WP], F32R)
        TL = sb("c_tl", [P, 2, SL + 1, WP], F32R)
        XR = sb("c_xr", [P, 2, SL * W])
        OUT = sb("c_out", [P, 2, SL * W])
        mask = sb("c_mask", [P, PER])
        b0 = sb("c_b0", [P, 1])
        w1 = sb("c_w1", [P, TAPS])
        WS = sb("c_ws", [P, 6, P])
        W0H, W0L = sb("c_w0h", [P, 6, P], F32R), sb("c_w0l", [P, 6, P], F32R)
        WFH, WFL = sb("c_wfh", [P, 6, P], F32R), sb("c_wfl", [P, 6, P], F32R)
        W3H, W3L = sb("c_w3h", [P, TAPS, P], F32R), sb("c_w3l", [P, TAPS, P], F32R)
        p0 = [ctx.enter_context(nc.psum_tensor(f"c_p0{s}", [P, SL * W], F32)) for s in range(2)]
        p3 = [ctx.enter_context(nc.psum_tensor(f"c_p3{s}", [P, SL * W], F32)) for s in range(3)]
        pf = [ctx.enter_context(nc.psum_tensor(f"c_pf{s}", [P, SL * W], F32)) for s in range(2)]

        const_in = sem("c_const_in")
        ws_in = sem("c_ws_in")
        cleared = sem("c_cleared")
        w_hi = sem("c_w_hi")
        w_lo = sem("c_w_lo")
        xt_in = [sem(f"c_xt_in{s}") for s in range(2)]
        xr_in = [sem(f"c_xr_in{s}") for s in range(2)]
        xn_done = sem("c_xn_done")
        xh_done = sem("c_xh_done")
        xl_done = sem("c_xl_done")
        w0_done = sem("c_w0_done")
        x0_out = sem("c_x0_out")
        x0_odd = [sem(f"c_x0_odd{s}") for s in range(2)]
        dw_done = sem("c_dw_done")
        yh_done = sem("c_yh_done")
        y0_done = sem("c_y0_done")
        yl_done = [sem(f"c_yl_done{s}") for s in range(2)]
        w3_done = sem("c_w3_done")
        mult_done = sem("c_mult_done")
        add_done = sem("c_add_done")
        lrelu_done = sem("c_lrelu_done")
        t_odd = [sem(f"c_t_odd{s}") for s in range(2)]
        th_done = sem("c_th_done")
        tl_done = sem("c_tl_done")
        wf_done = sem("c_wf_done")
        res_done = sem("c_res_done")
        fin_done = sem("c_fin_done")
        stored = [sem(f"c_stored{s}") for s in range(2)]

        block = ctx.enter_context(nc.Block())
        odd_rows = t.x_rows.rearrange("b c (r e) w -> e b c r w", e=2)
        even_rows = t.x.rearrange("b c (r e) w -> e b c r w", e=2)
        out_rows = t.x1.rearrange("b c (r e) w -> e b c r w", e=2)

        def at(tile, pairs=SL, off=0):
            return bass.ds(tile.i * SL + off, pairs)

        def in_ring(tile):
            return bass.ds(tile.n % RING * SL, SL)

        def rows(ap):
            return ap.rearrange("p (r w) -> p r w", w=W)

        @block.sync
        def _(sp):
            for dst, src in ((mask[:, :], t.mask), (b0[:, :], t.b0), (w1[:, :], t.w1)):
                sp.dma_start(dst, src).then_inc(const_in, 16)
            sp.dma_start(WS[:, :, :], t.w0blk).then_inc(ws_in, 16)
            wait(sp, w_lo, 1)
            sp.dma_start(WS[:, :, :], t.wfblk).then_inc(ws_in, 16)
            sp.wait_ge(cleared, 1)

            def body(at_stage):
                if x0 := at_stage["x0"]:
                    sp.wait_ge(x0_out, x0.n + 1)
                    wait(sp, x0_odd[x0.s], 32 * x0.half)
                    sp.dma_start(X0O[UP, at(x0), :], X0E[LO, in_ring(x0), :]).then_inc(x0_odd[x0.s], 16)
                    sp.dma_start(X0O[LO, at(x0, off=1), :], X0E[UP, in_ring(x0), :]).then_inc(x0_odd[x0.s], 16)
                if l := at_stage["lrelu"]:
                    sp.wait_ge(lrelu_done, l.n + 1)
                    sp.dma_start(TO[UP, at(l), 1:W + 1], rows(TE[LO, l.s, :])).then_inc(t_odd[l.s], 16)
                    sp.dma_start(TO[LO, at(l, off=1), 1:W + 1], rows(TE[UP, l.s, :])).then_inc(t_odd[l.s], 16)
                if f := at_stage["fin"]:
                    sp.wait_ge(fin_done, f.n + 1)
                    for e, half in enumerate((LO, UP)):
                        sp.dma_start(out_rows[e, f.b, :, bass.ds(f.i * SL, SL), :], rows(OUT[half, f.s, :]))\
                            .then_inc(stored[f.s], 16)
                if r := at_stage["xr"]:
                    wait(sp, fin_done, r.n - 1)
                    for e, half in enumerate((LO, UP)):
                        sp.dma_start(rows(XR[half, r.s, :]), even_rows[e, r.b, :, bass.ds(r.i * SL, SL), :])\
                            .then_inc(xr_in[r.s], 16)
                if x := at_stage["xt"]:
                    wait(sp, xl_done, x.n - 1)
                    for e, half in enumerate((LO, UP)):
                        sp.dma_start(XT[half, x.s, :, 1:W + 1],
                                     odd_rows[e, x.b, :, bass.ds(x.i * SL, SL + 1), :]).then_inc(xt_in[x.s], 16)

            pipeline(sp, TILES, PER, {"xt": 7, "x0": 4, "lrelu": -1, "xr": -3, "fin": -5}, body)
            for s in range(2):
                sp.wait_ge(stored[s], 32 * TILES // 2)

        @block.gpsimd
        def _(pool):
            def add(m, k):
                pool.wait_ge(mult_done, 9 * m.n + (2 * k + 2))
                if k > 1:
                    pool.wait_ge(add_done, 5 * m.n + (k - 1))
                pool.tensor_tensor(PR[:, 2 * k:2 * k + 2, :], PR[:, 2 * k - 2:2 * k, :], PR[:, 2 * k:2 * k + 2, :],
                                   ALU.add).then_inc(add_done, 1)

            def finish(m):
                pool.wait_ge(add_done, 5 * m.n + 3)
                wait(pool, lrelu_done, m.n - 1)
                pool.tensor_tensor(AC[:, m.s, :], PR[:, 6, :], PR[:, 7, :], ALU.add).then_inc(add_done, 1)

            def last_tap(m):
                pool.wait_ge(mult_done, 9 * m.n + 9)
                pool.wait_ge(add_done, 5 * m.n + 4)
                pool.tensor_tensor(AC[:, m.s, :], AC[:, m.s, :], PL[:, m.s, :], ALU.add).then_inc(add_done, 1)

            def body(at_stage):
                m, before = at_stage["main"], at_stage["sum"]
                if before:
                    finish(before)
                    last_tap(before)
                if ts := at_stage["tsplit"]:
                    pool.wait_ge(th_done, ts.n + 1)
                    wait(pool, wf_done, ts.n - 1)
                    pool.tensor_tensor(TL[:, ts.s, :, :], TO[:, at(ts, SL + 1), :], TH[:, ts.s, :, :],
                                       ALU.subtract).then_inc(tl_done, 1)
                if x := at_stage["norm"]:
                    pool.wait_ge(xh_done, x.n + 1)
                    pool.tensor_tensor(XL[:, x.s, :, :], XT[:, x.s, :, :], XH[:, x.s, :, :],
                                       ALU.subtract).then_inc(xl_done, 1)
                if m:
                    add(m, 1)
                if (y := at_stage["ysplit"]) and y.s == 0:
                    pool.wait_ge(yh_done, y.n + 1)
                    pool.tensor_tensor(YL[:, y.s, :], Y[:, y.s, :], YH[:, y.s, :], ALU.subtract)\
                        .then_inc(yl_done[0], 1)
                if m:
                    add(m, 2)
                    add(m, 3)

            pipeline(pool, TILES, PER, {"norm": 6, "ysplit": 1, "main": 0, "sum": -1, "tsplit": -3}, body)

        @block.scalar
        def _(act):
            act.wait_ge(ws_in, 16)
            act.activation(W0H[:, :, :], WS[:, :, :], ACT.Copy).then_inc(w_hi, 1)
            act.activation(W3H[:, :, :], t.w3f[:, :, :], ACT.Copy).then_inc(w_hi, 1)
            act.wait_ge(ws_in, 32)
            act.activation(WFH[:, :, :], WS[:, :, :], ACT.Copy).then_inc(w_hi, 1)
            act.wait_ge(const_in, 48)
            act.wait_ge(cleared, 1)

            def body(at_stage):
                if d := at_stage["dw"]:
                    act.wait_ge(x0_odd[d.s], 32 * d.half + 32)
                    wait(act, yl_done[d.s], d.half)
                    act.activation(rows(Y[:, d.s, :]), X0O[:, at(d), 0:W], ACT.Copy, scale=w1[:, 0:1])\
                        .then_inc(y0_done, 1)
                if ts := at_stage["tsplit"]:
                    nxt = ts.half + (ts.s + 1) // 2
                    act.wait_ge(t_odd[ts.s], 32 * ts.half + 32)
                    if not (isinstance(ts.n, int) and ts.n == TILES - 1):
                        act.wait_ge(t_odd[1 - ts.s], 32 * nxt + 32)
                    wait(act, wf_done, ts.n - 1)
                    act.activation(TH[:, ts.s, :, :], TO[:, at(ts, SL + 1), :], ACT.Copy).then_inc(th_done, 1)
                if y := at_stage["ysplit"]:
                    act.wait_ge(dw_done, 8 * y.n + 8)
                    wait(act, w3_done, 9 * y.n - 9)
                    act.activation(YH[:, y.s, :], Y[:, y.s, :], ACT.Copy).then_inc(yh_done, 1)
                if x0 := at_stage["x0"]:
                    act.wait_ge(w0_done, x0.n + 1)
                    act.activation(X0E[:, in_ring(x0), 1:W + 1], rows(p0[x0.s][:, :]), ACT.Identity,
                                   bias=b0[:, :]).then_inc(x0_out, 1)
                if x := at_stage["norm"]:
                    act.wait_ge(xt_in[x.s], 32 * x.half + 32)
                    act.activation(XT[:, x.s, :, 1:W + 1], XT[:, x.s, :, 1:W + 1], ACT.Identity,
                                   scale=t.gn0[:, 0, bass.ds(x.b, 1)], bias=t.gn0[:, 1, bass.ds(x.b, 1)])\
                        .then_inc(xn_done, 1)
                    act.wait_ge(xn_done, 3 * x.n + 1)
                    act.activation(XT[LO, x.s, 0, :], XT[LO, x.s, 0, :], ACT.Copy,
                                   scale=mask[LO, bass.ds(x.i, 1)]).then_inc(xn_done, 1)
                    act.activation(XT[UP, x.s, SL, :], XT[UP, x.s, SL, :], ACT.Copy,
                                   scale=mask[UP, bass.ds(x.i, 1)]).then_inc(xn_done, 1)
                    act.wait_ge(xn_done, 3 * x.n + 3)
                    wait(act, w0_done, x.n - 1)
                    act.activation(XH[:, x.s, :, :], XT[:, x.s, :, :], ACT.Copy).then_inc(xh_done, 1)
                if f := at_stage["res"]:
                    act.wait_ge(xr_in[f.s], 32 * f.half + 32)
                    act.activation(XR[:, f.s, :], XR[:, f.s, :], ACT.Identity,
                                   scale=t.gn0[:, 2, bass.ds(f.b, 1)], bias=t.gn0[:, 3, bass.ds(f.b, 1)])\
                        .then_inc(res_done, 1)

            pipeline(act, TILES, PER, {"norm": 6, "x0": 4, "dw": 2, "ysplit": 1, "tsplit": -3, "res": -4}, body)

        @block.tensor
        def _(pe):
            pe.wait_ge(w_hi, 3)
            pe.wait_ge(w_lo, 3)

            def conv(psum, wh, wl, xh, xl, s):
                todo = []
                for n in range(6):
                    d, dx = divmod(n, 3)
                    for w, x in ((wh, xh), (wh, xl), (wl, xh)):
                        todo.append((psum[s], w[:, n, :], x[:, s, d:d + SL, dx:dx + W]))
                return todo

            def body(at_stage):
                jobs = []
                if a := at_stage["w0"]:
                    pe.wait_ge(xh_done, a.n + 1)
                    pe.wait_ge(xl_done, a.n + 1)
                    wait(pe, x0_out, a.n - 1)
                    jobs.append((conv(p0, W0H, W0L, XH, XL, a.s), w0_done))
                if f := at_stage["wf"]:
                    pe.wait_ge(th_done, f.n + 1)
                    pe.wait_ge(tl_done, f.n + 1)
                    wait(pe, fin_done, f.n - 1)
                    jobs.append((conv(pf, WFH, WFL, TH, TL, f.s), wf_done))
                others = [(o, w, x, n == 0, n == len(job) - 1, s) for job, s in jobs for n, (o, w, x) in enumerate(job)]
                m = at_stage["main"]

                def some(n):
                    for o, w, x, first, final, s in others[:n]:
                        ins = pe.matmul(o[:, :], w, x, start=first, stop=final)
                        if final:
                            ins.then_inc(s, 1)
                    del others[:n]

                if m:
                    pe.wait_ge(yh_done, m.n + 1)
                    pe.wait_ge(yl_done[m.s], m.half + 1)
                    for k in range(TAPS):
                        wait(pe, mult_done, 9 * m.n + (k - 2))
                        for n, (w, y) in enumerate(((W3H, YH), (W3H, YL), (W3L, YH))):
                            last = pe.matmul(p3[k % 3][:, :], w[:, k, :], y[:, m.s, :], start=(n == 0), stop=(n == 2))
                        last.then_inc(w3_done, 1)
                        some(4)
                some(len(others))

            pipeline(pe, TILES, PER, {"w0": 5, "main": 0, "wf": -4}, body)

        @block.vector
        def _(dve):
            for s in range(2):
                dve.memset(XT[:, s, :, 0:WP:W + 1], 0.0)
            dve.memset(X0E[:, :, 0:WP:W + 1], 0.0)
            for buf in (X0O, TO):
                dve.memset(buf[:, :, 0:WP:W + 1], 0.0)
                dve.memset(buf[LO, 0, 1:W + 1], 0.0)
                last = dve.memset(buf[UP, H // 2, 1:W + 1], 0.0)
            last.then_inc(cleared, 1)
            dve.wait_ge(w_hi, 1)
            dve.tensor_tensor(W0L[:, :, :], WS[:, :, :], W0H[:, :, :], ALU.subtract).then_inc(w_lo, 1)
            dve.wait_ge(w_hi, 2)
            dve.tensor_tensor(W3L[:, :, :], t.w3f[:, :, :], W3H[:, :, :], ALU.subtract).then_inc(w_lo, 1)
            dve.wait_ge(w_hi, 3)
            dve.tensor_tensor(WFL[:, :, :], WS[:, :, :], WFH[:, :, :], ALU.subtract).then_inc(w_lo, 1)
            dve.wait_ge(const_in, 48)

            def shifted(tile, k):
                dy, dx = divmod(k, 3)
                if dy == 1:
                    return X0E[:, in_ring(tile), dx:dx + W]
                return X0O[:, at(tile, off=dy // 2), dx:dx + W]

            def body(at_stage):
                m, d = at_stage["main"], at_stage["dw"]
                if d:
                    nxt = d.half + (d.s + 1) // 2
                    dve.wait_ge(x0_odd[d.s], 32 * d.half + 32)
                    if not (isinstance(d.n, int) and d.n == TILES - 1):
                        dve.wait_ge(x0_odd[1 - d.s], 32 * nxt + 32)
                for k in range(TAPS):
                    if m:
                        dve.wait_ge(w3_done, 9 * m.n + (k + 1))
                        wait(dve, add_done, 5 * m.n - 5 + (k // 2 + 1 if k < 8 else 0))
                        dve.scalar_tensor_tensor(rows(PR[:, k, :] if k < 8 else PL[:, m.s, :]), rows(p3[k % 3][:, :]),
                                                 t.b3p[:, bass.ds(m.b, 1), k], shifted(m, k),
                                                 ALU.add, ALU.mult).then_inc(mult_done, 1)
                    if d and k > 0:
                        y = rows(Y[:, d.s, :])
                        if k == 1:
                            dve.wait_ge(y0_done, d.n + 1)
                        else:
                            dve.wait_ge(dw_done, 8 * d.n + (k - 1))
                        dve.scalar_tensor_tensor(y, shifted(d, k), w1[:, k:k + 1], y, ALU.mult, ALU.add)\
                            .then_inc(dw_done, 1)
                    if k == 3 and (y := at_stage["ysplit"]) and y.s == 1:
                        dve.wait_ge(yh_done, y.n + 1)
                        dve.tensor_tensor(YL[:, y.s, :], Y[:, y.s, :], YH[:, y.s, :], ALU.subtract)\
                            .then_inc(yl_done[1], 1)
                    if k == 4 and (l := at_stage["lrelu"]):
                        dve.wait_ge(add_done, 5 * l.n + 5)
                        wait(dve, t_odd[l.s], 32 * l.half)
                        dve.scalar_tensor_tensor(TE[:, l.s, :], AC[:, l.s, :], 0.2, AC[:, l.s, :],
                                                 ALU.mult, ALU.max).then_inc(lrelu_done, 1)
                    if k == 1 and (f := at_stage["fin"]):
                        dve.wait_ge(wf_done, f.n + 1)
                        dve.wait_ge(res_done, f.n + 1)
                        wait(dve, stored[f.s], 32 * f.half)
                        dve.tensor_tensor(OUT[:, f.s, :], pf[f.s][:, :], XR[:, f.s, :], ALU.add).then_inc(fin_done, 1)

            pipeline(dve, TILES, PER, {"dw": 2, "ysplit": 1, "main": 0, "lrelu": -1, "fin": -5}, body)


CT = 4
TILES_C = C // CT
MODES = F // 2 * F


def of_sample(tensor, b):
    if isinstance(b, int):
        return tensor[:, b]
    ap = tensor[:, bass.ds(b, 1)]
    return ap.rearrange("p o a c -> p (o a) c") if len(ap.shape) == 4 else ap.rearrange("p o a -> p (o a)")


class Chain:

    def __init__(self, eng, sem, length, turn):
        self.eng, self.sem, self.base, self.n, self.length = eng, sem, turn * length, 0, length

    def __call__(self, ins):
        self.n += 1
        ins.then_inc(self.sem, 1)
        self.eng.wait_ge(self.sem, self.base + self.n)


CHAIN = 12
CHAIN_SUMS, CHAIN_VAR = 3, 7


def group_scale_steps(dve, step, s, sums_done, sums, std_done, std, turn):
    ALU = mybir.AluOpType
    bn = s.bn[:, :, :].rearrange("p g (e k) -> p (g e) k", k=3)
    mean, m2 = bn[:, :, 1], bn[:, :, 2]
    step(dve.tensor_copy(s.sums[:, 0, :], mean))
    step(dve.tensor_tensor(s.sq[:, :], mean, mean, ALU.mult))
    step(dve.scalar_tensor_tensor(s.sums[:, 1, :], m2, 1.0 / W, s.sq[:, :], ALU.mult, ALU.add))
    dve.wait_ge(sums_done, turn + 1)
    step(dve.tensor_reduce(s.ms[:, :], sums[:, :].rearrange("p (g e) -> p g e", e=2), mybir.AxisListType.X, ALU.add))
    m, e2 = s.ms[:, 0:G], s.ms[:, G:2 * G]
    step(dve.tensor_tensor(s.var[:, :], m, m, ALU.mult))
    step(dve.tensor_tensor(s.var[:, :], e2, s.var[:, :], ALU.subtract))
    step(dve.tensor_scalar(s.var[:, :], s.var[:, :], EPS, None, ALU.add))
    dve.wait_ge(std_done, turn + 1)
    step(dve.reciprocal(s.r[:, :], std[:, :]))
    step(dve.tensor_tensor(s.t[:, :], s.r[:, :], s.r[:, :], ALU.mult))
    step(dve.tensor_tensor(s.t[:, :], s.t[:, :], s.var[:, :], ALU.mult))
    step(dve.tensor_scalar(s.t[:, :], s.t[:, :], -0.5, 1.5, ALU.mult, ALU.add))
    step(dve.tensor_tensor(s.r[:, :], s.r[:, :], s.t[:, :], ALU.mult))


class GroupScaleBuffers:
    def __init__(self, sb, name):
        F32 = mybir.dt.float32
        self.bn = sb(name + "_bn", [P, G, 6], F32)
        self.sums = sb(name + "_sums", [P, 2, 2 * G], F32)
        self.sq = sb(name + "_sq", [P, 2 * G], F32)
        self.ms = sb(name + "_ms", [P, 2 * G], F32)
        self.var = sb(name + "_var", [P, G], F32)
        self.std = sb(name + "_std", [P, G], F32)
        self.r = sb(name + "_r", [P, G], F32)
        self.t = sb(name + "_t", [P, G], F32)


def forward_rows(pe, psum, x, basis, q):
    for c in range(CT):
        last = pe.matmul(psum[:, c * P:(c + 1) * P], x[:, CT * q + c, :], basis[:, :], start=True, stop=True)
    return last


def forward_columns(pe, psum, T, basis):
    for u in range(F):
        half, u1 = divmod(u, F // 2)
        for k in range(4):
            last = pe.matmul(psum[C * half:C * half + C, u1 * F:(u1 + 1) * F], T[:, k * F + u, :],
                             basis[:, k, :], start=(k == 0), stop=(k == 3))
    return last


def tile_of_T(T, psum, q):
    return (T[:, :, CT * q:CT * q + CT],
            psum[:, :].rearrange("p (c k) -> p k c", c=CT))


class Mixing:

    QM = 128
    CHUNKS = MODES // QM
    EIGHT = 8

    def __init__(self, nc, ctx, sb, sem, name, hd, wt, out, banks):
        self.hd, self.wt, self.out, self.banks = hd, wt, out, banks
        self.w_in = [sem(f"{name}_w_in{s}") for s in range(2)]
        self.old_in = [sem(f"{name}_old_in{s}") for s in range(2)]
        self.hd_done = sem(f"{name}_hd_done")
        self.pe_done = sem(f"{name}_pe_done")
        self.out_done = sem(f"{name}_out_done")
        self.stored = [sem(f"{name}_stored{s}") for s in range(2)]

    def load(self, sp, weights, q):
        s = q % 2
        if q >= 2:
            sp.wait_ge(self.pe_done, 16 * (q - 1))
        for half in range(2):
            x = F // 2 * half + 4 * q
            sp.dma_start(self.wt[s][C * half:C * half + C, :, :],
                         weights[:, :, x:x + 4, :].rearrange("i o x y -> i o (x y)")).then_inc(self.w_in[s], 16)

    def load_old(self, sp, old, q):
        s = q % 2
        if q >= 2:
            sp.wait_ge(self.stored[s], 16)
        sp.dma_start(self.out[s], old[:, q * self.QM:(q + 1) * self.QM, :].rearrange("p m o -> p (m o)"))\
            .then_inc(self.old_in[s], 16)

    def store(self, sp, new, q):
        s = q % 2
        sp.wait_ge(self.out_done, 16 * q + 16)
        sp.dma_start(new[:, q * self.QM:(q + 1) * self.QM, :].rearrange("p m o -> p (m o)"), self.out[s])\
            .then_inc(self.stored[s], 16)

    def spread(self, dve, H, q):
        s = q % 2
        if q >= 2:
            dve.wait_ge(self.pe_done, 16 * (q - 1))
        for half in range(2):
            last = dve.tensor_copy(
                self.hd[C * half:C * half + C, s, :, B * half:B * half + B],
                H[C * half:C * half + C, :, q * self.QM:(q + 1) * self.QM].rearrange("p b m -> p m b"))
        last.then_inc(self.hd_done, 1)

    def multiply(self, pe, q):
        s = q % 2
        pe.wait_ge(self.w_in[s], 32 * (q // 2) + 32)
        pe.wait_ge(self.hd_done, q + 1)
        for n in range(self.QM // self.EIGHT):
            at = 16 * q + n
            if at >= len(self.banks):
                pe.wait_ge(self.out_done, at - len(self.banks) + 1)
            bank = self.banks[at % len(self.banks)]
            for j in range(self.EIGHT):
                m = n * self.EIGHT + j
                last = pe.matmul(bank[0:2 * B, C * j:C * j + C], self.hd[:, s, m, :], self.wt[s][:, :, m],
                                 start=True, stop=True)
            last.then_inc(self.pe_done, 1)

    def take(self, dve, q, add):
        s = q % 2
        if add:
            dve.wait_ge(self.old_in[s], 16 * (q // 2) + 16)
        elif q >= 2:
            dve.wait_ge(self.stored[s], 16 * (q // 2))
        for n in range(16):
            at = 16 * q + n
            dve.wait_ge(self.pe_done, at + 1)
            bank = self.banks[at % len(self.banks)]
            dst = self.out[s][:, n * 512:(n + 1) * 512]
            if add:
                ins = dve.tensor_tensor(dst, dst, bank[0:2 * B, :], mybir.AluOpType.add)
            else:
                ins = dve.tensor_copy(dst, bank[0:2 * B, :])
            ins.then_inc(self.out_done, 1)


def layer1_analyse(nc, t):
    F32 = mybir.dt.float32
    ALU = mybir.AluOpType
    ACT = mybir.ActivationFunctionType
    with ExitStack() as ctx:
        def sb(name, shape, dt=F32):
            return ctx.enter_context(nc.sbuf_tensor(name, shape, dt))

        def sem(name):
            return ctx.enter_context(nc.semaphore(name))

        def pb(name):
            return ctx.enter_context(nc.psum_tensor(name, [P, 512], F32))

        X = sb("a_x", [P, 2, C, W])
        T = sb("a_t", [P, P, C])
        HM = sb("a_h", [P, B, MODES])
        WT = sb("a_w", [P, 2, C, 128])
        HD = sb("a_hd", [P, 2, 128, 2 * B])
        rows_basis = sb("a_rows", [P, P])
        cols_basis = sb("a_cols", [P, 4, F])
        ones_modes = sb("a_ones_modes", [P, MODES])
        shift_modes = sb("a_shift_modes", [P, MODES])
        ones = sb("a_ones", [P, P])
        one = sb("a_one", [1, 1])
        st = GroupScaleBuffers(sb, "a_gs")
        SC = sb("a_sc", [P, 2, G])
        SCX = sb("a_scx", [1, 2, G, 2])
        SCP = sb("a_scp", [P, 2])
        pT = [pb(f"a_pt{i}") for i in range(4)]
        pH = pb("a_ph")
        pS = ctx.enter_context(nc.psum_tensor("a_ps", [P, 4 * G], F32))
        pP = ctx.enter_context(nc.psum_tensor("a_pp", [P, 2], F32))

        const_in = sem("a_const_in")
        ones_set = sem("a_ones_set")
        cleared = sem("a_cleared")
        x_in = [[sem(f"a_x_in{s}{h}") for h in range(2)] for s in range(2)]
        bn_done = sem("a_bn_done")
        chain = sem("a_chain")
        sums_done = sem("a_sums_done")
        std_done = sem("a_std_done")
        scale_done = sem("a_scale_done")
        expanded = sem("a_expanded")
        turned = sem("a_turned")
        scp_done = sem("a_scp_done")
        shift_done = sem("a_shift_done")
        rows_done = sem("a_rows_done")
        t_out = sem("a_t_out")
        cols_done = sem("a_cols_done")
        h_out = sem("a_h_out")
        mix = Mixing(nc, ctx, sb, sem, "a_mix", HD, [WT[:, s, :, :] for s in range(2)],
                     [X[0:2 * B, s, :, :].rearrange("p c w -> p (c w)") for s in range(2)], pT)
        NT = TILES_C
        LEAD = 4
        SUMS_AT, STD_AT = 9, 11

        block = ctx.enter_context(nc.Block())
        x1 = t.x1.rearrange("b c h w -> b h c w")

        @block.sync
        def _(sp):
            def load(b, s):
                for c in range(0, C, 8):
                    sp.dma_start(X[:, s, c:c + 8, :], x1[b, :, c:c + 8, :]).then_inc(x_in[s][c // 32], 16)

            load(0, 0)
            for dst, src in ((rows_basis[:, :], t.fwd_rows), (cols_basis[:, :, :], t.fwd_cols),
                             (ones_modes[:, :], t.ones_modes)):
                sp.dma_start(dst, src).then_inc(const_in, 16)
            load(1, 1)
            mix.load(sp, t.weights1, 0)
            mix.load(sp, t.weights1, 1)
            with sp.Fori(1, B // 2) as bb:
                for s in range(2):
                    sp.wait_ge(rows_done, NT * (2 * bb + (s - 1)))
                    sp.wait_ge(bn_done, 2 * bb + (s - 1))
                    load(2 * bb + s, s)
            for q in range(2, mix.CHUNKS):
                mix.load(sp, t.weights1, q)
                mix.store(sp, t.o_ht, q - 2)
            for q in range(mix.CHUNKS - 2, mix.CHUNKS):
                mix.store(sp, t.o_ht, q)
            for s in range(2):
                sp.wait_ge(mix.stored[s], 32)

        @block.scalar
        def _(act):
            def body(b):
                for q in range(NT):
                    act.wait_ge(rows_done, NT * b + (q + 1))
                    if q == 0 and not isinstance(b, int):
                        act.wait_ge(cols_done, b)
                    dst, src = tile_of_T(T, pT[q % 4], q)
                    act.activation(dst, src, ACT.Copy).then_inc(t_out, 1)
                    if q == STD_AT:
                        act.wait_ge(chain, CHAIN * b + CHAIN_VAR)
                        act.activation(st.std[:, :], st.var[:, :], ACT.Sqrt).then_inc(std_done, 1)
                act.wait_ge(scp_done, b + 1)
                if not isinstance(b, int):
                    act.wait_ge(h_out, b)
                act.activation(shift_modes[:, :], ones_modes[:, :], ACT.Copy, scale=SCP[:, 1:2])\
                    .then_inc(shift_done, 1)

            act.nop().then_inc(t_out, 4)
            act.wait_ge(const_in, 48)
            body(0)
            with act.Fori(1, B) as b:
                body(b)

        @block.tensor
        def _(pe):
            def columns(b):
                pe.wait_ge(t_out, NT * b + (NT + 4))
                if not isinstance(b, int):
                    pe.wait_ge(h_out, b)
                forward_columns(pe, pH, T, cols_basis).then_inc(cols_done, 1)

            def body(b, s, before):
                for q in range(NT):
                    if q % 8 == 0:
                        pe.wait_ge(x_in[s][q // 8], 64 * (b // 2) + 64)
                    if q == LEAD and before is not None:
                        columns(before)
                    if q == SUMS_AT:
                        pe.wait_ge(chain, CHAIN * b + CHAIN_SUMS)
                        pe.matmul(pS[:, :], ones[:, :], st.sums[:, :, :].rearrange("p a g -> p (a g)"), start=True,
                                  stop=True).then_inc(sums_done, 1)
                    pe.wait_ge(t_out, NT * b + (q + 1))
                    forward_rows(pe, pT[q % 4], X[:, s, :, :], rows_basis, q).then_inc(rows_done, 1)
                pe.wait_ge(expanded, b + 1)
                for half in range(2):
                    for k in range(2):
                        last = pe.matmul(pP[C * half:C * half + C, k:k + 1],
                                         SCX[:, k, :, :].rearrange("p g e -> p (g e)"), one[:, :],
                                         start=True, stop=True)
                last.then_inc(turned, 1)

            pe.wait_ge(const_in, 48)
            pe.wait_ge(ones_set, 1)
            body(0, 0, None)
            body(1, 1, 0)
            with pe.Fori(1, B // 2) as bb:
                for s in range(2):
                    body(2 * bb + s, s, 2 * bb + (s - 1))
            pe.wait_ge(h_out, B - 1)
            columns(B - 1)
            pe.wait_ge(t_out, NT * B + 4)
            for q in range(mix.CHUNKS):
                mix.multiply(pe, q)

        @block.vector
        def _(dve):
            def modes(b):
                dve.wait_ge(cols_done, b + 1)
                dve.wait_ge(shift_done, b + 1)
                dve.scalar_tensor_tensor(of_sample(HM, b), pH[:, :], SCP[:, 0:1], shift_modes[:, :],
                                         ALU.mult, ALU.add).then_inc(h_out, 1)
                dve.wait_ge(h_out, b + 1)

            def body(b, s, before):
                for g in range(G):
                    if g % 16 == 0:
                        dve.wait_ge(x_in[s][g // 16], 64 * (b // 2) + 64)
                    last = dve.bn_stats(st.bn[:, g, :], X[:, s, 2 * g:2 * g + 2, :].rearrange("p c w -> p (c w)"))
                last.then_inc(bn_done, 1)
                if before is not None:
                    modes(before)
                dve.wait_ge(bn_done, b + 1)
                step = Chain(dve, chain, CHAIN, b)
                group_scale_steps(dve, step, st, sums_done, pS, std_done, st.std, b)
                scale, shift = SC[:, 0, :], SC[:, 1, :]
                dve.tensor_copy(scale, st.r[:, :]).then_inc(scale_done, 1)
                dve.scalar_tensor_tensor(shift, st.ms[:, 0:G], -1.0, st.r[:, :], ALU.mult, ALU.mult)\
                    .then_inc(scale_done, 1)
                dve.wait_ge(scale_done, 2 * b + 2)
                for e in range(2):
                    last = dve.tensor_copy(SCX[:, :, :, e], SC[0:1, :, :])
                last.then_inc(expanded, 1)
                dve.tensor_copy(of_sample(t.gn1, b), SC[:, :, :])
                dve.wait_ge(turned, b + 1)
                dve.tensor_copy(SCP[:, :], pP[:, :]).then_inc(scp_done, 1)
                dve.wait_ge(scp_done, b + 1)

            dve.memset(one[:, :], 1.0)
            dve.memset(ones[:, :], 1.0 / 256).then_inc(ones_set, 1)
            dve.memset(HD[:, :, :, :], 0.0).then_inc(cleared, 1)
            dve.wait_ge(cleared, 1)
            body(0, 0, None)
            body(1, 1, 0)
            with dve.Fori(1, B // 2) as bb:
                for s in range(2):
                    body(2 * bb + s, s, 2 * bb + (s - 1))
            modes(B - 1)
            for q in range(2):
                mix.spread(dve, HM, q)
            for q in range(mix.CHUNKS):
                mix.take(dve, q, False)
                if q + 2 < mix.CHUNKS:
                    mix.spread(dve, HM, q + 2)


def inverse_columns(pe, psum, O, basis, q):
    for c in range(CT):
        last = pe.matmul(psum[:, c * W:(c + 1) * W], O[:, :, CT * q + c], basis[:, :], start=True, stop=True)
    return last


def inverse_rows(pe, psum, Z, basis):
    return pe.matmul(psum[:, :], basis[:, :], Z, start=True, stop=True)


def load_diagonal(sp, O, o_ht, b, sem):
    src = o_ht.rearrange("(h b) (u v) o -> b h v u o", h=2, v=F)
    for k in range(4):
        for half in range(2):
            u = F * k + F // 2 * half
            sp.dma_start(O[F * k:F * k + F, u:u + F // 2, :], src[b, half, :, :, :]).then_inc(sem, 16)


def layer1_refine(nc, t):
    F32 = mybir.dt.float32
    ALU = mybir.AluOpType
    ACT = mybir.ActivationFunctionType
    ERR_TH = 0.1
    with ExitStack() as ctx:
        def sb(name, shape, dt=F32):
            return ctx.enter_context(nc.sbuf_tensor(name, shape, dt))

        def sem(name):
            return ctx.enter_context(nc.semaphore(name))

        def pb(name):
            return ctx.enter_context(nc.psum_tensor(name, [P, 512], F32))

        X = sb("r_x", [P, 2, C, W])
        O = sb("r_o", [P, P, C])
        T = sb("r_t", [P, P, C])
        HM = sb("r_h", [P, B, MODES])
        WT = sb("r_w", [P, C, 128])
        HD = sb("r_hd", [P, 2, 128, 2 * B])
        Z = sb("r_z", [P, 2, CT * W])
        D = sb("r_d", [P, 3, CT * W])
        SC = sb("r_sc", [P, 2, 2, G])
        rows_basis = sb("r_rows", [P, P])
        cols_basis = sb("r_cols", [P, 4, F])
        inv_cols = sb("r_icols", [P, W])
        inv_rows = sb("r_irows", [P, P])
        pZ = [pb(f"r_pz{i}") for i in range(2)]
        pR = [pb(f"r_pr{i}") for i in range(2)]
        pT = [pb(f"r_pt{i}") for i in range(3)]
        pH = pb("r_ph")

        const_in = sem("r_const_in")
        cleared = sem("r_cleared")
        x_in = [sem(f"r_x_in{s}") for s in range(2)]
        o_in = sem("r_o_in")
        sc_ready = sem("r_sc_ready")
        norm_done = sem("r_norm_done")
        icols_done = sem("r_icols_done")
        z_out = sem("r_z_out")
        irows_done = sem("r_irows_done")
        diff_done = sem("r_diff_done")
        abs_done = sem("r_abs_done")
        masked = sem("r_masked")
        rows_done = sem("r_rows_done")
        t_out = sem("r_t_out")
        cols_done = sem("r_cols_done")
        h_out = sem("r_h_out")
        mix = Mixing(nc, ctx, sb, sem, "r_mix", HD,
                     [WT, O[:, :, :].rearrange("p a b -> p (a b)").rearrange("p (o m) -> p o m", o=C)],
                     [X[0:2 * B, s, :, :].rearrange("p c w -> p (c w)") for s in range(2)], [*pT, *pR])
        NT = TILES_C

        block = ctx.enter_context(nc.Block())
        x1 = t.x1.rearrange("b c h w -> b h c w")

        @block.sync
        def _(sp):
            for dst, src in ((rows_basis[:, :], t.fwd_rows), (cols_basis[:, :, :], t.fwd_cols),
                             (inv_cols[:, :], t.inv_cols), (inv_rows[:, :], t.inv_rows)):
                sp.dma_start(dst, src).then_inc(const_in, 16)

            def load(b, s):
                for c in range(0, C, 8):
                    sp.dma_start(X[:, s, c:c + 8, :], x1[b, :, c:c + 8, :]).then_inc(x_in[s], 16)

            load(0, 0)
            sp.wait_ge(cleared, 1)
            load_diagonal(sp, O, t.o_ht, 0, o_in)
            load(1, 1)
            mix.load(sp, t.refine1, 0)

            def body(b, s, load_x):
                sp.wait_ge(icols_done, NT * b + NT)
                load_diagonal(sp, O, t.o_ht, b + 1, o_in)
                if load_x:
                    sp.wait_ge(rows_done, NT * b + NT)
                    load(b + 2, s)

            with sp.Fori(0, B // 2 - 1) as bb:
                for s in range(2):
                    body(2 * bb + s, s, True)
            body(B - 2, 0, False)
            sp.wait_ge(rows_done, NT * B)
            mix.load(sp, t.refine1, 1)
            mix.load_old(sp, t.o_ht, 0)
            mix.load_old(sp, t.o_ht, 1)
            for q in range(2, mix.CHUNKS):
                mix.load(sp, t.refine1, q)
                mix.store(sp, t.o_sum, q - 2)
                mix.load_old(sp, t.o_ht, q)
            for q in range(mix.CHUNKS - 2, mix.CHUNKS):
                mix.store(sp, t.o_sum, q)
            for s in range(2):
                sp.wait_ge(mix.stored[s], 32)


        @block.scalar
        def _(act):
            def normalise(b, s, q):
                for g in (2 * q, 2 * q + 1):
                    last = act.activation(X[:, s, 2 * g:2 * g + 2, :], X[:, s, 2 * g:2 * g + 2, :], ACT.Identity,
                                          scale=SC[:, s, 0, g:g + 1], bias=SC[:, s, 1, g:g + 1])
                last.then_inc(norm_done, 1)

            def body(b, s, more):
                if more:
                    act.wait_ge(sc_ready, b + 2)
                    act.wait_ge(x_in[1 - s], 128 * ((b + 1) // 2) + 128)
                act.wait_ge(cols_done, b + 1)
                for q in range(NT + 5):
                    if q < NT:
                        act.wait_ge(icols_done, NT * b + (q + 1))
                        if q >= 2:
                            act.wait_ge(irows_done, NT * b + (q - 1))
                        act.activation(Z[:, q % 2, :], pZ[q % 2][:, :], ACT.Copy).then_inc(z_out, 1)
                    if 0 <= q - 2 < NT:
                        n = q - 2
                        act.wait_ge(diff_done, NT * b + (n + 1))
                        act.activation(D[:, n % 3, :], D[:, n % 3, :], ACT.Abs).then_inc(abs_done, 1)
                    if q < NT and more:
                        normalise(b + 1, 1 - s, q)
                    if 0 <= q - 5 < NT:
                        n = q - 5
                        act.wait_ge(rows_done, NT * b + (n + 1))
                        dst, src = tile_of_T(T, pT[n % 3], n)
                        act.activation(dst, src, ACT.Copy).then_inc(t_out, 1)

            act.wait_ge(sc_ready, 1)
            act.wait_ge(x_in[0], 128)
            for q in range(NT):
                normalise(0, 0, q)
            with act.Fori(0, B // 2 - 1) as bb:
                for s in range(2):
                    body(2 * bb + s, s, True)
            body(B - 2, 0, True)
            body(B - 1, 1, False)

        @block.tensor
        def _(pe):
            def body(b, s):
                pe.wait_ge(o_in, 128 * b + 128)
                for q in range(NT + 4):
                    if q < NT:
                        if q >= 2:
                            pe.wait_ge(z_out, NT * b + (q - 1))
                        inverse_columns(pe, pZ[q % 2], O, inv_cols, q).then_inc(icols_done, 1)
                    if 0 <= q - 1 < NT:
                        n = q - 1
                        pe.wait_ge(z_out, NT * b + (n + 1))
                        if n >= 2:
                            pe.wait_ge(diff_done, NT * b + (n - 1))
                        inverse_rows(pe, pR[n % 2], Z[:, n % 2, :], inv_rows).then_inc(irows_done, 1)
                    if 0 <= q - 4 < NT:
                        n = q - 4
                        pe.wait_ge(masked, NT * b + (n + 1))
                        if n >= 3:
                            pe.wait_ge(t_out, NT * b + (n - 2))
                        forward_rows(pe, pT[n % 3], X[:, s, :, :], rows_basis, n).then_inc(rows_done, 1)
                pe.wait_ge(t_out, NT * b + NT)
                pe.wait_ge(h_out, b + 1)
                forward_columns(pe, pH, T, cols_basis).then_inc(cols_done, 1)

            pe.nop().then_inc(cols_done, 1)
            pe.wait_ge(const_in, 64)
            with pe.Fori(0, B // 2) as bb:
                for s in range(2):
                    body(2 * bb + s, s)
            for q in range(mix.CHUNKS):
                mix.multiply(pe, q)

        @block.vector
        def _(dve):
            def scales(b, s):
                dve.tensor_copy(SC[:, s, :, :], of_sample(t.gn1, b)).then_inc(sc_ready, 1)

            def body(b, s, more):
                if more:
                    scales(b + 1, 1 - s)
                for q in range(NT + 3):
                    if q < NT:
                        dve.wait_ge(norm_done, NT * b + (q + 1))
                        dve.wait_ge(irows_done, NT * b + (q + 1))
                        if q >= 3:
                            dve.wait_ge(masked, NT * b + (q - 2))
                        dve.tensor_tensor(D[:, q % 3, :], X[:, s, CT * q:CT * q + CT, :].rearrange("p c w -> p (c w)"),
                                          pR[q % 2][:, :], ALU.subtract).then_inc(diff_done, 1)
                    if 0 <= q - 2 < NT:
                        n = q - 2
                        x = X[:, s, CT * n:CT * n + CT, :].rearrange("p c w -> p (c w)")
                        dve.wait_ge(abs_done, NT * b + (n + 1))
                        dve.scalar_tensor_tensor(x, D[:, n % 3, :], ERR_TH, x, ALU.is_gt, ALU.mult).then_inc(masked, 1)
                dve.wait_ge(cols_done, b + 2)
                dve.tensor_copy(of_sample(HM, b), pH[:, :]).then_inc(h_out, 1)

            dve.memset(O[:, :, :], 0.0).then_inc(cleared, 1)
            scales(0, 0)
            dve.memset(HD[:, :, :, :], 0.0).then_inc(cleared, 1)
            dve.wait_ge(cleared, 2)
            dve.nop().then_inc(h_out, 1)
            with dve.Fori(0, B // 2 - 1) as bb:
                for s in range(2):
                    body(2 * bb + s, s, True)
            body(B - 2, 0, True)
            body(B - 1, 1, False)
            dve.wait_ge(h_out, B + 1)
            for q in range(2):
                mix.spread(dve, HM, q)
            for q in range(mix.CHUNKS):
                mix.take(dve, q, True)
                if q + 2 < mix.CHUNKS:
                    mix.spread(dve, HM, q + 2)


def band_matrices(dve, bands, shifts, coefs, size, step):
    ALU = mybir.AluOpType
    for dx in range(size):
        for dy in range(size):
            diagonal, k = shifts[:, dy, :], coefs[:, dy * size + dx:dy * size + dx + 1]
            if dy == 0:
                step(dve.tensor_scalar(bands[:, dx, :], diagonal, k, None, ALU.mult))
            else:
                step(dve.scalar_tensor_tensor(bands[:, dx, :], diagonal, k, bands[:, dx, :], ALU.mult, ALU.add))


def layers2_and_3(nc, t):
    F32 = mybir.dt.float32
    F32R = mybir.dt.float32r
    ALU = mybir.AluOpType
    ACT = mybir.ActivationFunctionType
    S2, S3 = 3, 9
    PAD = S3 // 2
    NT = TILES_C
    HALF = NT // 2
    RING = 4
    with ExitStack() as ctx:
        def sb(name, shape, dt=F32):
            return ctx.enter_context(nc.sbuf_tensor(name, shape, dt))

        def sem(name):
            return ctx.enter_context(nc.semaphore(name))

        def pb(name):
            return ctx.enter_context(nc.psum_tensor(name, [P, 512], F32))

        X = sb("s_x", [P, 2, C, W])
        O = sb("s_o", [P, P, C])
        Z = sb("s_z", [P, 2, CT * W])
        GN = {n: sb(f"s_g{n}", [P, 2, CT, W + 2 * PAD]) for n in (2, 3)}
        GH = {n: sb(f"s_gh{n}", [P, RING, CT, W + 2 * PAD], F32R) for n in (2, 3)}
        GL = {n: sb(f"s_gl{n}", [P, RING, CT, W + 2 * PAD], F32R) for n in (2, 3)}
        BF = {2: sb("s_b2", [P, S2, P]), 3: sb("s_b3", [P, S3, P])}
        BH = {2: sb("s_bh2", [P, S2, P], F32R), 3: sb("s_bh3", [P, S3, P], F32R)}
        BL = {2: sb("s_bl2", [P, S2, P], F32R), 3: sb("s_bl3", [P, S3, P], F32R)}
        shifts = sb("s_shifts", [P, S2, P])
        alpha = sb("s_alpha", [P, 9])
        beta = sb("s_beta", [P, 1])
        stencils = sb("s_stencils", [P, 8, S2 * S2])
        K2 = sb("s_k2", [P, S2 * S2])
        small = sb("s_small", [P, 2])
        inv_cols = sb("s_icols", [P, W])
        inv_rows = sb("s_irows", [P, P])
        ones = sb("s_ones", [P, P])
        ST = {n: GroupScaleBuffers(sb, f"s_gs{n}") for n in (2, 3)}
        SC = {n: sb(f"s_sc{n}", [P, 2, 2, G]) for n in (2, 3)}
        pZ = [pb(f"s_pz{i}") for i in range(2)]
        pA = [pb(f"s_pa{i}") for i in range(2)]
        pC = [pb(f"s_pc{i}") for i in range(3)]
        pS = ctx.enter_context(nc.psum_tensor("s_ps", [P, 4 * G], F32))

        bases_in = sem("s_bases_in")
        const_in = sem("s_const_in")
        cleared = sem("s_cleared")
        built = sem("s_built")
        b_hi = sem("s_b_hi")
        b_lo = sem("s_b_lo")
        x_in = [[sem(f"s_x_in{s}{q}") for q in range(4)] for s in range(2)]
        o_in = sem("s_o_in")
        icols_done = sem("s_icols_done")
        z_out = sem("s_z_out")
        irows_done = sem("s_irows_done")
        x_sum = {n: sem(f"s_x_sum{n}") for n in (2, 3)}
        bn_done = {n: sem(f"s_bn_done{n}") for n in (2, 3)}
        chain = {n: sem(f"s_chain{n}") for n in (2, 3)}
        sums_done = {n: sem(f"s_sums_done{n}") for n in (2, 3)}
        std_done = {n: sem(f"s_std_done{n}") for n in (2, 3)}
        scale_done = {n: sem(f"s_scale_done{n}") for n in (2, 3)}
        g_done = {n: sem(f"s_g_done{n}") for n in (2, 3)}
        gl_done = {n: sem(f"s_gl_done{n}") for n in (2, 3)}
        conv_done = {n: sem(f"s_conv_done{n}") for n in (2, 3)}
        out_done = sem("s_out_done")
        stored = [[sem(f"s_stored{s}{q}") for q in range(4)] for s in range(2)]

        block = ctx.enter_context(nc.Block())
        x1 = t.x1.rearrange("b c h w -> b h c w")
        out = t.out.rearrange("b c h w -> b h c w")
        BUILT = 12 + S2 * S2

        def steps(eng, body):
            body(0, 0, True, False)
            with eng.Fori(0, B // 2 - 1) as bb:
                for u in range(2):
                    body(2 * bb + (1 + u), (1 + u) % 2, True, True)
            body(B - 1, (B - 1) % 2, True, True)
            body(B, B % 2, False, True)

        def tile_of(s, q):
            return X[:, s, CT * q:CT * q + CT, :].rearrange("p c w -> p (c w)")


        @block.sync
        def _(sp):
            for dst, src in ((inv_cols[:, :], t.inv_cols), (inv_rows[:, :], t.inv_rows)):
                sp.dma_start(dst, src).then_inc(bases_in, 16)
            sp.wait_ge(cleared, 1)
            load_diagonal(sp, O, t.o_sum, 0, o_in)
            for dst, src in ((shifts[:, :, :], t.shifts), (alpha[:, :], t.alpha),
                             (beta[:, :], t.beta),
                             (stencils[:, :, :].rearrange("p a k -> p (a k)"), t.stencils),
                             (BF[3][:, :, :], t.band3)):
                sp.dma_start(dst, src).then_inc(const_in, 16)

            def load(b, s, q):
                for c in range(16 * q, 16 * q + 16, 8):
                    sp.dma_start(X[:, s, c:c + 8, :], x1[b, :, c:c + 8, :]).then_inc(x_in[s][q], 16)

            for q in range(4):
                load(0, 0, q)

            def body(b, s, here, before):
                if here and not (isinstance(b, int) and b == B - 1):
                    sp.wait_ge(icols_done, NT * b + NT)
                    load_diagonal(sp, O, t.o_sum, b + 1, o_in)
                for q in range(4):
                    if before:
                        sp.wait_ge(out_done, NT * (b - 1) + (4 * q + 4))
                        for c in range(16 * q, 16 * q + 16, 8):
                            sp.dma_start(out[b - 1, :, c:c + 8, :], X[:, 1 - s, c:c + 8, :]).then_inc(stored[1 - s][q], 16)
                    if here and not (isinstance(b, int) and b == B - 1):
                        if before:
                            sp.wait_ge(stored[1 - s][q], 32 * ((b + 1) // 2))
                        load(b + 1, 1 - s, q)

            steps(sp, body)
            for s in range(2):
                for q in range(4):
                    sp.wait_ge(stored[s][q], 32 * B // 2)

        def normalised_tiles(act, n, b, s, tiles):
            for q in tiles:
                at, g = NT * b + q, 2 * q
                if q >= 2:
                    act.wait_ge(gl_done[n], NT * b + (q - 1))
                for i in range(2):
                    last = act.activation(GN[n][:, q % 2, 2 * i:2 * i + 2, PAD:PAD + W],
                                          X[:, s, CT * q + 2 * i:CT * q + 2 * i + 2, :], ACT.Identity,
                                          scale=SC[n][:, s, 0, g + i:g + i + 1], bias=SC[n][:, s, 1, g + i:g + i + 1])
                last.then_inc(g_done[n], 1)
                act.wait_ge(g_done[n], 2 * NT * b + (2 * q + 1))
                if q >= RING:
                    act.wait_ge(conv_done[n], NT * b + (q + 1 - RING))
                act.activation(GH[n][:, q % RING, :, :], GN[n][:, q % 2, :, :], ACT.Copy).then_inc(g_done[n], 1)

        @block.scalar
        def _(act):
            def std(n, b):
                act.wait_ge(chain[n], CHAIN * b + CHAIN_VAR)
                act.activation(ST[n].std[:, :], ST[n].var[:, :], ACT.Sqrt).then_inc(std_done[n], 1)

            def body(b, s, here, before):
                if here:
                    for q in range(NT):
                        act.wait_ge(icols_done, NT * b + (q + 1))
                        if q >= 2:
                            act.wait_ge(irows_done, NT * b + (q - 1))
                        act.activation(Z[:, q % 2, :], pZ[q % 2][:, :], ACT.Copy).then_inc(z_out, 1)
                if before:
                    if not here:
                        act.wait_ge(conv_done[3], NT * (b - 1))
                    normalised_tiles(act, 3, b - 1, 1 - s, range(2, 5))
                if here:
                    std(2, b)
                if before:
                    normalised_tiles(act, 3, b - 1, 1 - s, range(5, HALF + 2))
                if here:
                    act.wait_ge(scale_done[2], b + 1)
                    normalised_tiles(act, 2, b, s, range(NT))
                if before:
                    normalised_tiles(act, 3, b - 1, 1 - s, range(HALF + 2, HALF + 4))
                if here:
                    std(3, b)
                if before:
                    normalised_tiles(act, 3, b - 1, 1 - s, range(HALF + 4, NT))
                if here:
                    act.wait_ge(scale_done[3], b + 1)
                    if before:
                        act.wait_ge(gl_done[3], NT * b)
                        act.wait_ge(conv_done[3], NT * b + (2 - RING))
                    normalised_tiles(act, 3, b, s, range(2))

            act.wait_ge(built, BUILT)
            act.wait_ge(const_in, 16 * 5)
            for n in (2, 3):
                act.activation(BH[n][:, :, :], BF[n][:, :, :], ACT.Copy).then_inc(b_hi, 1)
            steps(act, body)

        @block.gpsimd
        def _(pool):
            def low_parts(n, b, tiles):
                for q in tiles:
                    pool.wait_ge(g_done[n], 2 * NT * b + (2 * q + 2))
                    pool.tensor_tensor(GL[n][:, q % RING, :, :], GN[n][:, q % 2, :, :], GH[n][:, q % RING, :, :],
                                       ALU.subtract).then_inc(gl_done[n], 1)

            def body(b, s, here, before):
                if before:
                    low_parts(3, b - 1, range(2, HALF + 2))
                if here:
                    low_parts(2, b, range(NT))
                if before:
                    low_parts(3, b - 1, range(HALF + 2, NT))
                if here:
                    low_parts(3, b, range(2))

            for n in (2, 3):
                pool.wait_ge(b_hi, n - 1)
                pool.tensor_tensor(BL[n][:, :, :], BF[n][:, :, :], BH[n][:, :, :], ALU.subtract).then_inc(b_lo, 1)
            steps(pool, body)

        @block.tensor
        def _(pe):
            def sums(n, b):
                pe.wait_ge(chain[n], CHAIN * b + CHAIN_SUMS)
                pe.matmul(pS[:, :], ones[:, :], ST[n].sums[:, :, :].rearrange("p a g -> p (a g)"), start=True,
                          stop=True).then_inc(sums_done[n], 1)

            def convolve(n, b, tiles, banks, taken):
                size = {2: S2, 3: S3}[n]
                off = PAD - size // 2
                for q in tiles:
                    bank = banks[q % len(banks)]
                    pe.wait_ge(gl_done[n], NT * b + (q + 1))
                    if q >= len(banks):
                        pe.wait_ge(taken, NT * b + (q + 1 - len(banks)))
                    for dx in range(size):
                        for k, (w, g) in enumerate(((BH, GH), (BH, GL), (BL, GH))):
                            last = pe.matmul(bank[:, :], w[n][:, dx, :], g[n][:, q % RING, :, off + dx:off + dx + W],
                                             start=(dx == 0 and k == 0), stop=(dx == size - 1 and k == 2))
                    last.then_inc(conv_done[n], 1)

            def body(b, s, here, before):
                if here:
                    pe.wait_ge(o_in, 128 * b + 128)
                    for q in range(NT + 1):
                        if q < NT:
                            if q >= 2:
                                pe.wait_ge(z_out, NT * b + (q - 1))
                            inverse_columns(pe, pZ[q % 2], O, inv_cols, q).then_inc(icols_done, 1)
                        if q >= 1:
                            pe.wait_ge(z_out, NT * b + q)
                            if q >= 3:
                                pe.wait_ge(x_sum[2], NT * b + (q - 2))
                            inverse_rows(pe, pA[(q - 1) % 2], Z[:, (q - 1) % 2, :], inv_rows).then_inc(irows_done, 1)
                if before:
                    if not here:
                        pe.wait_ge(out_done, NT * (b - 1))
                    convolve(3, b - 1, range(1), pC, out_done)
                if here:
                    sums(2, b)
                if before:
                    convolve(3, b - 1, range(1, HALF), pC, out_done)
                if here:
                    if not before:
                        pe.wait_ge(b_hi, 2)
                        pe.wait_ge(b_lo, 2)
                    convolve(2, b, range(NT), pA, x_sum[3])
                if before:
                    convolve(3, b - 1, range(HALF, HALF + 1), pC, out_done)
                if here:
                    sums(3, b)
                if before:
                    convolve(3, b - 1, range(HALF + 1, NT), pC, out_done)

            pe.wait_ge(bases_in, 32)
            steps(pe, body)

        @block.vector
        def _(dve):
            def tile_sum(n, b, s, q, bank):
                x = tile_of(s, q)
                dve.tensor_tensor(x, x, bank[:, :], ALU.add).then_inc(x_sum[n], 1)

            def tile_statistics(n, b, s, q):
                dve.wait_ge(x_sum[n], NT * b + (q + 1))
                for g in (2 * q, 2 * q + 1):
                    last = dve.bn_stats(ST[n].bn[:, g, :], X[:, s, 2 * g:2 * g + 2, :].rearrange("p c w -> p (c w)"))
                if q == NT - 1:
                    last.then_inc(bn_done[n], 1)

            def scales(n, b, s):
                dve.wait_ge(bn_done[n], b + 1)
                step = Chain(dve, chain[n], CHAIN, b)
                group_scale_steps(dve, step, ST[n], sums_done[n], pS, std_done[n], ST[n].std, b)
                dve.tensor_copy(SC[n][:, s, 0, :], ST[n].r[:, :])
                dve.scalar_tensor_tensor(SC[n][:, s, 1, :], ST[n].ms[:, 0:G], -1.0, ST[n].r[:, :], ALU.mult, ALU.mult)\
                    .then_inc(scale_done[n], 1)
                dve.wait_ge(scale_done[n], b + 1)

            def results(b, s, tiles):
                for q in tiles:
                    x = tile_of(s, q)
                    dve.wait_ge(conv_done[3], NT * b + (q + 1))
                    dve.tensor_tensor(x, x, pC[q % 3][:, :], ALU.add).then_inc(out_done, 1)

            def body(b, s, here, before):
                if here:
                    for q in range(NT + 1):
                        if q < NT:
                            if q % 4 == 0:
                                dve.wait_ge(x_in[s][q // 4], 32 * (b // 2) + 32)
                            dve.wait_ge(irows_done, NT * b + (q + 1))
                            tile_sum(2, b, s, q, pA[q % 2])
                        if q >= 1:
                            tile_statistics(2, b, s, q - 1)
                    scales(2, b, s)
                if before:
                    results(b - 1, 1 - s, range(HALF))
                if here:
                    for q in range(NT + 1):
                        if q < NT:
                            dve.wait_ge(conv_done[2], NT * b + (q + 1))
                            tile_sum(3, b, s, q, pA[q % 2])
                        if q >= 1:
                            tile_statistics(3, b, s, q - 1)
                    scales(3, b, s)
                if before:
                    results(b - 1, 1 - s, range(HALF, NT))

            dve.memset(O[:, :, :], 0.0).then_inc(cleared, 1)
            for n in (2, 3):
                for s in range(2):
                    dve.memset(GN[n][:, s, :, 0:PAD], 0.0)
                    dve.memset(GN[n][:, s, :, PAD + W:], 0.0)
            dve.memset(ones[:, :], 1.0 / 256)
            dve.wait_ge(const_in, 16 * 5)
            done = [0]

            def step(ins):
                done[0] += 1
                ins.then_inc(built, 1)
                dve.wait_ge(built, done[0])

            step(dve.tensor_scalar(K2[:, :], stencils[:, 0, :], alpha[:, 0:1], None, ALU.mult))
            for a in range(1, 8):
                step(dve.scalar_tensor_tensor(K2[:, :], stencils[:, a, :], alpha[:, a:a + 1], K2[:, :],
                                              ALU.mult, ALU.add))
            step(dve.tensor_scalar(small[:, 0:1], alpha[:, 8:9], -1.0 / 9.0, None, ALU.mult))
            step(dve.tensor_tensor(small[:, 1:2], alpha[:, 8:9], beta[:, :], ALU.add))
            step(dve.tensor_scalar(K2[:, :], K2[:, :], small[:, 0:1], None, ALU.add))
            step(dve.tensor_tensor(K2[:, 4:5], K2[:, 4:5], small[:, 1:2], ALU.add))
            band_matrices(dve, BF[2], shifts, K2, S2, step)
            assert done[0] == BUILT
            steps(dve, body)


def conv_blocks(w):
    import numpy as np
    blocks = np.zeros((2, C, 6, 2, C), np.float32)
    for d in range(2):
        for row_in in range(2):
            for row_out in range(2):
                dy = 2 * d + row_in - row_out
                if 0 <= dy < 3:
                    for dx in range(3):
                        blocks[row_in, :, 3 * d + dx, row_out, :] = w[:, :, dy, dx].T
    return blocks.reshape(P, 6, P)


def layer0_arrays(x, w0, b0, w1, b1, w2, b2, w3, b3, wf, bf):
    import numpy as np
    f32 = np.float32

    def both(a):
        return np.concatenate([a, a]).astype(f32)

    w3blk = np.zeros((2, C, 9, 2, C), f32)
    for p in range(2):
        w3blk[p, :, :, p, :] = w3.reshape(C, 9, C).transpose(2, 1, 0)
    taps = both(w0.reshape(C, C, 9).transpose(1, 2, 0))
    grp = np.zeros((P, P), f32)
    band = np.zeros((C, 2, C), f32)
    for c in range(C):
        for p in range(P):
            grp[p, [c0 + q for q in (0, C) for c0 in range(C) if c0 // 2 == (p % C) // 2]] = 0.25
        for k in range(3):
            if 0 <= c + k - 1 < C:
                band[c + k - 1, :, c] = w2[0, 0, k]
    cnt = np.zeros((2, C, 3, 3), f32)
    for h in range(2):
        for dy in range(3):
            for dx in range(3):
                gone = (dy == 0 and h == 1) or (dy == 2 and h == 0)
                cnt[h, :, dy, dx] = (H // 2 - gone) * (W - (dx != 1))
    half = np.zeros((2, C, 2), f32)
    half[0, :, 0] = half[1, :, 1] = -1.0
    mask = np.ones((2, C, 16), f32)
    mask[0, :, 0] = mask[1, :, 15] = 0.0
    b12 = np.zeros((2, C, 3), f32)
    b12[:, :, 0], b12[:, :, 1], b12[:, :, 2] = b1, bf, b2[0]
    x_rows = np.zeros((B, C, H + 2, W), f32)
    x_rows[:, :, 1:H + 1] = x
    return {
        "x": x, "x_rows": x_rows, "w0taps": taps, "grp": grp, "band": band.reshape(C, P),
        "cnt": cnt.reshape(P, 9), "half": half.reshape(P, 2), "b0": both(b0).reshape(P, 1),
        "b12": b12.reshape(P, 3), "b3": both(b3.reshape(C, 9)), "w3blk": w3blk.reshape(P, 9, P),
        "w0blk": conv_blocks(w0), "wfblk": conv_blocks(wf), "w1": both(w1.reshape(C, 9)),
        "mask": mask.reshape(P, 16),
    }


def spectral_bases():
    import numpy as np
    tau = 2 * np.pi / H
    n, k = np.meshgrid(np.arange(H), np.arange(F), indexing="ij")
    fa, fb = tau * (n * k % H), tau * ((n + 1) * k % H)
    ia, ib = fa.T, (tau * (n * (k + 1) % H)).T
    f32 = np.float32
    ones = sum(np.outer(x.sum(0), y.sum(0)) * sign for x, y, sign in (
        (np.cos(fa), np.cos(fa), 1), (np.sin(fa), np.sin(fa), -1), (np.cos(fb), np.sin(fb), -1),
        (np.sin(fb), np.cos(fb), -1)))
    return {
        "ones_modes": np.repeat(ones.reshape(2, 1, MODES), C, 1).reshape(P, MODES).astype(f32),
        "fwd_rows": np.concatenate([np.cos(fa), np.sin(fa), np.cos(fb), np.sin(fb)], 1).astype(f32),
        "fwd_cols": np.stack([np.cos(fa), -np.sin(fa), -np.sin(fb), -np.cos(fb)], 1).astype(f32),
        "inv_cols": np.concatenate([np.cos(ia), np.sin(ia), np.cos(ib), np.sin(ib)], 0).astype(f32),
        "inv_rows": (np.concatenate([np.cos(ia), -np.sin(ia), -np.sin(ib), -np.cos(ib)], 0) / (H * W)).astype(f32),
    }


def row_shifts():
    import numpy as np
    return np.stack([np.eye(P, k=1 - dy) for dy in range(3)], 1).astype(np.float32)


def stencil_arrays(alpha, beta, kernels, k3):
    import numpy as np
    flat = {"alpha": alpha, "beta": beta, "stencils": kernels}
    band3 = np.zeros((P, 9, P), np.float32)
    for dy in range(9):
        for out in range(max(0, 4 - dy), min(P, P + 4 - dy)):
            band3[out + dy - 4, :, out] = k3[0, 0, dy]
    return {"band3": band3, **{name: np.ascontiguousarray(np.broadcast_to(a.reshape(1, -1), (P, a.size)))
                               for name, a in flat.items()}}


_INS = ["x", "x_rows", "w0taps", "grp", "band", "cnt", "half", "b0", "b12", "b3", "w3blk", "w0blk", "wfblk", "w1",
        "mask", "weights1", "refine1", "fwd_rows", "fwd_cols", "inv_cols", "inv_rows", "ones_modes",
        "shifts", "alpha", "beta",
        "stencils", "band3"]


class Arrays:

    def __init__(self, args):
        (self.x, self.x_rows, self.w0taps, self.grp, self.band, self.cnt, self.half, self.b0, self.b12, self.b3,
         self.w3blk, self.w0blk, self.wfblk, self.w1, self.mask, self.weights1, self.refine1, self.fwd_rows,
         self.fwd_cols, self.inv_cols, self.inv_rows, self.ones_modes, self.shifts, self.alpha, self.beta, self.stencils, self.band3,
         self.out) = args


def conv_stack_kernel(nc, *args):
    F32 = mybir.dt.float32
    t = Arrays(args)
    t.x1 = nc.dram_tensor("x1", (B, C, H, W), F32, kind="Internal").ap()
    t.o_ht = nc.dram_tensor("o_ht", (2 * B, MODES, C), F32, kind="Internal").ap()
    t.o_sum = nc.dram_tensor("o_sum", (2 * B, MODES, C), F32, kind="Internal").ap()
    with ExitStack() as ctx:
        t.gn0 = ctx.enter_context(nc.sbuf_tensor("gn0", [P, 4, B], F32))
        t.b3p = ctx.enter_context(nc.sbuf_tensor("b3p", [P, B, 9], F32))
        t.w3f = ctx.enter_context(nc.sbuf_tensor("w3f", [P, 9, P], F32))
        layer0_statistics(nc, t)
        layer0_convolutions(nc, t)
    with ExitStack() as ctx:
        t.gn1 = ctx.enter_context(nc.sbuf_tensor("gn1", [P, B, 2, G], F32))
        layer1_analyse(nc, t)
        layer1_refine(nc, t)
    layers2_and_3(nc, t)


def kernel(**inputs):
    import numpy as np
    import concourse.bacc as bacc
    from concourse.bass_utils import run_bass_kernel_spmd

    given = {name: np.asarray(a) for name, a in inputs.items()}
    laid_out = {
        **layer0_arrays(given["x"], *[given[f"L0_conv_{k}"]
                                      for k in ("w0", "b0", "w1", "b1", "w2", "b2", "w3", "b3", "wf", "bf")]),
        "weights1": given["L1_conv_weights1"], "refine1": given["L1_conv_refine_weights1"],
        **spectral_bases(), "shifts": row_shifts(),
        **stencil_arrays(given["L2_conv_alpha"], given["L2_conv_beta"], given["L2_conv_kernels"],
                         given["L3_conv_K"]),
    }
    nc = bacc.Bacc("TRN2", target_bir_lowering=False, num_devices=1)
    arrays, args = {}, []
    for name in _INS:
        a = np.ascontiguousarray(laid_out[name])
        arrays[f"in_{name}_dram"] = a
        args.append(nc.dram_tensor(f"in_{name}_dram", a.shape, mybir.dt.from_np(a.dtype), kind="ExternalInput").ap())
    args.append(nc.dram_tensor("out_dram", (B, C, H, W), mybir.dt.float32, kind="ExternalOutput").ap())
    conv_stack_kernel(nc, *args)
    r = run_bass_kernel_spmd(nc, [arrays], core_ids=[0])
    return r.results[0]["out_dram"]
```

```python
from contextlib import ExitStack

import concourse.bass as bass
from concourse import mybir

B, C, H, W = 8, 64, 128, 128
P = 128
G = 32
F = 32
EPS = 1e-5


def layer0_statistics(nc, t):
    F32 = mybir.dt.float32
    ALU = mybir.AluOpType
    ACT = mybir.ActivationFunctionType
    AX = mybir.AxisListType.X
    with ExitStack() as ctx:
        def sb(name, shape, dt=F32):
            return ctx.enter_context(nc.sbuf_tensor(name, shape, dt))

        def sem(name):
            return ctx.enter_context(nc.semaphore(name))

        ROWS = H // 2
        CH = 16
        NCH = ROWS // CH
        NBUF = 4
        XC = sb("st_x", [P, NBUF, CH * W])
        BS = sb("st_bn", [P, B, NCH * 4 * 6])
        EC = sb("st_edgecols", [P, B, NCH, 2])
        ER = sb("st_edgerow", [P, B, W])
        MV = sb("st_mv", [P, B, 2])
        EX = sb("st_ex", [P, 2, B])
        M = sb("st_m", [P, 2, B])
        VAR = sb("st_var", [P, B])
        RX = sb("st_rx", [P, 3, B])
        D = sb("st_d", [P, 3, B])
        ECS = sb("st_ecs", [P, B, 2])
        V = sb("st_v", [P, 9, B])
        V2 = sb("st_v2", [P, 9, B])
        w0blk = sb("st_w0blk", [P, 6, P])
        wfblk = sb("st_wfblk", [P, 6, P])
        w3blk = sb("st_w3blk", [P, 9, P])
        taps = sb("st_w0taps", [P, 9, C])
        grp = sb("st_grp", [P, P])
        band = sb("st_band", [C, P])
        cnt = sb("st_cnt", [P, 9])
        half = sb("st_half", [P, 2])
        b0 = sb("st_b0", [C, 1])
        b12 = sb("st_b12", [P, 3])
        b3 = sb("st_b3", [P, 9])
        XM = sb("st_xm", [C, B])
        X2 = sb("st_x2", [P, B])
        STD = sb("st_std", [P, B])
        pg = ctx.enter_context(nc.psum_tensor("st_pg", [P, 2 * B], F32))
        pm = ctx.enter_context(nc.psum_tensor("st_pm", [C, B], F32))
        px = ctx.enter_context(nc.psum_tensor("st_px", [P, B], F32))
        p3 = ctx.enter_context(nc.psum_tensor("st_p3", [P, 9 * B], F32))

        chunk_in = [sem(f"st_chunk_in{n}") for n in range(NBUF)]
        const_in = sem("st_const_in")
        weights_in = sem("st_weights_in")
        weights_hi = sem("st_weights_hi")
        weights_lo = sem("st_weights_lo")
        chunk_used = sem("st_chunk_used")
        chain = sem("st_chain")
        group_done = sem("st_group_done")
        std_done = sem("st_std_done")
        mean_done = sem("st_mean_done")
        xm_done = sem("st_xm_done")
        x2_done = sem("st_x2_done")
        x2_out = sem("st_x2_out")
        b3_done = sem("st_b3_done")

        C_EX = B + 4
        C_VAR = C_EX + 4
        C_V = C_VAR + 14 + 3 + 18

        block = ctx.enter_context(nc.Block())
        halves = t.x.rearrange("b c (h r) w -> b h c (r w)", h=2)

        @block.sync
        def _(sp):
            for q in range(NCH):
                for h in range(2):
                    sp.dma_start(XC[C * h:C * h + C, q, :], halves[0, h, :, q * CH * W:(q + 1) * CH * W])\
                        .then_inc(chunk_in[q], 16)
            with sp.Fori(1, B) as b:
                for q in range(NCH):
                    sp.wait_ge(chunk_used, b * NCH + (q + 1 - NCH))
                    for h in range(2):
                        sp.dma_start(XC[C * h:C * h + C, q, :], halves[b, h, :, q * CH * W:(q + 1) * CH * W])\
                            .then_inc(chunk_in[q], 16)

        @block.scalar
        def _(act):
            for dst, src in ((taps[:, :, :], t.w0taps), (grp[:, :], t.grp), (band[:, :], t.band),
                             (cnt[:, :], t.cnt), (half[:, :], t.half), (b0[:, :], t.b0[0:C, :]),
                             (b12[:, :], t.b12), (b3[:, :], t.b3),
                             (ER[0:C, :, :], t.x[:, :, 0, :].rearrange("b c w -> c b w")),
                             (ER[C:P, :, :], t.x[:, :, H - 1, :].rearrange("b c w -> c b w"))):
                act.dma_start(dst, src).then_inc(const_in, 16)
            for dst, src in ((w3blk, t.w3blk), (w0blk, t.w0blk), (wfblk, t.wfblk)):
                act.dma_start(dst[:, :, :], src).then_inc(weights_in, 16)
            act.wait_ge(weights_in, 48)
            for w, parts in ((w3blk, t.w3), (w0blk, t.w0), (wfblk, t.wf)):
                act.activation(parts[0][:, :, :], w[:, :, :], mybir.ActivationFunctionType.Copy)\
                    .then_inc(weights_hi, 1)
            act.wait_ge(chain, C_VAR)
            act.activation(STD[:, :], VAR[:, :], ACT.Sqrt).then_inc(std_done, 1)
            act.wait_ge(mean_done, 1)
            act.activation(XM[:, :], pm[:, :], ACT.Identity, scale=1.0 / (H * W), bias=b0[:, :]).then_inc(xm_done, 1)
            act.wait_ge(x2_done, 1)
            act.activation(X2[:, :], px[:, :], ACT.Identity, bias=b12[:, 2:3]).then_inc(x2_out, 1)
            act.wait_ge(x2_out, 1)
            act.activation(X2[:, :], X2[:, :], ACT.Identity, bias=b12[:, 0:1]).then_inc(x2_out, 1)

        N_CONST = 10 * 16

        @block.gpsimd
        def _(pool):
            for n, (w, parts) in enumerate(((w3blk, t.w3), (w0blk, t.w0), (wfblk, t.wf))):
                pool.wait_ge(weights_hi, n + 1)
                pool.tensor_tensor(parts[1][:, :, :], w[:, :, :], parts[0][:, :, :], ALU.subtract)\
                    .then_inc(weights_lo, 1)
            pool.wait_ge(weights_lo, 3)

        @block.tensor
        def _(pe):
            pe.wait_ge(chain, C_EX)
            pe.matmul(pg[:, :], grp[:, :], EX[:, :, :].rearrange("p a b -> p (a b)"), start=True, stop=True)\
                .then_inc(group_done, 1)
            pe.wait_ge(chain, C_V)
            for k in range(9):
                last = pe.matmul(pm[:, :], taps[:, k, :], V[:, k, :], start=(k == 0), stop=(k == 8))
            last.then_inc(mean_done, 1)
            pe.wait_ge(xm_done, 1)
            pe.matmul(px[:, :], band[:, :], XM[:, :], start=True, stop=True).then_inc(x2_done, 1)
            pe.wait_ge(x2_out, 2)
            pe.wait_ge(weights_in, 48)
            for k in range(9):
                last = pe.matmul(p3[:, k * B:(k + 1) * B], w3blk[:, k, :], X2[:, :], start=True, stop=True)
            last.then_inc(b3_done, 1)

        @block.vector
        def _(dve):
            done = [0]

            def step(ins):
                done[0] += 1
                ins.then_inc(chain, 1)
                dve.wait_ge(chain, done[0])

            def also(ins):
                done[0] += 1
                ins.then_inc(chain, 1)

            with dve.Fori(0, B) as b:
                for q in range(NCH):
                    dve.wait_ge(chunk_in[q], 32 * b + 32)
                    for j in range(4):
                        at = (4 * q + j) * 6
                        dve.bn_stats(BS[:, bass.ds(b, 1), at:at + 6], XC[:, q, 512 * j:512 * j + 512])
                    dve.tensor_reduce(EC[:, bass.ds(b, 1), q, :],
                                      XC[:, q, :].rearrange("p (r w) -> p w r", w=W)[:, 0:W:W - 1, :],
                                      AX, ALU.add).then_inc(chunk_used, 1)
            dve.wait_ge(chunk_used, NCH * B)
            for b in range(B):
                also(dve.bn_aggr(MV[:, b, :], BS[:, b, :]))
            dve.wait_ge(const_in, N_CONST)
            step(dve.tensor_reduce(RX[:, 1, :], ER[:, :, :], AX, ALU.add))
            mean, var = MV[:, :, 0], MV[:, :, 1]
            step(dve.tensor_copy(EX[:, 0, :], mean))
            step(dve.tensor_tensor(EX[:, 1, :], mean, mean, ALU.mult))
            step(dve.tensor_tensor(EX[:, 1, :], EX[:, 1, :], var, ALU.add))
            assert done[0] == C_EX
            dve.wait_ge(group_done, 1)
            step(dve.tensor_copy(M[:, :, :].rearrange("p a b -> p (a b)"), pg[:, :]))
            step(dve.tensor_tensor(VAR[:, :], M[:, 0, :], M[:, 0, :], ALU.mult))
            step(dve.tensor_tensor(VAR[:, :], M[:, 1, :], VAR[:, :], ALU.subtract))
            step(dve.tensor_scalar(VAR[:, :], VAR[:, :], EPS, None, ALU.add))
            assert done[0] == C_VAR
            dve.wait_ge(std_done, 1)
            scale, shift = t.gn0[:, 0, :], t.gn0[:, 1, :]
            step(dve.reciprocal(scale, STD[:, :]))
            step(dve.tensor_tensor(STD[:, :], scale, scale, ALU.mult))
            step(dve.tensor_tensor(STD[:, :], STD[:, :], VAR[:, :], ALU.mult))
            step(dve.tensor_scalar(STD[:, :], STD[:, :], -0.5, 1.5, ALU.mult, ALU.add))
            step(dve.tensor_tensor(scale, scale, STD[:, :], ALU.mult))
            step(dve.scalar_tensor_tensor(shift, M[:, 0, :], -1.0, scale, ALU.mult, ALU.mult))
            step(dve.tensor_scalar(t.gn0[:, 2, :], scale, 1.0, None, ALU.add))
            step(dve.tensor_scalar(t.gn0[:, 3, :], shift, b12[:, 1:2], None, ALU.add))
            step(dve.tensor_reduce(ECS[:, :, :], EC[:, :, :, :].rearrange("p b q e -> p b e q"), AX, ALU.add))
            step(dve.tensor_scalar(D[:, 1, :], mean, float(ROWS * W), None, ALU.mult))
            step(dve.tensor_tensor(D[:, 0, :], D[:, 1, :], ECS[:, :, 1], ALU.subtract))
            step(dve.tensor_tensor(D[:, 2, :], D[:, 1, :], ECS[:, :, 0], ALU.subtract))
            step(dve.tensor_tensor(RX[:, 0, :], RX[:, 1, :], ER[:, :, W - 1], ALU.subtract))
            step(dve.tensor_tensor(RX[:, 2, :], RX[:, 1, :], ER[:, :, 0], ALU.subtract))
            step(dve.tensor_copy(V2[:, 3:6, :], D[:, :, :]))
            step(dve.scalar_tensor_tensor(V2[:, 0:3, :], RX[:, :, :], half[:, 1:2], D[:, :, :], ALU.mult, ALU.add))
            step(dve.scalar_tensor_tensor(V2[:, 6:9, :], RX[:, :, :], half[:, 0:1], D[:, :, :], ALU.mult, ALU.add))
            for k in range(9):
                also(dve.tensor_tensor(V[:, k, :], V2[:, k, :], scale, ALU.mult))
            dve.wait_ge(chain, done[0])
            for k in range(9):
                also(dve.scalar_tensor_tensor(V[:, k, :], shift, cnt[:, k:k + 1], V[:, k, :], ALU.mult, ALU.add))
            dve.wait_ge(chain, done[0])
            assert done[0] == C_V
            dve.wait_ge(b3_done, 1)
            for k in range(9):
                dve.tensor_scalar(t.b3p[:, :, k], p3[:, k * B:(k + 1) * B], b3[:, k:k + 1], None, ALU.add)\
                    .then_inc(chain, 1)
            dve.wait_ge(chain, done[0] + 9)


class Tile:

    def __init__(self, pair, offset, per_sample):
        self.n = 2 * pair + offset if offset else 2 * pair
        self.half = pair + offset // 2 if offset // 2 else pair
        self.s = offset % 2
        self.i = self.n % per_sample
        self.b = self.n // per_sample


def pipeline(eng, tiles, per_sample, offsets, body):
    lo, hi = -min(offsets.values()) + 2, tiles - max(offsets.values())
    hi -= (hi - lo) % 2

    def straight(g):
        body({k: Tile((g + o) // 2, (g + o) % 2, per_sample) if 0 <= g + o < tiles else None
              for k, o in offsets.items()})

    for g in range(-max(offsets.values()), lo):
        straight(g)
    with eng.Fori(0, (hi - lo) // 2) as n:
        for u in range(2):
            body({k: Tile(n, lo + u + o, per_sample) for k, o in offsets.items()})
    for g in range(hi, tiles - min(offsets.values())):
        straight(g)


def wait(eng, sem, value):
    if not isinstance(value, int) or value > 0:
        eng.wait_ge(sem, value)


def layer0_convolutions(nc, t):
    F32 = mybir.dt.float32
    F32R = mybir.dt.float32r
    ALU = mybir.AluOpType
    ACT = mybir.ActivationFunctionType
    SL = 4
    PER = H // 2 // SL
    TILES = B * PER
    WP = W + 2
    TAPS = 9
    RING = 8
    LO = slice(0, C)
    UP = slice(C, P)
    with ExitStack() as ctx:
        def sb(name, shape, dt=F32):
            return ctx.enter_context(nc.sbuf_tensor(name, shape, dt))

        def sem(name):
            return ctx.enter_context(nc.semaphore(name))

        XT = sb("c_x", [P, 2, SL + 1, WP])
        XH = sb("c_xh", [P, 2, SL + 1, WP], F32R)
        XL = sb("c_xl", [P, 2, SL + 1, WP], F32R)
        X0E = sb("c_x0e", [P, RING * SL, WP])
        X0O = sb("c_x0o", [P, H // 2 + 1, WP])
        Y = sb("c_y", [P, 2, SL * W])
        YH = sb("c_yh", [P, 2, SL * W], F32R)
        YL = sb("c_yl", [P, 2, SL * W], F32R)
        PR = sb("c_pr", [P, 8, SL * W])
        PL = sb("c_pl", [P, 2, SL * W])
        AC = sb("c_ac", [P, 2, SL * W])
        TE = sb("c_te", [P, 2, SL * W])
        TO = sb("c_to", [P, H // 2 + 1, WP])
        TH = sb("c_th", [P, 2, SL + 1, WP], F32R)
        TL = sb("c_tl", [P, 2, SL + 1, WP], F32R)
        XR = sb("c_xr", [P, 2, SL * W])
        OUT = sb("c_out", [P, 2, SL * W])
        mask = sb("c_mask", [P, PER])
        b0 = sb("c_b0", [P, 1])
        w1 = sb("c_w1", [P, TAPS])
        p0 = [ctx.enter_context(nc.psum_tensor(f"c_p0{s}", [P, SL * W], F32)) for s in range(2)]
        p3 = [ctx.enter_context(nc.psum_tensor(f"c_p3{s}", [P, SL * W], F32)) for s in range(3)]
        pf = [ctx.enter_context(nc.psum_tensor(f"c_pf{s}", [P, SL * W], F32)) for s in range(2)]

        const_in = sem("c_const_in")
        cleared = sem("c_cleared")
        xt_in = [sem(f"c_xt_in{s}") for s in range(2)]
        xr_in = [sem(f"c_xr_in{s}") for s in range(2)]
        xn_done = sem("c_xn_done")
        xh_done = sem("c_xh_done")
        xl_done = sem("c_xl_done")
        w0_done = sem("c_w0_done")
        x0_out = sem("c_x0_out")
        x0_odd = [sem(f"c_x0_odd{s}") for s in range(2)]
        dw_done = sem("c_dw_done")
        yh_done = sem("c_yh_done")
        y0_done = sem("c_y0_done")
        yl_done = [sem(f"c_yl_done{s}") for s in range(2)]
        w3_done = sem("c_w3_done")
        mult_done = sem("c_mult_done")
        add_done = sem("c_add_done")
        lrelu_done = sem("c_lrelu_done")
        t_odd = [sem(f"c_t_odd{s}") for s in range(2)]
        th_done = sem("c_th_done")
        tl_done = sem("c_tl_done")
        wf_done = sem("c_wf_done")
        res_done = sem("c_res_done")
        fin_done = sem("c_fin_done")
        stored = [sem(f"c_stored{s}") for s in range(2)]

        block = ctx.enter_context(nc.Block())
        odd_rows = t.x_rows.rearrange("b c (r e) w -> e b c r w", e=2)
        even_rows = t.x.rearrange("b c (r e) w -> e b c r w", e=2)
        out_rows = t.x1.rearrange("b c (r e) w -> e b c r w", e=2)

        def at(tile, pairs=SL, off=0):
            return bass.ds(tile.i * SL + off, pairs)

        def in_ring(tile):
            return bass.ds(tile.n % RING * SL, SL)

        def rows(ap):
            return ap.rearrange("p (r w) -> p r w", w=W)

        @block.sync
        def _(sp):
            for dst, src in ((mask[:, :], t.mask), (b0[:, :], t.b0), (w1[:, :], t.w1)):
                sp.dma_start(dst, src).then_inc(const_in, 16)
            sp.wait_ge(cleared, 1)

            def body(at_stage):
                if x0 := at_stage["x0"]:
                    sp.wait_ge(x0_out, x0.n + 1)
                    wait(sp, x0_odd[x0.s], 32 * x0.half)
                    sp.dma_start(X0O[UP, at(x0), :], X0E[LO, in_ring(x0), :]).then_inc(x0_odd[x0.s], 16)
                    sp.dma_start(X0O[LO, at(x0, off=1), :], X0E[UP, in_ring(x0), :]).then_inc(x0_odd[x0.s], 16)
                if l := at_stage["lrelu"]:
                    sp.wait_ge(lrelu_done, l.n + 1)
                    sp.dma_start(TO[UP, at(l), 1:W + 1], rows(TE[LO, l.s, :])).then_inc(t_odd[l.s], 16)
                    sp.dma_start(TO[LO, at(l, off=1), 1:W + 1], rows(TE[UP, l.s, :])).then_inc(t_odd[l.s], 16)
                if f := at_stage["fin"]:
                    sp.wait_ge(fin_done, f.n + 1)
                    for e, half in enumerate((LO, UP)):
                        sp.dma_start(out_rows[e, f.b, :, bass.ds(f.i * SL, SL), :], rows(OUT[half, f.s, :]))\
                            .then_inc(stored[f.s], 16)
                if r := at_stage["xr"]:
                    wait(sp, fin_done, r.n - 1)
                    for e, half in enumerate((LO, UP)):
                        sp.dma_start(rows(XR[half, r.s, :]), even_rows[e, r.b, :, bass.ds(r.i * SL, SL), :])\
                            .then_inc(xr_in[r.s], 16)
                if x := at_stage["xt"]:
                    wait(sp, xl_done, x.n - 1)
                    for e, half in enumerate((LO, UP)):
                        sp.dma_start(XT[half, x.s, :, 1:W + 1],
                                     odd_rows[e, x.b, :, bass.ds(x.i * SL, SL + 1), :]).then_inc(xt_in[x.s], 16)

            pipeline(sp, TILES, PER, {"xt": 7, "x0": 4, "lrelu": -1, "xr": -3, "fin": -5}, body)
            for s in range(2):
                sp.wait_ge(stored[s], 32 * TILES // 2)

        @block.gpsimd
        def _(pool):
            def add(m, k):
                pool.wait_ge(mult_done, 9 * m.n + (2 * k + 2))
                if k > 1:
                    pool.wait_ge(add_done, 5 * m.n + (k - 1))
                pool.tensor_tensor(PR[:, 2 * k:2 * k + 2, :], PR[:, 2 * k - 2:2 * k, :], PR[:, 2 * k:2 * k + 2, :],
                                   ALU.add).then_inc(add_done, 1)

            def finish(m):
                pool.wait_ge(add_done, 5 * m.n + 3)
                wait(pool, lrelu_done, m.n - 1)
                pool.tensor_tensor(AC[:, m.s, :], PR[:, 6, :], PR[:, 7, :], ALU.add).then_inc(add_done, 1)

            def last_tap(m):
                pool.wait_ge(mult_done, 9 * m.n + 9)
                pool.wait_ge(add_done, 5 * m.n + 4)
                pool.tensor_tensor(AC[:, m.s, :], AC[:, m.s, :], PL[:, m.s, :], ALU.add).then_inc(add_done, 1)

            def body(at_stage):
                m, before = at_stage["main"], at_stage["sum"]
                if before:
                    finish(before)
                    last_tap(before)
                if ts := at_stage["tsplit"]:
                    pool.wait_ge(th_done, ts.n + 1)
                    wait(pool, wf_done, ts.n - 1)
                    pool.tensor_tensor(TL[:, ts.s, :, :], TO[:, at(ts, SL + 1), :], TH[:, ts.s, :, :],
                                       ALU.subtract).then_inc(tl_done, 1)
                if x := at_stage["norm"]:
                    pool.wait_ge(xh_done, x.n + 1)
                    pool.tensor_tensor(XL[:, x.s, :, :], XT[:, x.s, :, :], XH[:, x.s, :, :],
                                       ALU.subtract).then_inc(xl_done, 1)
                if m:
                    add(m, 1)
                if (y := at_stage["ysplit"]) and y.s == 0:
                    pool.wait_ge(yh_done, y.n + 1)
                    pool.tensor_tensor(YL[:, y.s, :], Y[:, y.s, :], YH[:, y.s, :], ALU.subtract)\
                        .then_inc(yl_done[0], 1)
                if m:
                    add(m, 2)
                    add(m, 3)

            pipeline(pool, TILES, PER, {"norm": 6, "ysplit": 1, "main": 0, "sum": -1, "tsplit": -3}, body)

        @block.scalar
        def _(act):
            act.wait_ge(const_in, 48)
            act.wait_ge(cleared, 1)

            def body(at_stage):
                if d := at_stage["dw"]:
                    act.wait_ge(x0_odd[d.s], 32 * d.half + 32)
                    wait(act, yl_done[d.s], d.half)
                    act.activation(rows(Y[:, d.s, :]), X0O[:, at(d), 0:W], ACT.Copy, scale=w1[:, 0:1])\
                        .then_inc(y0_done, 1)
                if ts := at_stage["tsplit"]:
                    nxt = ts.half + (ts.s + 1) // 2
                    act.wait_ge(t_odd[ts.s], 32 * ts.half + 32)
                    if not (isinstance(ts.n, int) and ts.n == TILES - 1):
                        act.wait_ge(t_odd[1 - ts.s], 32 * nxt + 32)
                    wait(act, wf_done, ts.n - 1)
                    act.activation(TH[:, ts.s, :, :], TO[:, at(ts, SL + 1), :], ACT.Copy).then_inc(th_done, 1)
                if y := at_stage["ysplit"]:
                    act.wait_ge(dw_done, 8 * y.n + 8)
                    wait(act, w3_done, 9 * y.n - 9)
                    act.activation(YH[:, y.s, :], Y[:, y.s, :], ACT.Copy).then_inc(yh_done, 1)
                if x0 := at_stage["x0"]:
                    act.wait_ge(w0_done, x0.n + 1)
                    act.activation(X0E[:, in_ring(x0), 1:W + 1], rows(p0[x0.s][:, :]), ACT.Identity,
                                   bias=b0[:, :]).then_inc(x0_out, 1)
                if x := at_stage["norm"]:
                    act.wait_ge(xt_in[x.s], 32 * x.half + 32)
                    act.activation(XT[:, x.s, :, 1:W + 1], XT[:, x.s, :, 1:W + 1], ACT.Identity,
                                   scale=t.gn0[:, 0, bass.ds(x.b, 1)], bias=t.gn0[:, 1, bass.ds(x.b, 1)])\
                        .then_inc(xn_done, 1)
                    act.wait_ge(xn_done, 3 * x.n + 1)
                    act.activation(XT[LO, x.s, 0, :], XT[LO, x.s, 0, :], ACT.Copy,
                                   scale=mask[LO, bass.ds(x.i, 1)]).then_inc(xn_done, 1)
                    act.activation(XT[UP, x.s, SL, :], XT[UP, x.s, SL, :], ACT.Copy,
                                   scale=mask[UP, bass.ds(x.i, 1)]).then_inc(xn_done, 1)
                    act.wait_ge(xn_done, 3 * x.n + 3)
                    wait(act, w0_done, x.n - 1)
                    act.activation(XH[:, x.s, :, :], XT[:, x.s, :, :], ACT.Copy).then_inc(xh_done, 1)
                if f := at_stage["res"]:
                    act.wait_ge(xr_in[f.s], 32 * f.half + 32)
                    act.activation(XR[:, f.s, :], XR[:, f.s, :], ACT.Identity,
                                   scale=t.gn0[:, 2, bass.ds(f.b, 1)], bias=t.gn0[:, 3, bass.ds(f.b, 1)])\
                        .then_inc(res_done, 1)

            pipeline(act, TILES, PER, {"norm": 6, "x0": 4, "dw": 2, "ysplit": 1, "tsplit": -3, "res": -4}, body)

        @block.tensor
        def _(pe):
            w3h, w3l = t.w3

            def conv(psum, wh, wl, xh, xl, s):
                todo = []
                for n in range(6):
                    d, dx = divmod(n, 3)
                    for w, x in ((wh, xh), (wh, xl), (wl, xh)):
                        todo.append((psum[s], w[:, n, :], x[:, s, d:d + SL, dx:dx + W]))
                return todo

            def body(at_stage):
                jobs = []
                if a := at_stage["w0"]:
                    pe.wait_ge(xh_done, a.n + 1)
                    pe.wait_ge(xl_done, a.n + 1)
                    wait(pe, x0_out, a.n - 1)
                    jobs.append((conv(p0, *t.w0, XH, XL, a.s), w0_done))
                if f := at_stage["wf"]:
                    pe.wait_ge(th_done, f.n + 1)
                    pe.wait_ge(tl_done, f.n + 1)
                    wait(pe, fin_done, f.n - 1)
                    jobs.append((conv(pf, *t.wf, TH, TL, f.s), wf_done))
                others = [(o, w, x, n == 0, n == len(job) - 1, s) for job, s in jobs for n, (o, w, x) in enumerate(job)]
                m = at_stage["main"]

                def some(n):
                    for o, w, x, first, final, s in others[:n]:
                        ins = pe.matmul(o[:, :], w, x, start=first, stop=final)
                        if final:
                            ins.then_inc(s, 1)
                    del others[:n]

                if m:
                    pe.wait_ge(yh_done, m.n + 1)
                    pe.wait_ge(yl_done[m.s], m.half + 1)
                    for k in range(TAPS):
                        wait(pe, mult_done, 9 * m.n + (k - 2))
                        for n, (w, y) in enumerate(((w3h, YH), (w3h, YL), (w3l, YH))):
                            last = pe.matmul(p3[k % 3][:, :], w[:, k, :], y[:, m.s, :], start=(n == 0), stop=(n == 2))
                        last.then_inc(w3_done, 1)
                        some(4)
                some(len(others))

            pipeline(pe, TILES, PER, {"w0": 5, "main": 0, "wf": -4}, body)

        @block.vector
        def _(dve):
            for s in range(2):
                dve.memset(XT[:, s, :, 0:WP:W + 1], 0.0)
            dve.memset(X0E[:, :, 0:WP:W + 1], 0.0)
            for buf in (X0O, TO):
                dve.memset(buf[:, :, 0:WP:W + 1], 0.0)
                dve.memset(buf[LO, 0, 1:W + 1], 0.0)
                last = dve.memset(buf[UP, H // 2, 1:W + 1], 0.0)
            last.then_inc(cleared, 1)
            dve.wait_ge(const_in, 48)

            def shifted(tile, k):
                dy, dx = divmod(k, 3)
                if dy == 1:
                    return X0E[:, in_ring(tile), dx:dx + W]
                return X0O[:, at(tile, off=dy // 2), dx:dx + W]

            def body(at_stage):
                m, d = at_stage["main"], at_stage["dw"]
                if d:
                    nxt = d.half + (d.s + 1) // 2
                    dve.wait_ge(x0_odd[d.s], 32 * d.half + 32)
                    if not (isinstance(d.n, int) and d.n == TILES - 1):
                        dve.wait_ge(x0_odd[1 - d.s], 32 * nxt + 32)
                for k in range(TAPS):
                    if m:
                        dve.wait_ge(w3_done, 9 * m.n + (k + 1))
                        wait(dve, add_done, 5 * m.n - 5 + (k // 2 + 1 if k < 8 else 0))
                        dve.scalar_tensor_tensor(rows(PR[:, k, :] if k < 8 else PL[:, m.s, :]), rows(p3[k % 3][:, :]),
                                                 t.b3p[:, bass.ds(m.b, 1), k], shifted(m, k),
                                                 ALU.add, ALU.mult).then_inc(mult_done, 1)
                    if d and k > 0:
                        y = rows(Y[:, d.s, :])
                        if k == 1:
                            dve.wait_ge(y0_done, d.n + 1)
                        else:
                            dve.wait_ge(dw_done, 8 * d.n + (k - 1))
                        dve.scalar_tensor_tensor(y, shifted(d, k), w1[:, k:k + 1], y, ALU.mult, ALU.add)\
                            .then_inc(dw_done, 1)
                    if k == 3 and (y := at_stage["ysplit"]) and y.s == 1:
                        dve.wait_ge(yh_done, y.n + 1)
                        dve.tensor_tensor(YL[:, y.s, :], Y[:, y.s, :], YH[:, y.s, :], ALU.subtract)\
                            .then_inc(yl_done[1], 1)
                    if k == 4 and (l := at_stage["lrelu"]):
                        dve.wait_ge(add_done, 5 * l.n + 5)
                        wait(dve, t_odd[l.s], 32 * l.half)
                        dve.scalar_tensor_tensor(TE[:, l.s, :], AC[:, l.s, :], 0.2, AC[:, l.s, :],
                                                 ALU.mult, ALU.max).then_inc(lrelu_done, 1)
                    if k == 1 and (f := at_stage["fin"]):
                        dve.wait_ge(wf_done, f.n + 1)
                        dve.wait_ge(res_done, f.n + 1)
                        wait(dve, stored[f.s], 32 * f.half)
                        dve.tensor_tensor(OUT[:, f.s, :], pf[f.s][:, :], XR[:, f.s, :], ALU.add).then_inc(fin_done, 1)

            pipeline(dve, TILES, PER, {"dw": 2, "ysplit": 1, "main": 0, "lrelu": -1, "fin": -5}, body)


CT = 4
TILES_C = C // CT
MODES = F // 2 * F


def of_sample(tensor, b):
    if isinstance(b, int):
        return tensor[:, b]
    ap = tensor[:, bass.ds(b, 1)]
    return ap.rearrange("p o a c -> p (o a) c") if len(ap.shape) == 4 else ap.rearrange("p o a -> p (o a)")


class Chain:

    def __init__(self, eng, sem, length, turn):
        self.eng, self.sem, self.base, self.n, self.length = eng, sem, turn * length, 0, length

    def __call__(self, ins):
        self.n += 1
        ins.then_inc(self.sem, 1)
        self.eng.wait_ge(self.sem, self.base + self.n)


CHAIN = 12
CHAIN_SUMS, CHAIN_VAR = 3, 7


def group_scale_steps(dve, step, s, sums_done, sums, std_done, std, turn):
    ALU = mybir.AluOpType
    bn = s.bn[:, :, :].rearrange("p g (e k) -> p (g e) k", k=3)
    mean, m2 = bn[:, :, 1], bn[:, :, 2]
    step(dve.tensor_copy(s.sums[:, 0, :], mean))
    step(dve.tensor_tensor(s.sq[:, :], mean, mean, ALU.mult))
    step(dve.scalar_tensor_tensor(s.sums[:, 1, :], m2, 1.0 / W, s.sq[:, :], ALU.mult, ALU.add))
    dve.wait_ge(sums_done, turn + 1)
    step(dve.tensor_reduce(s.ms[:, :], sums[:, :].rearrange("p (g e) -> p g e", e=2), mybir.AxisListType.X, ALU.add))
    m, e2 = s.ms[:, 0:G], s.ms[:, G:2 * G]
    step(dve.tensor_tensor(s.var[:, :], m, m, ALU.mult))
    step(dve.tensor_tensor(s.var[:, :], e2, s.var[:, :], ALU.subtract))
    step(dve.tensor_scalar(s.var[:, :], s.var[:, :], EPS, None, ALU.add))
    dve.wait_ge(std_done, turn + 1)
    step(dve.reciprocal(s.r[:, :], std[:, :]))
    step(dve.tensor_tensor(s.t[:, :], s.r[:, :], s.r[:, :], ALU.mult))
    step(dve.tensor_tensor(s.t[:, :], s.t[:, :], s.var[:, :], ALU.mult))
    step(dve.tensor_scalar(s.t[:, :], s.t[:, :], -0.5, 1.5, ALU.mult, ALU.add))
    step(dve.tensor_tensor(s.r[:, :], s.r[:, :], s.t[:, :], ALU.mult))


class GroupScaleBuffers:
    def __init__(self, sb, name):
        F32 = mybir.dt.float32
        self.bn = sb(name + "_bn", [P, G, 6], F32)
        self.sums = sb(name + "_sums", [P, 2, 2 * G], F32)
        self.sq = sb(name + "_sq", [P, 2 * G], F32)
        self.ms = sb(name + "_ms", [P, 2 * G], F32)
        self.var = sb(name + "_var", [P, G], F32)
        self.std = sb(name + "_std", [P, G], F32)
        self.r = sb(name + "_r", [P, G], F32)
        self.t = sb(name + "_t", [P, G], F32)


def forward_rows(pe, psum, x, basis, q):
    for c in range(CT):
        last = pe.matmul(psum[:, c * P:(c + 1) * P], x[:, CT * q + c, :], basis[:, :], start=True, stop=True)
    return last


def forward_columns(pe, psum, T, basis, us=range(F)):
    for u in us:
        half, u1 = divmod(u, F // 2)
        for k in range(4):
            last = pe.matmul(psum[C * half:C * half + C, u1 * F:(u1 + 1) * F], T[:, k * F + u, :],
                             basis[:, k, :], start=(k == 0), stop=(k == 3))
    return last


def tile_of_T(T, psum, q):
    return (T[:, :, CT * q:CT * q + CT],
            psum[:, :].rearrange("p (c k) -> p k c", c=CT))


class Mixing:

    QM = 128
    CHUNKS = MODES // QM
    EIGHT = 8

    def __init__(self, nc, ctx, sb, sem, name, hd, wt, out, banks):
        self.hd, self.wt, self.out, self.banks = hd, wt, out, banks
        self.w_in = [sem(f"{name}_w_in{s}") for s in range(2)]
        self.old_in = [sem(f"{name}_old_in{s}") for s in range(2)]
        self.hd_done = sem(f"{name}_hd_done")
        self.pe_done = sem(f"{name}_pe_done")
        self.out_done = sem(f"{name}_out_done")
        self.stored = [sem(f"{name}_stored{s}") for s in range(2)]

    def load(self, sp, weights, q):
        s = q % 2
        if q >= 2:
            sp.wait_ge(self.pe_done, 16 * (q - 1))
        for half in range(2):
            x = F // 2 * half + 4 * q
            sp.dma_start(self.wt[s][C * half:C * half + C, :, :],
                         weights[:, :, x:x + 4, :].rearrange("i o x y -> i o (x y)")).then_inc(self.w_in[s], 16)

    def load_old(self, sp, old, q):
        s = q % 2
        if q >= 2:
            sp.wait_ge(self.stored[s], 16)
        sp.dma_start(self.out[s], old[:, q * self.QM:(q + 1) * self.QM, :].rearrange("p m o -> p (m o)"))\
            .then_inc(self.old_in[s], 16)

    def store(self, sp, new, q):
        s = q % 2
        sp.wait_ge(self.out_done, 16 * q + 16)
        sp.dma_start(new[:, q * self.QM:(q + 1) * self.QM, :].rearrange("p m o -> p (m o)"), self.out[s])\
            .then_inc(self.stored[s], 16)

    def spread(self, dve, H, q):
        s = q % 2
        if q >= 2:
            dve.wait_ge(self.pe_done, 16 * (q - 1))
        for half in range(2):
            last = dve.tensor_copy(
                self.hd[C * half:C * half + C, s, :, B * half:B * half + B],
                H[C * half:C * half + C, :, q * self.QM:(q + 1) * self.QM].rearrange("p b m -> p m b"))
        last.then_inc(self.hd_done, 1)

    def multiply(self, pe, q):
        s = q % 2
        pe.wait_ge(self.w_in[s], 32 * (q // 2) + 32)
        pe.wait_ge(self.hd_done, q + 1)
        for n in range(self.QM // self.EIGHT):
            at = 16 * q + n
            if at >= len(self.banks):
                pe.wait_ge(self.out_done, at - len(self.banks) + 1)
            bank = self.banks[at % len(self.banks)]
            for j in range(self.EIGHT):
                m = n * self.EIGHT + j
                last = pe.matmul(bank[0:2 * B, C * j:C * j + C], self.hd[:, s, m, :], self.wt[s][:, :, m],
                                 start=True, stop=True)
            last.then_inc(self.pe_done, 1)

    def take(self, dve, q, add):
        s = q % 2
        if add:
            dve.wait_ge(self.old_in[s], 16 * (q // 2) + 16)
        elif q >= 2:
            dve.wait_ge(self.stored[s], 16 * (q // 2))
        for n in range(16):
            at = 16 * q + n
            dve.wait_ge(self.pe_done, at + 1)
            bank = self.banks[at % len(self.banks)]
            dst = self.out[s][:, n * 512:(n + 1) * 512]
            if add:
                ins = dve.tensor_tensor(dst, dst, bank[0:2 * B, :], mybir.AluOpType.add)
            else:
                ins = dve.tensor_copy(dst, bank[0:2 * B, :])
            ins.then_inc(self.out_done, 1)


def layer1_analyse(nc, t):
    F32 = mybir.dt.float32
    ALU = mybir.AluOpType
    ACT = mybir.ActivationFunctionType
    with ExitStack() as ctx:
        def sb(name, shape, dt=F32):
            return ctx.enter_context(nc.sbuf_tensor(name, shape, dt))

        def sem(name):
            return ctx.enter_context(nc.semaphore(name))

        def pb(name):
            return ctx.enter_context(nc.psum_tensor(name, [P, 512], F32))

        X = sb("a_x", [P, 2, C, W])
        HM = sb("a_h", [P, B, MODES])
        WT = sb("a_w", [P, C, 128])
        T = [sb(f"a_t{s}", [P, P, C]) for s in range(2)]
        HD = sb("a_hd", [P, 2, 128, 2 * B])
        rows_basis = sb("a_rows", [P, P])
        cols_basis = sb("a_cols", [P, 4, F])
        ones_modes = sb("a_ones_modes", [P, MODES])
        shift_modes = sb("a_shift_modes", [P, 2, MODES])
        ones = sb("a_ones", [P, P])
        one = sb("a_one", [1, 1])
        st = GroupScaleBuffers(sb, "a_gs")
        SC = sb("a_sc", [P, 2, G])
        SCX = sb("a_scx", [1, 2, G, 2])
        SCP = sb("a_scp", [P, 2, 2])
        pT = [pb(f"a_pt{i}") for i in range(4)]
        pH = [pb(f"a_ph{s}") for s in range(2)]
        pS = ctx.enter_context(nc.psum_tensor("a_ps", [P, 4 * G], F32))
        pP = ctx.enter_context(nc.psum_tensor("a_pp", [P, 2], F32))

        const_in = sem("a_const_in")
        ones_set = sem("a_ones_set")
        cleared = sem("a_cleared")
        x_in = [[sem(f"a_x_in{s}{h}") for h in range(2)] for s in range(2)]
        bn_done = sem("a_bn_done")
        chain = sem("a_chain")
        sums_done = sem("a_sums_done")
        std_done = sem("a_std_done")
        scale_done = sem("a_scale_done")
        expanded = sem("a_expanded")
        turned = sem("a_turned")
        scp_done = sem("a_scp_done")
        shift_done = sem("a_shift_done")
        rows_done = sem("a_rows_done")
        t_out = sem("a_t_out")
        cols_done = sem("a_cols_done")
        h_out = sem("a_h_out")
        mix = Mixing(nc, ctx, sb, sem, "a_mix", HD,
                     [WT, T[1][:, :, :].rearrange("p a b -> p (a b)").rearrange("p (o m) -> p o m", o=C)],
                     [X[0:2 * B, s, :, :].rearrange("p c w -> p (c w)") for s in range(2)], pT)
        NT = TILES_C
        GROUP = 4
        SUMS_AT, STD_AT = 11, 13

        block = ctx.enter_context(nc.Block())
        x1 = t.x1.rearrange("b c h w -> b h c w")

        @block.sync
        def _(sp):
            def load(b, s):
                for c in range(0, C, 8):
                    sp.dma_start(X[:, s, c:c + 8, :], x1[b, :, c:c + 8, :]).then_inc(x_in[s][c // 32], 16)

            load(0, 0)
            load(1, 1)
            mix.load(sp, t.weights1, 0)
            with sp.Fori(1, B // 2) as bb:
                for s in range(2):
                    sp.wait_ge(rows_done, NT * (2 * bb + (s - 1)))
                    sp.wait_ge(bn_done, 2 * bb + (s - 1))
                    load(2 * bb + s, s)
            sp.wait_ge(cols_done, B)
            mix.load(sp, t.weights1, 1)
            for q in range(2, mix.CHUNKS):
                mix.load(sp, t.weights1, q)
                mix.store(sp, t.o_ht, q - 2)
            for q in range(mix.CHUNKS - 2, mix.CHUNKS):
                mix.store(sp, t.o_ht, q)
            for s in range(2):
                sp.wait_ge(mix.stored[s], 32)

        @block.scalar
        def _(act):
            def body(b, s):
                for q in range(NT):
                    act.wait_ge(rows_done, NT * b + (q + 1))
                    if q == 0 and not isinstance(b, int):
                        act.wait_ge(cols_done, b - 1)
                    dst, src = tile_of_T(T[s], pT[q % 4], q)
                    act.activation(dst, src, ACT.Copy).then_inc(t_out, 1)
                    if q == STD_AT:
                        act.wait_ge(chain, CHAIN * b + CHAIN_VAR)
                        act.activation(st.std[:, :], st.var[:, :], ACT.Sqrt).then_inc(std_done, 1)
                act.wait_ge(scp_done, b + 1)
                act.wait_ge(h_out, b + 1)
                act.activation(shift_modes[:, s, :], ones_modes[:, :], ACT.Copy, scale=SCP[:, s, 1:2])\
                    .then_inc(shift_done, 1)

            for dst, src in ((rows_basis[:, :], t.fwd_rows), (cols_basis[:, :, :], t.fwd_cols),
                             (ones_modes[:, :], t.ones_modes)):
                act.dma_start(dst, src).then_inc(const_in, 16)
            act.nop().then_inc(t_out, 4)
            act.wait_ge(const_in, 48)
            body(0, 0)
            body(1, 1)
            with act.Fori(1, B // 2) as bb:
                for s in range(2):
                    body(2 * bb + s, s)

        @block.tensor
        def _(pe):
            def columns(b, s, part):
                if part == 0:
                    pe.wait_ge(t_out, NT * b + (NT + 4))
                    pe.wait_ge(h_out, b + 1)
                size = F * GROUP // NT
                last = forward_columns(pe, pH[s], T[s], cols_basis, range(size * part, size * (part + 1)))
                if part == NT // GROUP - 1:
                    last.then_inc(cols_done, 1)

            def turn(b):
                pe.wait_ge(expanded, b + 1)
                for half in range(2):
                    for k in range(2):
                        last = pe.matmul(pP[C * half:C * half + C, k:k + 1],
                                         SCX[:, k, :, :].rearrange("p g e -> p (g e)"), one[:, :],
                                         start=True, stop=True)
                last.then_inc(turned, 1)

            def body(b, s, before):
                for q in range(NT):
                    if q % 8 == 0:
                        pe.wait_ge(x_in[s][q // 8], 64 * (b // 2) + 64)
                    if q == SUMS_AT:
                        pe.wait_ge(chain, CHAIN * b + CHAIN_SUMS)
                        pe.matmul(pS[:, :], ones[:, :], st.sums[:, :, :].rearrange("p a g -> p (a g)"), start=True,
                                  stop=True).then_inc(sums_done, 1)
                    pe.wait_ge(t_out, NT * b + (q + 1))
                    forward_rows(pe, pT[q % 4], X[:, s, :, :], rows_basis, q).then_inc(rows_done, 1)
                    if before is not None:
                        if q == 0:
                            turn(before)
                        if q % GROUP == GROUP - 1:
                            columns(before, 1 - s, q // GROUP)

            pe.wait_ge(const_in, 48)
            pe.wait_ge(ones_set, 1)
            body(0, 0, None)
            body(1, 1, 0)
            with pe.Fori(1, B // 2) as bb:
                for s in range(2):
                    body(2 * bb + s, s, 2 * bb + (s - 1))
            turn(B - 1)
            for part in range(NT // GROUP):
                columns(B - 1, (B - 1) % 2, part)
            pe.wait_ge(t_out, NT * B + 4)
            for q in range(mix.CHUNKS):
                mix.multiply(pe, q)

        @block.vector
        def _(dve):
            def modes(b, s):
                dve.wait_ge(cols_done, b + 1)
                dve.wait_ge(shift_done, b + 1)
                dve.scalar_tensor_tensor(of_sample(HM, b), pH[s][:, :], SCP[:, s, 0:1], shift_modes[:, s, :],
                                         ALU.mult, ALU.add).then_inc(h_out, 1)

            def body(b, s, before):
                for g in range(G):
                    if g % 16 == 0:
                        dve.wait_ge(x_in[s][g // 16], 64 * (b // 2) + 64)
                    last = dve.bn_stats(st.bn[:, g, :], X[:, s, 2 * g:2 * g + 2, :].rearrange("p c w -> p (c w)"))
                last.then_inc(bn_done, 1)
                if before is not None:
                    modes(before, s)
                dve.wait_ge(bn_done, b + 1)
                step = Chain(dve, chain, CHAIN, b)
                group_scale_steps(dve, step, st, sums_done, pS, std_done, st.std, b)
                scale, shift = SC[:, 0, :], SC[:, 1, :]
                dve.tensor_copy(scale, st.r[:, :]).then_inc(scale_done, 1)
                dve.scalar_tensor_tensor(shift, st.ms[:, 0:G], -1.0, st.r[:, :], ALU.mult, ALU.mult)\
                    .then_inc(scale_done, 1)
                dve.wait_ge(scale_done, 2 * b + 2)
                for e in range(2):
                    last = dve.tensor_copy(SCX[:, :, :, e], SC[0:1, :, :])
                last.then_inc(expanded, 1)
                dve.tensor_copy(of_sample(t.gn1, b), SC[:, :, :])
                dve.wait_ge(turned, b + 1)
                dve.tensor_copy(SCP[:, s, :], pP[:, :]).then_inc(scp_done, 1)
                dve.wait_ge(scp_done, b + 1)

            dve.memset(one[:, :], 1.0)
            dve.memset(ones[:, :], 1.0 / 256).then_inc(ones_set, 1)
            dve.memset(HD[:, :, :, :], 0.0).then_inc(cleared, 1)
            dve.wait_ge(cleared, 1)
            dve.nop().then_inc(h_out, 2)
            body(0, 0, None)
            body(1, 1, None)
            with dve.Fori(1, B // 2) as bb:
                for s in range(2):
                    body(2 * bb + s, s, 2 * bb + (s - 2))
            modes(B - 2, 0)
            modes(B - 1, 1)
            dve.wait_ge(h_out, B + 2)
            for q in range(2):
                mix.spread(dve, HM, q)
            for q in range(mix.CHUNKS):
                mix.take(dve, q, False)
                if q + 2 < mix.CHUNKS:
                    mix.spread(dve, HM, q + 2)


def inverse_columns(pe, psum, O, basis, q):
    for c in range(CT):
        last = pe.matmul(psum[:, c * W:(c + 1) * W], O[:, :, CT * q + c], basis[:, :], start=True, stop=True)
    return last


def inverse_rows(pe, psum, ZH, ZL, basis):
    pe.matmul(psum[:, :], basis[:, 0, :], ZH, start=True, stop=False)
    pe.matmul(psum[:, :], basis[:, 0, :], ZL, start=False, stop=False)
    return pe.matmul(psum[:, :], basis[:, 1, :], ZH, start=False, stop=True)


def load_diagonal(sp, O, o_ht, b, sem):
    src = o_ht.rearrange("(h b) (u v) o -> b h v u o", h=2, v=F)
    for k in range(4):
        for half in range(2):
            u = F * k + F // 2 * half
            sp.dma_start(O[F * k:F * k + F, u:u + F // 2, :], src[b, half, :, :, :]).then_inc(sem, 16)


def sample_steps(eng, body):
    body(0, 0, True, False)
    with eng.Fori(0, B // 2 - 1) as bb:
        for u in range(2):
            body(2 * bb + (1 + u), (1 + u) % 2, True, True)
    body(B - 1, (B - 1) % 2, True, True)
    body(B, B % 2, False, True)


def layer1_refine(nc, t):
    F32 = mybir.dt.float32
    F32R = mybir.dt.float32r
    ALU = mybir.AluOpType
    ACT = mybir.ActivationFunctionType
    ERR_TH = 0.1
    ZRING = 4
    DRING = 4
    with ExitStack() as ctx:
        def sb(name, shape, dt=F32):
            return ctx.enter_context(nc.sbuf_tensor(name, shape, dt))

        def sem(name):
            return ctx.enter_context(nc.semaphore(name))

        def pb(name):
            return ctx.enter_context(nc.psum_tensor(name, [P, 512], F32))

        X = sb("r_x", [P, 2, C, W])
        O = [sb(f"r_o{s}", [P, P, C]) for s in range(2)]
        T = sb("r_t", [P, P, C])
        HM = sb("r_h", [P, B, MODES])
        HD = T[:, 0:2 * 128 * 2 * B // C, :].rearrange("p a c -> p (a c)")\
            .rearrange("p (s m k) -> p s m k", s=2, k=2 * B)
        ZH = sb("r_zh", [P, ZRING, CT * W], F32R)
        ZL = sb("r_zl", [P, ZRING, CT * W], F32R)
        D = sb("r_d", [P, DRING, CT * W])
        SC = sb("r_sc", [P, 2, 2, G])
        rows_basis = sb("r_rows", [P, P])
        cols_basis = sb("r_cols", [P, 4, F])
        inv_cols = sb("r_icols", [P, W])
        inv_rows = sb("r_irows", [P, P])
        inv_parts = sb("r_iparts", [P, 2, P], F32R)
        pZ = [pb(f"r_pz{i}") for i in range(2)]
        pR = [pb(f"r_pr{i}") for i in range(2)]
        pT = [pb(f"r_pt{i}") for i in range(2)]
        pH = pb("r_ph")

        inv_in = sem("r_inv_in")
        fwd_in = sem("r_fwd_in")
        cleared = sem("r_cleared")
        pool_cleared = sem("r_pool_cleared")
        x_in = [[sem(f"r_x_in{s}{h}") for h in range(2)] for s in range(2)]
        o_in = [sem(f"r_o_in{s}") for s in range(2)]
        sc_ready = sem("r_sc_ready")
        norm_done = sem("r_norm_done")
        basis_split = sem("r_basis_split")
        icols_done = sem("r_icols_done")
        zh_out = sem("r_zh_out")
        zl_out = sem("r_zl_out")
        irows_done = sem("r_irows_done")
        diff_done = sem("r_diff_done")
        abs_done = sem("r_abs_done")
        masked = sem("r_masked")
        rows_done = sem("r_rows_done")
        t_out = sem("r_t_out")
        cols_done = sem("r_cols_done")
        h_out = sem("r_h_out")
        mix = Mixing(nc, ctx, sb, sem, "r_mix", HD,
                     [o[:, :, :].rearrange("p a b -> p (a b)").rearrange("p (o m) -> p o m", o=C) for o in O],
                     [X[0:2 * B, s, :, :].rearrange("p c w -> p (c w)") for s in range(2)], [*pT, *pR])
        NT = TILES_C

        block = ctx.enter_context(nc.Block())
        x1 = t.x1.rearrange("b c h w -> b h c w")

        INV, MASK, FWD, TO_T = 2, 3, 5, 6

        def tile_at(b, s, here, before, q, lag):
            n = q - lag
            if n >= 0:
                return (b, s, n) if here else None
            return (b - 1, 1 - s, n + NT) if before else None

        def flat(s, n):
            return X[:, s, CT * n:CT * n + CT, :].rearrange("p c w -> p (c w)")

        @block.sync
        def _(sp):
            def load(b, s):
                for c in range(0, C, 8):
                    sp.dma_start(X[:, s, c:c + 8, :], x1[b, :, c:c + 8, :]).then_inc(x_in[s][c // 32], 16)

            for dst, src in ((inv_cols[:, :], t.inv_cols), (inv_rows[:, :], t.inv_rows)):
                sp.dma_start(dst, src).then_inc(inv_in, 16)
            sp.wait_ge(cleared, 1)
            sp.wait_ge(pool_cleared, 1)
            load_diagonal(sp, O[0], t.o_ht, 0, o_in[0])
            load(0, 0)
            for dst, src in ((rows_basis[:, :], t.fwd_rows), (cols_basis[:, :, :], t.fwd_cols)):
                sp.dma_start(dst, src).then_inc(fwd_in, 16)
            load(1, 1)
            sp.wait_ge(pool_cleared, 2)
            load_diagonal(sp, O[1], t.o_ht, 1, o_in[1])

            def next_diagonal(b, s):
                sp.wait_ge(icols_done, NT * b + NT)
                load_diagonal(sp, O[s], t.o_ht, b + 2, o_in[s])

            def next_x(b, s):
                sp.wait_ge(rows_done, NT * b)
                load(b + 1, 1 - s)

            next_diagonal(0, 0)
            next_x(1, 1)
            next_diagonal(1, 1)
            with sp.Fori(1, B // 2 - 1) as bb:
                for s in range(2):
                    next_x(2 * bb + s, s)
                    next_diagonal(2 * bb + s, s)
            next_x(B - 2, 0)
            sp.wait_ge(icols_done, NT * (B - 1))
            mix.load(sp, t.refine1, 0)
            sp.wait_ge(icols_done, NT * B)
            mix.load(sp, t.refine1, 1)
            sp.wait_ge(rows_done, NT * B)
            mix.load_old(sp, t.o_ht, 0)
            mix.load_old(sp, t.o_ht, 1)
            for q in range(2, mix.CHUNKS):
                mix.load(sp, t.refine1, q)
                mix.store(sp, t.o_sum, q - 2)
                mix.load_old(sp, t.o_ht, q)
            for q in range(mix.CHUNKS - 2, mix.CHUNKS):
                mix.store(sp, t.o_sum, q)
            for s in range(2):
                sp.wait_ge(mix.stored[s], 32)

        @block.scalar
        def _(act):
            def body(b, s, here, before):
                if here:
                    act.wait_ge(sc_ready, b + 1)
                for q in range(NT if here else INV):
                    if here:
                        act.wait_ge(icols_done, NT * b + (q + 1))
                        wait(act, irows_done, NT * b + (q + 1 - ZRING))
                        act.activation(ZH[:, q % ZRING, :], pZ[q % 2][:, :], ACT.Copy).then_inc(zh_out, 1)
                        if q % 8 == 0:
                            act.wait_ge(x_in[s][q // 8], 64 * (b // 2) + 64)
                        for g in (2 * q, 2 * q + 1):
                            last = act.activation(X[:, s, 2 * g:2 * g + 2, :], X[:, s, 2 * g:2 * g + 2, :], ACT.Identity,
                                                  scale=SC[:, s, 0, g:g + 1], bias=SC[:, s, 1, g:g + 1])
                        last.then_inc(norm_done, 1)
                    if at := tile_at(b, s, here, before, q, INV):
                        b1, _, n = at
                        act.wait_ge(diff_done, NT * b1 + (n + 1))
                        act.activation(D[:, n % DRING, :], D[:, n % DRING, :], ACT.Abs).then_inc(abs_done, 1)

            act.wait_ge(inv_in, 32)
            act.activation(inv_parts[:, 0, :], inv_rows[:, :], ACT.Copy).then_inc(basis_split, 1)
            sample_steps(act, body)

        @block.gpsimd
        def _(pool):
            pool.memset(O[0][:, P // 2:P, :], 0.0).then_inc(pool_cleared, 1)
            pool.memset(O[1][:, :, :], 0.0).then_inc(pool_cleared, 1)

        @block.tensor
        def _(pe):
            def body(b, s, here, before):
                for q in range(NT if here else FWD + 1):
                    if here:
                        if q == 0:
                            pe.wait_ge(o_in[s], 128 * (b // 2) + 128)
                        wait(pe, zl_out, NT * b + (q - 1))
                        inverse_columns(pe, pZ[q % 2], O[s], inv_cols, q).then_inc(icols_done, 1)
                    if at := tile_at(b, s, here, before, q, INV):
                        b1, _, n = at
                        pe.wait_ge(zl_out, NT * b1 + (n + 1))
                        wait(pe, diff_done, NT * b1 + (n - 1))
                        inverse_rows(pe, pR[n % 2], ZH[:, n % ZRING, :], ZL[:, n % ZRING, :], inv_parts)\
                            .then_inc(irows_done, 1)
                    if q == FWD and before:
                        pe.wait_ge(t_out, NT * b)
                        wait(pe, h_out, b - 1)
                        forward_columns(pe, pH, T, cols_basis).then_inc(cols_done, 1)
                    if at := tile_at(b, s, here, before, q, FWD):
                        b1, s1, n = at
                        if q == FWD and not before:
                            pe.wait_ge(fwd_in, 32)
                        pe.wait_ge(masked, NT * b1 + (n + 1))
                        wait(pe, t_out, NT * b1 + (n - 1))
                        forward_rows(pe, pT[n % 2], X[:, s1, :, :], rows_basis, n).then_inc(rows_done, 1)

            pe.wait_ge(basis_split, 2)
            sample_steps(pe, body)
            for q in range(mix.CHUNKS):
                mix.multiply(pe, q)

        @block.vector
        def _(dve):
            def scales(b, s):
                dve.tensor_copy(SC[:, s, :, :], of_sample(t.gn1, b)).then_inc(sc_ready, 1)

            def body(b, s, here, before):
                for q in range(NT if here else TO_T + 1):
                    if here and q == NT // 2 and not (isinstance(b, int) and b == B - 1):
                        scales(b + 1, 1 - s)
                    if q == TO_T and before:
                        dve.wait_ge(cols_done, b)
                        dve.tensor_copy(of_sample(HM, b - 1), pH[:, :]).then_inc(h_out, 1)
                    if at := tile_at(b, s, here, before, q, TO_T):
                        b1, _, n = at
                        dve.wait_ge(rows_done, NT * b1 + (n + 1))
                        dst, src = tile_of_T(T, pT[n % 2], n)
                        dve.tensor_copy(dst, src).then_inc(t_out, 1)
                    if at := tile_at(b, s, here, before, q, INV):
                        b1, s1, n = at
                        dve.wait_ge(norm_done, NT * b1 + (n + 1))
                        dve.wait_ge(irows_done, NT * b1 + (n + 1))
                        wait(dve, masked, NT * b1 + (n + 1 - DRING))
                        dve.tensor_tensor(D[:, n % DRING, :], flat(s1, n), pR[n % 2][:, :], ALU.subtract)\
                            .then_inc(diff_done, 1)
                    if at := tile_at(b, s, here, before, q, MASK):
                        b1, s1, n = at
                        dve.wait_ge(abs_done, NT * b1 + (n + 1))
                        dve.scalar_tensor_tensor(flat(s1, n), D[:, n % DRING, :], ERR_TH, flat(s1, n),
                                                 ALU.is_gt, ALU.mult).then_inc(masked, 1)
                    if here:
                        dve.wait_ge(zh_out, NT * b + (q + 1))
                        dve.tensor_tensor(ZL[:, q % ZRING, :], pZ[q % 2][:, :], ZH[:, q % ZRING, :], ALU.subtract)\
                            .then_inc(zl_out, 1)

            dve.memset(O[0][:, 0:P // 2, :], 0.0).then_inc(cleared, 1)
            scales(0, 0)
            dve.wait_ge(basis_split, 1)
            dve.tensor_tensor(inv_parts[:, 1, :], inv_rows[:, :], inv_parts[:, 0, :], ALU.subtract)\
                .then_inc(basis_split, 1)
            sample_steps(dve, body)
            dve.memset(HD[:, :, :, :], 0.0).then_inc(cleared, 1)
            dve.wait_ge(cleared, 2)
            dve.wait_ge(h_out, B)
            for q in range(2):
                mix.spread(dve, HM, q)
            for q in range(mix.CHUNKS):
                mix.take(dve, q, True)
                if q + 2 < mix.CHUNKS:
                    mix.spread(dve, HM, q + 2)


def band_matrices(dve, bands, shifts, coefs, size, step):
    ALU = mybir.AluOpType
    for dx in range(size):
        for dy in range(size):
            diagonal, k = shifts[:, dy, :], coefs[:, dy * size + dx:dy * size + dx + 1]
            if dy == 0:
                step(dve.tensor_scalar(bands[:, dx, :], diagonal, k, None, ALU.mult))
            else:
                step(dve.scalar_tensor_tensor(bands[:, dx, :], diagonal, k, bands[:, dx, :], ALU.mult, ALU.add))


def layers2_and_3(nc, t):
    F32 = mybir.dt.float32
    F32R = mybir.dt.float32r
    ALU = mybir.AluOpType
    ACT = mybir.ActivationFunctionType
    S2, S3 = 3, 9
    PAD = S3 // 2
    NT = TILES_C
    HALF = NT // 2
    RING = 4
    with ExitStack() as ctx:
        def sb(name, shape, dt=F32):
            return ctx.enter_context(nc.sbuf_tensor(name, shape, dt))

        def sem(name):
            return ctx.enter_context(nc.semaphore(name))

        def pb(name):
            return ctx.enter_context(nc.psum_tensor(name, [P, 512], F32))

        X = sb("s_x", [P, 2, C, W])
        O = sb("s_o", [P, P, C])
        Z = sb("s_z", [P, 2, CT * W])
        ZH = sb("s_zh", [P, RING, CT * W], F32R)
        ZL = sb("s_zl", [P, RING, CT * W], F32R)
        GN = {n: sb(f"s_g{n}", [P, 2, CT, W + 2 * PAD]) for n in (2, 3)}
        GH = {n: sb(f"s_gh{n}", [P, RING, CT, W + 2 * PAD], F32R) for n in (2, 3)}
        GL = {n: sb(f"s_gl{n}", [P, RING, CT, W + 2 * PAD], F32R) for n in (2, 3)}
        BF = {2: sb("s_b2", [P, S2, P]), 3: sb("s_b3", [P, S3, P])}
        BH = {2: sb("s_bh2", [P, S2, P], F32R), 3: sb("s_bh3", [P, S3, P], F32R)}
        BL = {2: sb("s_bl2", [P, S2, P], F32R), 3: sb("s_bl3", [P, S3, P], F32R)}
        shifts = sb("s_shifts", [P, S2, P])
        alpha = sb("s_alpha", [P, 9])
        beta = sb("s_beta", [P, 1])
        stencils = sb("s_stencils", [P, 8, S2 * S2])
        K2 = sb("s_k2", [P, S2 * S2])
        small = sb("s_small", [P, 2])
        inv_cols = sb("s_icols", [P, W])
        inv_rows = sb("s_irows", [P, P])
        inv_parts = sb("s_iparts", [P, 2, P], F32R)
        ones = sb("s_ones", [P, P])
        ST = {n: GroupScaleBuffers(sb, f"s_gs{n}") for n in (2, 3)}
        SC = {n: sb(f"s_sc{n}", [P, 2, 2, G]) for n in (2, 3)}
        pZ = [pb(f"s_pz{i}") for i in range(2)]
        pA = [pb(f"s_pa{i}") for i in range(2)]
        pC = [pb(f"s_pc{i}") for i in range(3)]
        pS = ctx.enter_context(nc.psum_tensor("s_ps", [P, 4 * G], F32))

        bases_in = sem("s_bases_in")
        const_in = sem("s_const_in")
        cleared = sem("s_cleared")
        pool_cleared = sem("s_pool_cleared")
        built = sem("s_built")
        b_hi = sem("s_b_hi")
        b_lo = sem("s_b_lo")
        x_in = [[sem(f"s_x_in{s}{h}") for h in range(2)] for s in range(2)]
        o_in = sem("s_o_in")
        icols_done = sem("s_icols_done")
        basis_split = sem("s_basis_split")
        z_out = sem("s_z_out")
        zh_out = sem("s_zh_out")
        zl_out = sem("s_zl_out")
        irows_done = sem("s_irows_done")
        x_sum = {n: sem(f"s_x_sum{n}") for n in (2, 3)}
        bn_done = {n: sem(f"s_bn_done{n}") for n in (2, 3)}
        chain = {n: sem(f"s_chain{n}") for n in (2, 3)}
        sums_done = {n: sem(f"s_sums_done{n}") for n in (2, 3)}
        std_done = {n: sem(f"s_std_done{n}") for n in (2, 3)}
        scale_done = {n: sem(f"s_scale_done{n}") for n in (2, 3)}
        g_done = {n: sem(f"s_g_done{n}") for n in (2, 3)}
        gl_done = {n: sem(f"s_gl_done{n}") for n in (2, 3)}
        conv_done = {n: sem(f"s_conv_done{n}") for n in (2, 3)}
        out_done = sem("s_out_done")
        stored = [[sem(f"s_stored{s}{q}") for q in range(4)] for s in range(2)]

        block = ctx.enter_context(nc.Block())
        x1 = t.x1.rearrange("b c h w -> b h c w")
        out = t.out.rearrange("b c h w -> b h c w")
        BUILT = 12 + S2 * S2

        def tile_of(s, q):
            return X[:, s, CT * q:CT * q + CT, :].rearrange("p c w -> p (c w)")


        @block.sync
        def _(sp):
            for dst, src in ((inv_cols[:, :], t.inv_cols), (inv_rows[:, :], t.inv_rows)):
                sp.dma_start(dst, src).then_inc(bases_in, 16)
            sp.wait_ge(cleared, 1)
            sp.wait_ge(pool_cleared, 1)
            load_diagonal(sp, O, t.o_sum, 0, o_in)
            for dst, src in ((shifts[:, :, :], t.shifts), (alpha[:, :], t.alpha),
                             (beta[:, :], t.beta),
                             (stencils[:, :, :].rearrange("p a k -> p (a k)"), t.stencils),
                             (BF[3][:, :, :], t.band3)):
                sp.dma_start(dst, src).then_inc(const_in, 16)

            def load(b, s, q):
                for c in range(16 * q, 16 * q + 16, 8):
                    sp.dma_start(X[:, s, c:c + 8, :], x1[b, :, c:c + 8, :]).then_inc(x_in[s][q // 2], 16)

            for q in range(4):
                load(0, 0, q)

            def body(b, s, here, before):
                if here and not (isinstance(b, int) and b == B - 1):
                    sp.wait_ge(icols_done, NT * b + NT)
                    load_diagonal(sp, O, t.o_sum, b + 1, o_in)
                for q in range(4):
                    if before:
                        sp.wait_ge(out_done, NT * (b - 1) + (4 * q + 4))
                        for c in range(16 * q, 16 * q + 16, 8):
                            sp.dma_start(out[b - 1, :, c:c + 8, :], X[:, 1 - s, c:c + 8, :])\
                                .then_inc(stored[1 - s][q], 16)
                    if here and not (isinstance(b, int) and b == B - 1):
                        if before:
                            sp.wait_ge(stored[1 - s][q], 32 * ((b + 1) // 2))
                        load(b + 1, 1 - s, q)

            sample_steps(sp, body)
            for s in range(2):
                for q in range(4):
                    sp.wait_ge(stored[s][q], 32 * B // 2)

        def normalised_tiles(act, n, b, s, tiles):
            for q in tiles:
                g = 2 * q
                if q >= 2:
                    act.wait_ge(gl_done[n], NT * b + (q - 1))
                for i in range(2):
                    last = act.activation(GN[n][:, q % 2, 2 * i:2 * i + 2, PAD:PAD + W],
                                          X[:, s, CT * q + 2 * i:CT * q + 2 * i + 2, :], ACT.Identity,
                                          scale=SC[n][:, s, 0, g + i:g + i + 1], bias=SC[n][:, s, 1, g + i:g + i + 1])
                last.then_inc(g_done[n], 1)
                act.wait_ge(g_done[n], 2 * NT * b + (2 * q + 1))
                if q >= RING:
                    act.wait_ge(conv_done[n], NT * b + (q + 1 - RING))
                act.activation(GH[n][:, q % RING, :, :], GN[n][:, q % 2, :, :], ACT.Copy).then_inc(g_done[n], 1)

        @block.scalar
        def _(act):
            def std(n, b):
                act.wait_ge(chain[n], CHAIN * b + CHAIN_VAR)
                act.activation(ST[n].std[:, :], ST[n].var[:, :], ACT.Sqrt).then_inc(std_done[n], 1)

            def body(b, s, here, before):
                if here:
                    for q in range(NT):
                        tile = NT * b + (q + 1)
                        act.wait_ge(icols_done, tile)
                        if q >= 2:
                            act.wait_ge(zl_out, NT * b + (q - 1))
                        act.activation(Z[:, q % 2, :], pZ[q % 2][:, :], ACT.Copy).then_inc(z_out, 1)
                        act.wait_ge(z_out, tile)
                        act.activation(ZH[:, q % RING, :], Z[:, q % 2, :], ACT.Copy).then_inc(zh_out, 1)
                if not before:
                    act.wait_ge(built, BUILT)
                    act.wait_ge(const_in, 16 * 5)
                    for n in (2, 3):
                        act.activation(BH[n][:, :, :], BF[n][:, :, :], ACT.Copy).then_inc(b_hi, 1)
                if before:
                    if not here:
                        act.wait_ge(conv_done[3], NT * (b - 1))
                    normalised_tiles(act, 3, b - 1, 1 - s, range(2, 5))
                if here:
                    std(2, b)
                if before:
                    normalised_tiles(act, 3, b - 1, 1 - s, range(5, HALF + 2))
                if here:
                    act.wait_ge(scale_done[2], b + 1)
                    normalised_tiles(act, 2, b, s, range(NT))
                if before:
                    normalised_tiles(act, 3, b - 1, 1 - s, range(HALF + 2, HALF + 4))
                if here:
                    std(3, b)
                if before:
                    normalised_tiles(act, 3, b - 1, 1 - s, range(HALF + 4, NT))
                if here:
                    act.wait_ge(scale_done[3], b + 1)
                    if before:
                        act.wait_ge(gl_done[3], NT * b)
                        act.wait_ge(conv_done[3], NT * b + (2 - RING))
                    normalised_tiles(act, 3, b, s, range(2))

            act.wait_ge(bases_in, 32)
            act.activation(inv_parts[:, 0, :], inv_rows[:, :], ACT.Copy).then_inc(basis_split, 1)
            sample_steps(act, body)

        @block.gpsimd
        def _(pool):
            def low_parts(n, b, tiles):
                for q in tiles:
                    pool.wait_ge(g_done[n], 2 * NT * b + (2 * q + 2))
                    pool.tensor_tensor(GL[n][:, q % RING, :, :], GN[n][:, q % 2, :, :], GH[n][:, q % RING, :, :],
                                       ALU.subtract).then_inc(gl_done[n], 1)

            def body(b, s, here, before):
                if here:
                    for q in range(NT):
                        pool.wait_ge(zh_out, NT * b + (q + 1))
                        pool.tensor_tensor(ZL[:, q % RING, :], Z[:, q % 2, :], ZH[:, q % RING, :], ALU.subtract)\
                            .then_inc(zl_out, 1)
                if not before:
                    for n in (2, 3):
                        pool.wait_ge(b_hi, n - 1)
                        pool.tensor_tensor(BL[n][:, :, :], BF[n][:, :, :], BH[n][:, :, :], ALU.subtract)\
                            .then_inc(b_lo, 1)
                if before:
                    low_parts(3, b - 1, range(2, HALF + 2))
                if here:
                    low_parts(2, b, range(NT))
                if before:
                    low_parts(3, b - 1, range(HALF + 2, NT))
                if here:
                    low_parts(3, b, range(2))

            pool.memset(O[:, P // 2:P, :], 0.0).then_inc(pool_cleared, 1)
            pool.wait_ge(basis_split, 1)
            pool.tensor_tensor(inv_parts[:, 1, :], inv_rows[:, :], inv_parts[:, 0, :], ALU.subtract)\
                .then_inc(basis_split, 1)
            sample_steps(pool, body)

        @block.tensor
        def _(pe):
            def sums(n, b):
                pe.wait_ge(chain[n], CHAIN * b + CHAIN_SUMS)
                pe.matmul(pS[:, :], ones[:, :], ST[n].sums[:, :, :].rearrange("p a g -> p (a g)"), start=True,
                          stop=True).then_inc(sums_done[n], 1)

            def convolve(n, b, tiles, banks, taken):
                size = {2: S2, 3: S3}[n]
                off = PAD - size // 2
                for q in tiles:
                    bank = banks[q % len(banks)]
                    pe.wait_ge(gl_done[n], NT * b + (q + 1))
                    if q >= len(banks):
                        pe.wait_ge(taken, NT * b + (q + 1 - len(banks)))
                    for dx in range(size):
                        for k, (w, g) in enumerate(((BH, GH), (BH, GL), (BL, GH))):
                            last = pe.matmul(bank[:, :], w[n][:, dx, :], g[n][:, q % RING, :, off + dx:off + dx + W],
                                             start=(dx == 0 and k == 0), stop=(dx == size - 1 and k == 2))
                    last.then_inc(conv_done[n], 1)

            def inverse_first(b):
                pe.wait_ge(o_in, 128 * b + 128)
                for q in range(2):
                    inverse_columns(pe, pZ[q], O, inv_cols, q).then_inc(icols_done, 1)

            def inverse(b, n):
                pe.wait_ge(zl_out, NT * b + (n + 1))
                if n >= 2:
                    pe.wait_ge(x_sum[2], NT * b + (n - 1))
                inverse_rows(pe, pA[n % 2], ZH[:, n % RING, :], ZL[:, n % RING, :], inv_parts).then_inc(irows_done, 1)

            def body(b, s, here, before):
                if here:
                    for q in range(2, NT + 1):
                        if q < NT:
                            pe.wait_ge(z_out, NT * b + (q - 1))
                            inverse_columns(pe, pZ[q % 2], O, inv_cols, q).then_inc(icols_done, 1)
                        inverse(b, q - 2)
                if before:
                    if not here:
                        pe.wait_ge(out_done, NT * (b - 1))
                    convolve(3, b - 1, range(1), pC, out_done)
                if here:
                    inverse(b, NT - 1)
                if before:
                    convolve(3, b - 1, range(1, 2), pC, out_done)
                if here:
                    sums(2, b)
                if before:
                    convolve(3, b - 1, range(2, HALF), pC, out_done)
                if here:
                    if not before:
                        pe.wait_ge(b_hi, 2)
                        pe.wait_ge(b_lo, 2)
                    convolve(2, b, range(NT), pA, x_sum[3])
                if before:
                    convolve(3, b - 1, range(HALF, HALF + 1), pC, out_done)
                if here:
                    sums(3, b)
                if before:
                    convolve(3, b - 1, range(HALF + 1, NT - 1), pC, out_done)
                if here and not (isinstance(b, int) and b == B - 1):
                    inverse_first(b + 1)
                if before:
                    convolve(3, b - 1, range(NT - 1, NT), pC, out_done)

            pe.wait_ge(bases_in, 32)
            pe.wait_ge(basis_split, 2)
            inverse_first(0)
            sample_steps(pe, body)

        @block.vector
        def _(dve):
            def tile_sum(n, b, s, q, bank):
                x = tile_of(s, q)
                dve.tensor_tensor(x, x, bank[:, :], ALU.add).then_inc(x_sum[n], 1)

            def tile_statistics(n, b, s, q):
                dve.wait_ge(x_sum[n], NT * b + (q + 1))
                for g in (2 * q, 2 * q + 1):
                    last = dve.bn_stats(ST[n].bn[:, g, :], X[:, s, 2 * g:2 * g + 2, :].rearrange("p c w -> p (c w)"))
                if q == NT - 1:
                    last.then_inc(bn_done[n], 1)

            def scales(n, b, s):
                dve.wait_ge(bn_done[n], b + 1)
                step = Chain(dve, chain[n], CHAIN, b)
                group_scale_steps(dve, step, ST[n], sums_done[n], pS, std_done[n], ST[n].std, b)
                dve.tensor_copy(SC[n][:, s, 0, :], ST[n].r[:, :])
                dve.scalar_tensor_tensor(SC[n][:, s, 1, :], ST[n].ms[:, 0:G], -1.0, ST[n].r[:, :], ALU.mult, ALU.mult)\
                    .then_inc(scale_done[n], 1)
                dve.wait_ge(scale_done[n], b + 1)

            def results(b, s, tiles):
                for q in tiles:
                    x = tile_of(s, q)
                    dve.wait_ge(conv_done[3], NT * b + (q + 1))
                    dve.tensor_tensor(x, x, pC[q % 3][:, :], ALU.add).then_inc(out_done, 1)

            def body(b, s, here, before):
                if here:
                    for q in range(NT + 1):
                        if q < NT:
                            if q % 8 == 0:
                                dve.wait_ge(x_in[s][q // 8], 64 * (b // 2) + 64)
                            dve.wait_ge(irows_done, NT * b + (q + 1))
                            tile_sum(2, b, s, q, pA[q % 2])
                        if q >= 1:
                            tile_statistics(2, b, s, q - 1)
                    scales(2, b, s)
                if before:
                    results(b - 1, 1 - s, range(HALF))
                if here:
                    for q in range(NT + 1):
                        if q < NT:
                            dve.wait_ge(conv_done[2], NT * b + (q + 1))
                            tile_sum(3, b, s, q, pA[q % 2])
                        if q >= 1:
                            tile_statistics(3, b, s, q - 1)
                    scales(3, b, s)
                if before:
                    results(b - 1, 1 - s, range(HALF, NT))

            dve.memset(O[:, 0:P // 2, :], 0.0).then_inc(cleared, 1)
            for n in (2, 3):
                for s in range(2):
                    dve.memset(GN[n][:, s, :, 0:PAD], 0.0)
                    dve.memset(GN[n][:, s, :, PAD + W:], 0.0)
            dve.memset(ones[:, :], 1.0 / 256)
            dve.wait_ge(const_in, 16 * 5)
            done = [0]

            def step(ins):
                done[0] += 1
                ins.then_inc(built, 1)
                dve.wait_ge(built, done[0])

            step(dve.tensor_scalar(K2[:, :], stencils[:, 0, :], alpha[:, 0:1], None, ALU.mult))
            for a in range(1, 8):
                step(dve.scalar_tensor_tensor(K2[:, :], stencils[:, a, :], alpha[:, a:a + 1], K2[:, :],
                                              ALU.mult, ALU.add))
            step(dve.tensor_scalar(small[:, 0:1], alpha[:, 8:9], -1.0 / 9.0, None, ALU.mult))
            step(dve.tensor_tensor(small[:, 1:2], alpha[:, 8:9], beta[:, :], ALU.add))
            step(dve.tensor_scalar(K2[:, :], K2[:, :], small[:, 0:1], None, ALU.add))
            step(dve.tensor_tensor(K2[:, 4:5], K2[:, 4:5], small[:, 1:2], ALU.add))
            band_matrices(dve, BF[2], shifts, K2, S2, step)
            assert done[0] == BUILT
            sample_steps(dve, body)


def conv_blocks(w):
    import numpy as np
    blocks = np.zeros((2, C, 6, 2, C), np.float32)
    for d in range(2):
        for row_in in range(2):
            for row_out in range(2):
                dy = 2 * d + row_in - row_out
                if 0 <= dy < 3:
                    for dx in range(3):
                        blocks[row_in, :, 3 * d + dx, row_out, :] = w[:, :, dy, dx].T
    return blocks.reshape(P, 6, P)


def layer0_arrays(x, w0, b0, w1, b1, w2, b2, w3, b3, wf, bf):
    import numpy as np
    f32 = np.float32

    def both(a):
        return np.concatenate([a, a]).astype(f32)

    w3blk = np.zeros((2, C, 9, 2, C), f32)
    for p in range(2):
        w3blk[p, :, :, p, :] = w3.reshape(C, 9, C).transpose(2, 1, 0)
    taps = both(w0.reshape(C, C, 9).transpose(1, 2, 0))
    grp = np.zeros((P, P), f32)
    band = np.zeros((C, 2, C), f32)
    for c in range(C):
        for p in range(P):
            grp[p, [c0 + q for q in (0, C) for c0 in range(C) if c0 // 2 == (p % C) // 2]] = 0.25
        for k in range(3):
            if 0 <= c + k - 1 < C:
                band[c + k - 1, :, c] = w2[0, 0, k]
    cnt = np.zeros((2, C, 3, 3), f32)
    for h in range(2):
        for dy in range(3):
            for dx in range(3):
                gone = (dy == 0 and h == 1) or (dy == 2 and h == 0)
                cnt[h, :, dy, dx] = (H // 2 - gone) * (W - (dx != 1))
    half = np.zeros((2, C, 2), f32)
    half[0, :, 0] = half[1, :, 1] = -1.0
    mask = np.ones((2, C, 16), f32)
    mask[0, :, 0] = mask[1, :, 15] = 0.0
    b12 = np.zeros((2, C, 3), f32)
    b12[:, :, 0], b12[:, :, 1], b12[:, :, 2] = b1, bf, b2[0]
    x_rows = np.zeros((B, C, H + 2, W), f32)
    x_rows[:, :, 1:H + 1] = x
    return {
        "x": x, "x_rows": x_rows, "w0taps": taps, "grp": grp, "band": band.reshape(C, P),
        "cnt": cnt.reshape(P, 9), "half": half.reshape(P, 2), "b0": both(b0).reshape(P, 1),
        "b12": b12.reshape(P, 3), "b3": both(b3.reshape(C, 9)), "w3blk": w3blk.reshape(P, 9, P),
        "w0blk": conv_blocks(w0), "wfblk": conv_blocks(wf), "w1": both(w1.reshape(C, 9)),
        "mask": mask.reshape(P, 16),
    }


def spectral_bases():
    import numpy as np
    tau = 2 * np.pi / H
    n, k = np.meshgrid(np.arange(H), np.arange(F), indexing="ij")
    fa, fb = tau * (n * k % H), tau * ((n + 1) * k % H)
    ia, ib = fa.T, (tau * (n * (k + 1) % H)).T
    f32 = np.float32
    ones = sum(np.outer(x.sum(0), y.sum(0)) * sign for x, y, sign in (
        (np.cos(fa), np.cos(fa), 1), (np.sin(fa), np.sin(fa), -1), (np.cos(fb), np.sin(fb), -1),
        (np.sin(fb), np.cos(fb), -1)))
    return {
        "ones_modes": np.repeat(ones.reshape(2, 1, MODES), C, 1).reshape(P, MODES).astype(f32),
        "fwd_rows": np.concatenate([np.cos(fa), np.sin(fa), np.cos(fb), np.sin(fb)], 1).astype(f32),
        "fwd_cols": np.stack([np.cos(fa), -np.sin(fa), -np.sin(fb), -np.cos(fb)], 1).astype(f32),
        "inv_cols": np.concatenate([np.cos(ia), np.sin(ia), np.cos(ib), np.sin(ib)], 0).astype(f32),
        "inv_rows": (np.concatenate([np.cos(ia), -np.sin(ia), -np.sin(ib), -np.cos(ib)], 0) / (H * W)).astype(f32),
    }


def row_shifts():
    import numpy as np
    return np.stack([np.eye(P, k=1 - dy) for dy in range(3)], 1).astype(np.float32)


def stencil_arrays(alpha, beta, kernels, k3):
    import numpy as np
    flat = {"alpha": alpha, "beta": beta, "stencils": kernels}
    band3 = np.zeros((P, 9, P), np.float32)
    for dy in range(9):
        for out in range(max(0, 4 - dy), min(P, P + 4 - dy)):
            band3[out + dy - 4, :, out] = k3[0, 0, dy]
    return {"band3": band3, **{name: np.ascontiguousarray(np.broadcast_to(a.reshape(1, -1), (P, a.size)))
                               for name, a in flat.items()}}


_INS = ["x", "x_rows", "w0taps", "grp", "band", "cnt", "half", "b0", "b12", "b3", "w3blk", "w0blk", "wfblk", "w1",
        "mask", "weights1", "refine1", "fwd_rows", "fwd_cols", "inv_cols", "inv_rows", "ones_modes", "shifts",
        "alpha", "beta", "stencils", "band3"]


class Arrays:

    def __init__(self, args):
        (self.x, self.x_rows, self.w0taps, self.grp, self.band, self.cnt, self.half, self.b0, self.b12,
         self.b3, self.w3blk, self.w0blk, self.wfblk, self.w1, self.mask, self.weights1, self.refine1,
         self.fwd_rows, self.fwd_cols, self.inv_cols, self.inv_rows, self.ones_modes, self.shifts,
         self.alpha, self.beta, self.stencils, self.band3, self.out) = args


def conv_stack_kernel(nc, *args):
    F32 = mybir.dt.float32
    t = Arrays(args)
    t.x1 = nc.dram_tensor("x1", (B, C, H, W), F32, kind="Internal").ap()
    t.o_ht = nc.dram_tensor("o_ht", (2 * B, MODES, C), F32, kind="Internal").ap()
    t.o_sum = nc.dram_tensor("o_sum", (2 * B, MODES, C), F32, kind="Internal").ap()
    with ExitStack() as ctx:
        t.gn0 = ctx.enter_context(nc.sbuf_tensor("gn0", [P, 4, B], F32))
        t.b3p = ctx.enter_context(nc.sbuf_tensor("b3p", [P, B, 9], F32))
        t.w0, t.wf, t.w3 = [[ctx.enter_context(nc.sbuf_tensor(f"{name}_{part}", [P, n, P], mybir.dt.float32r))
                             for part in ("hi", "lo")] for name, n in (("w0", 6), ("wf", 6), ("w3", 9))]
        layer0_statistics(nc, t)
        layer0_convolutions(nc, t)
    with ExitStack() as ctx:
        t.gn1 = ctx.enter_context(nc.sbuf_tensor("gn1", [P, B, 2, G], F32))
        layer1_analyse(nc, t)
        layer1_refine(nc, t)
    layers2_and_3(nc, t)


def kernel(**inputs):
    import numpy as np
    import concourse.bacc as bacc
    from concourse.bass_utils import run_bass_kernel_spmd

    given = {name: np.asarray(a) for name, a in inputs.items()}
    laid_out = {
        **layer0_arrays(given["x"], *[given[f"L0_conv_{k}"]
                                      for k in ("w0", "b0", "w1", "b1", "w2", "b2", "w3", "b3", "wf", "bf")]),
        "weights1": given["L1_conv_weights1"], "refine1": given["L1_conv_refine_weights1"],
        **spectral_bases(), "shifts": row_shifts(),
        **stencil_arrays(given["L2_conv_alpha"], given["L2_conv_beta"], given["L2_conv_kernels"],
                         given["L3_conv_K"]),
    }
    nc = bacc.Bacc("TRN2", target_bir_lowering=False, num_devices=1)
    arrays, args = {}, []
    for name in _INS:
        a = np.ascontiguousarray(laid_out[name])
        arrays[f"in_{name}_dram"] = a
        args.append(nc.dram_tensor(f"in_{name}_dram", a.shape, mybir.dt.from_np(a.dtype), kind="ExternalInput").ap())
    args.append(nc.dram_tensor("out_dram", (B, C, H, W), mybir.dt.float32, kind="ExternalOutput").ap())
    conv_stack_kernel(nc, *args)
    r = run_bass_kernel_spmd(nc, [arrays], core_ids=[0])
    return r.results[0]["out_dram"]
```
